# Optimizing a Trainium2 kernel written in Bass

```python
import numpy as np
import jax
import jax.numpy as jnp

def _softmax(x, axis=-1):
    return jax.nn.softmax(x, axis=axis)

def _gelu(x):
    return jax.nn.gelu(x, approximate=True)

def _silu(x):
    return jax.nn.silu(x)

def _sigmoid(x):
    return jax.nn.sigmoid(x)

def _layernorm(x, axis=-1, eps=1e-05):
    m = jnp.mean(x, axis=axis, keepdims=True)
    v = jnp.var(x, axis=axis, keepdims=True)
    return (x - m) / jnp.sqrt(v + eps)

def _scatter_add(tgt, idx, src, axis=0):
    return tgt.at[idx].add(src)

def _segment_sum(src, seg, n):
    return jax.ops.segment_sum(src, seg, n)
kernel_name = 'mk_adaln_d1_jaxref_r8_17d791'

def setup_inputs(seed: int=0):
    np.random.seed(seed)
    _w = jnp.asarray

    def _L0_attn_setup():
        import jax, jax.numpy as jnp
        import numpy as np
        B, S, H = (2, 256, 256)
        NH, NKV, HD = (16, 8, 128)
        WINDOW = 128
        THETA = 100000.0

        def _rope(x, cos, sin):
            d2 = x.shape[-1] // 2
            x1, x2 = (x[..., :d2], x[..., d2:])
            c = cos[None, :, None, :]
            s = sin[None, :, None, :]
            return jnp.concatenate([x1 * c - x2 * s, x2 * c + x1 * s], axis=-1)

        def _causal_conv2(x, w):
            x_prev = jnp.pad(x, ((0, 0), (1, 0), (0, 0), (0, 0)))[:, :-1]
            return w[None, None, :, 0:1] * x_prev + w[None, None, :, 1:2] * x
        key = jax.random.key(seed)
        ks = jax.random.split(key, 5)
        hidden = jax.random.normal(ks[0], (B, S, H), jnp.float32)
        W_pack = jax.random.normal(ks[1], (H, NH * HD + 2 * NKV * HD), jnp.float32) * H ** (-0.5)
        W_o = jax.random.normal(ks[2], (NH * HD, H), jnp.float32) * (NH * HD) ** (-0.5)
        conv_k = jax.nn.softmax(jax.random.normal(ks[3], (NKV, 2), jnp.float32), axis=-1)
        conv_v = jax.nn.softmax(jax.random.normal(ks[4], (NKV, 2), jnp.float32), axis=-1)
        return {'hidden': hidden, 'W_pack': W_pack, 'W_o': W_o, 'conv_k': conv_k, 'conv_v': conv_v}
    _L0_attn_in = _L0_attn_setup()

    def _L0_ffn_setup():
        import jax, jax.numpy as jnp
        import numpy as np
        B, S, H = (2, 256, 256)
        E, K, F = (32, 4, 176)
        FS = 704
        EPS = 1e-06
        CAP = 128
        key = jax.random.key(seed)
        ks = jax.random.split(key, 10)
        s = 0.02
        return {'hidden_states': jax.random.normal(ks[0], (B, S, H), jnp.float32), 'w_norm': 1.0 + 0.02 * jax.random.normal(ks[1], (H,), jnp.float32), 'w_router': s * jax.random.normal(ks[2], (H, E), jnp.float32), 'w_gate': s * jax.random.normal(ks[3], (E, H, F), jnp.float32), 'w_up': s * jax.random.normal(ks[4], (E, H, F), jnp.float32), 'w_down': s * jax.random.normal(ks[5], (E, F, H), jnp.float32), 'sw_gate': s * jax.random.normal(ks[6], (H, FS), jnp.float32), 'sw_up': s * jax.random.normal(ks[7], (H, FS), jnp.float32), 'sw_down': s * jax.random.normal(ks[8], (FS, H), jnp.float32), 'w_shared_gate': s * jax.random.normal(ks[9], (H, 1), jnp.float32)}
    _L0_ffn_in = _L0_ffn_setup()
    _L0_c = _w((lambda *s: np.random.randn(*s).astype(np.float32) * 0.05)(8, 256))
    _L0_wmod = _w((lambda *s: np.random.randn(*s).astype(np.float32) * 0.05)(256, 6 * 256) * 256 ** (-0.5))
    _d = {'L0_attn_hidden': _L0_attn_in['hidden'], 'L0_attn_W_pack': _L0_attn_in['W_pack'], 'L0_attn_W_o': _L0_attn_in['W_o'], 'L0_attn_conv_k': _L0_attn_in['conv_k'], 'L0_attn_conv_v': _L0_attn_in['conv_v'], 'L0_ffn_w_norm': _L0_ffn_in['w_norm'], 'L0_ffn_w_router': _L0_ffn_in['w_router'], 'L0_ffn_w_gate': _L0_ffn_in['w_gate'], 'L0_ffn_w_up': _L0_ffn_in['w_up'], 'L0_ffn_w_down': _L0_ffn_in['w_down'], 'L0_ffn_sw_gate': _L0_ffn_in['sw_gate'], 'L0_ffn_sw_up': _L0_ffn_in['sw_up'], 'L0_ffn_sw_down': _L0_ffn_in['sw_down'], 'L0_ffn_w_shared_gate': _L0_ffn_in['w_shared_gate'], 'L0_c': _L0_c, 'L0_wmod': _L0_wmod}
    _x0 = _d['L0_attn_hidden']
    _d['L0_attn_hidden'] = jax.random.normal(jax.random.fold_in(jax.random.key(seed), 1), (8, 256, 256), dtype=_x0.dtype)
    del _x0
    return _d

def reference(L0_attn_hidden, L0_attn_W_pack, L0_attn_W_o, L0_attn_conv_k, L0_attn_conv_v, L0_ffn_w_norm, L0_ffn_w_router, L0_ffn_w_gate, L0_ffn_w_up, L0_ffn_w_down, L0_ffn_sw_gate, L0_ffn_sw_up, L0_ffn_sw_down, L0_ffn_w_shared_gate, L0_c, L0_wmod):

    def _L0_attn_ref(hidden, W_pack, W_o, conv_k, conv_v):
        import jax, jax.numpy as jnp
        import numpy as np
        B, S, H = (2, 256, 256)
        NH, NKV, HD = (16, 8, 128)
        WINDOW = 128
        THETA = 100000.0

        def _rope(x, cos, sin):
            d2 = x.shape[-1] // 2
            x1, x2 = (x[..., :d2], x[..., d2:])
            c = cos[None, :, None, :]
            s = sin[None, :, None, :]
            return jnp.concatenate([x1 * c - x2 * s, x2 * c + x1 * s], axis=-1)

        def _causal_conv2(x, w):
            x_prev = jnp.pad(x, ((0, 0), (1, 0), (0, 0), (0, 0)))[:, :-1]
            return w[None, None, :, 0:1] * x_prev + w[None, None, :, 1:2] * x
        b, s, _ = hidden.shape
        qkv = hidden @ W_pack
        q = qkv[..., :NH * HD].reshape(b, s, NH, HD)
        k = qkv[..., NH * HD:NH * HD + NKV * HD].reshape(b, s, NKV, HD)
        v = qkv[..., NH * HD + NKV * HD:].reshape(b, s, NKV, HD)
        inv_freq = 1.0 / THETA ** (jnp.arange(0, HD, 2, dtype=jnp.float32) / HD)
        freqs = jnp.outer(jnp.arange(s, dtype=jnp.float32), inv_freq)
        cos, sin = (jnp.cos(freqs), jnp.sin(freqs))
        q = _rope(q, cos, sin)
        k = _rope(k, cos, sin)
        k = _causal_conv2(k, conv_k)
        v = _causal_conv2(v, conv_v)
        group = NH // NKV
        k = jnp.repeat(k, group, axis=2)
        v = jnp.repeat(v, group, axis=2)
        scores = jnp.einsum('bqhd,bkhd->bhqk', q, k) / jnp.sqrt(jnp.float32(HD))
        i = jnp.arange(s)[:, None]
        j = jnp.arange(s)[None, :]
        mask = (j <= i) & (i - j < WINDOW)
        scores = jnp.where(mask[None, None], scores, jnp.finfo(scores.dtype).min)
        probs = jax.nn.softmax(scores, axis=-1)
        out = jnp.einsum('bhqk,bkhd->bqhd', probs, v).reshape(b, s, NH * HD)
        return out @ W_o

    def _L0_ffn_ref(hidden_states, w_norm, w_router, w_gate, w_up, w_down, sw_gate, sw_up, sw_down, w_shared_gate):
        import jax, jax.numpy as jnp
        import numpy as np
        B, S, H = (2, 256, 256)
        E, K, F = (32, 4, 176)
        FS = 704
        EPS = 1e-06
        CAP = 128
        inp = hidden_states
        xf = inp.astype(jnp.float32)
        var = jnp.mean(xf * xf, axis=-1, keepdims=True)
        x = (w_norm * (xf * jax.lax.rsqrt(var + EPS))).astype(inp.dtype)
        Bq, Sq, Hq = x.shape
        x = x.reshape(-1, Hq)
        T = Bq * Sq
        logits = x @ w_router
        probs = jax.nn.softmax(logits.astype(jnp.float32), axis=-1)
        w_topk, sel = jax.lax.top_k(probs, K)
        w_topk = w_topk.astype(x.dtype)
        flat_e = sel.reshape(-1)
        order = jnp.argsort(flat_e)
        sorted_e = flat_e[order]
        counts = jnp.zeros((E,), jnp.int32).at[flat_e].add(1)
        starts = jnp.cumsum(counts) - counts
        pos = jnp.arange(T * K) - starts[sorted_e]
        tok = order // K
        valid = pos < CAP
        dest = jnp.where(valid, pos, CAP)
        buf = jnp.zeros((E, CAP + 1, Hq), x.dtype).at[sorted_e, dest].set(x[tok])
        buf = buf[:, :CAP]
        g = jnp.einsum('ech,ehf->ecf', buf, w_gate)
        u = jnp.einsum('ech,ehf->ecf', buf, w_up)
        y = jnp.einsum('ecf,efh->ech', jax.nn.silu(g) * u, w_down)
        wv = w_topk.reshape(-1)[order] * valid.astype(x.dtype)
        gath = y[sorted_e, jnp.minimum(pos, CAP - 1)]
        out = jnp.zeros((T, Hq), x.dtype).at[tok].add(gath * wv[:, None])
        sh = jax.nn.silu(x @ sw_gate) * (x @ sw_up) @ sw_down
        sh = jax.nn.sigmoid(x @ w_shared_gate) * sh
        out = out + sh
        return inp + out.reshape(Bq, Sq, Hq)
    x = L0_attn_hidden
    mod = (_silu(L0_c) @ L0_wmod).reshape(L0_c.shape[0], 6, 1, -1)
    sa, ca, ga, sb, cb, gb = (mod[:, 0], mod[:, 1], mod[:, 2], mod[:, 3], mod[:, 4], mod[:, 5])
    ga = (2 * (ga >= 0) - 1) * jnp.maximum(jnp.abs(ga), 0.25)
    gb = (2 * (gb >= 0) - 1) * jnp.maximum(jnp.abs(gb), 0.25)
    h = _layernorm(x, axis=-1) * (1 + ca) + sa
    x = x + ga * _L0_attn_ref(h, L0_attn_W_pack, L0_attn_W_o, L0_attn_conv_k, L0_attn_conv_v)
    h = _layernorm(x, axis=-1) * (1 + cb) + sb
    x = x + gb * _L0_ffn_ref(h, L0_ffn_w_norm, L0_ffn_w_router, L0_ffn_w_gate, L0_ffn_w_up, L0_ffn_w_down, L0_ffn_sw_gate, L0_ffn_sw_up, L0_ffn_sw_down, L0_ffn_w_shared_gate)
    return x

_drawn_inputs = setup_inputs


def setup_inputs(seed=0):
    import zlib

    import numpy as np

    out = dict(_drawn_inputs(seed))
    spreads = {}
    factors = {'L0_attn_conv_k': 4.403,
     'L0_attn_conv_v': 4.121,
     'L0_ffn_w_norm': 8.0,
     'L0_ffn_w_router': 8.0,
     'L0_ffn_w_gate': 8.0,
     'L0_ffn_w_up': 8.0,
     'L0_ffn_w_down': 8.0,
     'L0_ffn_sw_gate': 8.0,
     'L0_ffn_sw_up': 8.0,
     'L0_ffn_sw_down': 8.0,
     'L0_ffn_w_shared_gate': 8.0}
    for name, (base, spread) in spreads.items():
        noise = np.random.default_rng([zlib.crc32(name.encode()), seed]).standard_normal(out[name].shape)
        drawn = base * np.exp(spread * noise) if base else spread * noise
        out[name] = jnp.asarray(drawn.astype(out[name].dtype))
    for name, factor in factors.items():
        out[name] = (out[name] * factor).astype(out[name].dtype)
    return out
```

```python
from contextlib import ExitStack

import concourse.bass as bass
from concourse import mybir

F32 = mybir.dt.float32
F32R = mybir.dt.float32r
I32 = mybir.dt.int32
ALU = mybir.AluOpType
ACT = mybir.ActivationFunctionType
AXX = mybir.AxisListType.X

PN = 128
B, S, H = 8, 256, 256
HC = H // PN
NH, NKV, HD = 16, 8, 128
E, TOPK, F, CAP = 32, 4, 176, 128
FH = F // 2
FS = 704
FT = -(-FS // PN)
NPAIR = B // 2
TOK = 2 * S
TT = TOK // PN
GROUPS = NKV
UNITS = 4 * GROUPS
ROPES = 3 * GROUPS
QKV = (NH + 2 * NKV) * HD
LN_EPS, RMS_EPS = 1e-5, 1e-6
ROPE_OF = {0: 0, 1: 1, 3: 2}
T_LAG, PV_LAG = 2, 3
PROB_FLOOR = -87.34
SENTINEL, TAKEN = 1.0, -1000.0
SKIP = 2 * E * CAP
RING = 4
FREE = 1
LCOL = 64


def adaln_block(nc, x, w_pack, w_o, conv_k, conv_v, w_norm, w_router, w_gate, w_up, w_down, sw_gate, sw_up,
                sw_down, w_sgate, c_in, wmod, cos_t, sin_t, mask_t, ident_t, tri_t, ebase_t, out):
    ctx = ExitStack()
    with ctx:
        def sb(name, shape, dt=F32, where=ctx):
            return where.enter_context(nc.sbuf_tensor(name, shape, dt))

        def sem(name):
            return ctx.enter_context(nc.semaphore(name))

        mod_d = nc.dram_tensor("mod_rows", [B, 6 * H], F32, kind="Internal").ap()
        slots_d = nc.dram_tensor("slot_rows", [E * CAP, H], F32, kind="Internal").ap()
        y_d = nc.dram_tensor("expert_rows", [E * CAP, H], F32, kind="Internal").ap()
        base_d = nc.dram_tensor("residual_rows", [B * S, H], F32, kind="Internal").ap()
        xnt_d = nc.dram_tensor("xn_transposed", [NPAIR, PN, 2, HC, TOK], F32, kind="Internal").ap()

        cosT = sb("cosT", [PN, S])
        sinT = sb("sinT", [PN, S])
        mask = sb("mask", [PN, 3 * PN])
        ident = sb("ident", [PN, PN])
        tri = sb("tri", [PN, PN])
        ones = sb("ones", [PN, PN])
        ebase = sb("ebase", [PN, E])
        wnorm = sb("wnorm", [PN, H])
        cwk = sb("cwk", [PN, 2 * NKV])
        cwv = sb("cwv", [PN, 2 * NKV])
        modT = sb("modT", [PN, 4, B + 2])
        scT = sb("scT", [PN, HC, B])
        wr = sb("wr", [PN, HC, E + 2])
        wr_hi = sb("wr_hi", [PN, HC, E + 2], F32R)
        wr_lo = sb("wr_lo", [PN, HC, E + 2], F32R)
        gidx = sb("gidx", [PN, NPAIR, TT * TOPK], I32)
        wsel = sb("wsel", [PN, NPAIR, TT * TOPK])
        sgate = sb("sgate", [PN, NPAIR, TT])
        carry = sb("carry", [PN, 2, E])

        att = ExitStack()
        hT_hi = sb("hT_hi", [PN, HC, TOK], F32R, att)
        hT_lo = sb("hT_lo", [PN, HC, TOK], F32R, att)
        bcm = sb("bcm", [PN, 2, 4 * H], F32, att)
        xin = sb("xin", [PN, TT, H], F32, att)
        xres = sb("xres", [PN, TT, H], F32, att)
        qsw = sb("qsw", [PN, 2, TOK], F32, att)
        qr = sb("qr", [PN, 2, 2, TOK], F32, att)
        kr = sb("kr", [PN, TOK], F32, att)
        k0 = sb("k0", [PN, 2, S + 1], F32, att)
        v0 = sb("v0", [PN, 2, S + 1], F32, att)
        kc = sb("kc", [PN, 2, TOK], F32, att)
        vT = sb("vT", [PN, TOK], F32, att)
        vN = sb("vN", [PN, 2, TOK], F32, att)
        rows8 = ExitStack()
        c_sb = sb("c_sb", [B, H], F32, rows8)
        sc = sb("sc", [B, H], F32, rows8)
        gabs = sb("gabs", [B, H], F32, rows8)
        gsgn = sb("gsgn", [B, H], F32, rows8)
        rows8.close()
        sneg = sb("sneg", [PN, 2, 3 * PN], F32, att)
        nmax = sb("nmax", [PN, 4, 2], F32, att)
        prob = sb("prob", [PN, 3, 3 * PN], F32, att)
        rsum = sb("rsum", [PN, 4, 2], F32, att)
        rinv = sb("rinv", [PN, 4, 2], F32, att)
        pT = sb("pT", [PN, 2, 3 * PN], F32, att)
        wo = sb("wo", [PN, NH, H], F32, att)
        st1 = sb("st1", [PN, TT, 6], F32, att)
        mv1 = sb("mv1", [PN, TT, 2], F32, att)
        std1 = sb("std1", [PN, 2, TT], F32, att)
        mods = ExitStack()
        wm = sb("wm", [PN, HC, 6 * H], F32, mods)
        mod = sb("mod", [B, 6 * H], F32, mods)
        mods.close()
        xnT_hi = sb("xnT_hi", [PN, HC, S], F32R, att)
        xnT_lo = sb("xnT_lo", [PN, HC, S], F32R, att)
        yg = sb("yg", [PN, 2, 2, H], F32, att)
        h2 = sb("h2", [PN, TT, H], F32, att)
        xn = sb("xn", [PN, TT, H], F32, att)
        st2 = sb("st2", [PN, TT, 6], F32, att)
        mv2 = sb("mv2", [PN, TT, 2], F32, att)
        std2 = sb("std2", [PN, 2, TT], F32, att)
        rms = sb("rms", [PN, 3, TT], F32, att)
        zz = sb("zz", [PN, TT, E + TOPK], F32, att)
        zz2 = sb("zz2", [PN, TT, E + TOPK], F32, att)
        top8 = sb("top8", [PN, TT, 8], F32, att)
        key8 = sb("key8", [PN, TT, 8], F32, att)
        red = sb("red", [PN, 4, TT], F32, att)
        ex = sb("ex", [PN, TT, E], F32, att)
        chosen = sb("chosen", [PN, TT, E], F32, att)
        kept = sb("kept", [PN, TT, E], F32, att)
        key = sb("key", [PN, TT, E], F32, att)
        late = sb("late", [PN, TT, TOPK], F32, att)
        sidx = sb("sidx", [PN, TT * TOPK], I32, att)
        eq = sb("eq", [PN, TT, TOPK, E], F32, att)
        raws = ExitStack()
        wraw = sb("wraw", [PN, HC, QKV], F32, raws)
        raws.close()
        outs = ExitStack()
        oT = sb("oT", [PN, NH, TOK], F32, outs)
        proj_w = ExitStack()
        w_hi = sb("w_hi", [PN, HC, QKV], F32R, proj_w)
        w_lo = sb("w_lo", [PN, HC, QKV], F32R, proj_w)
        proj_w.close()

        exps = ExitStack()
        wgu = sb("wgu", [PN, RING, HC, 2 * F], F32, exps)
        wd = sb("wd", [FH, RING, 2, H], F32, exps)
        xe = sb("xe", [PN, RING, H], F32, exps)
        xeT = sb("xeT", [PN, 2, H], F32, exps)
        sgl = sb("sgl", [PN, 2, F], F32, exps)
        hh = sb("hh", [PN, 2, F], F32, exps)
        hhT = sb("hhT", [FH, 2, 2 * PN], F32, exps)
        ye = sb("ye", [PN, 2, H], F32, exps)
        sw_hi = sb("sw_hi", [PN, HC, 2 * FS], F32R, exps)
        sw_lo = sb("sw_lo", [PN, HC, 2 * FS], F32R, exps)
        swd = sb("swd", [PN, FT, H], F32, exps)
        exps.close()
        outs.close()
        shar = ExitStack()
        swraw = sb("swraw", [PN, HC, 2 * FS], F32, shar)
        xs_hi = sb("xs_hi", [PN, 2, HC, TOK], F32R, shar)
        xs_lo = sb("xs_lo", [PN, 2, HC, TOK], F32R, shar)
        shar.close()
        att.close()
        hs = sb("hs", [PN, 2, FT, TOK])
        sg2 = sb("sg2", [PN, 2, TOK])
        gat = sb("gat", [PN, TT, TOPK, H])
        gball = sb("gball", [PN, B, H])
        bas = sb("bas", [PN, 2, H])
        acc = sb("acc", [PN, 2, H])
        fin = sb("fin", [PN, 2, H])
        idxc = sb("idxc", [PN, 2, TT * TOPK], I32)

        def bank(name):
            return ctx.enter_context(nc.psum_tensor(name, [PN, 512], F32))

        PJ = [bank("PJ0"), bank("PJ1")]
        SC = [bank("SC0"), bank("SC1")]
        PT = [bank("PT0"), bank("PT1")]
        OB = bank("OB")
        XB = bank("XB")

        ld_c, ld_wm, ld_xin, ld_xres, ld_bcm = sem("ld_c"), sem("ld_wm"), sem("ld_xin"), sem("ld_xres"), sem("ld_bcm")
        ld_const, ld_wo = sem("ld_const"), sem("ld_wo")
        ld_w = [sem(f"ld_w{j}") for j in range(8)]
        st_mod, st_zero, st_base, st_xnt, st_scat = sem("st_mod"), sem("st_zero"), sem("st_base"), sem("st_xnt"), sem("st_scat")
        silu_done, sct_ps, sct_done, mod_ps, mod_done, modt_ps, modt_done = (
            sem(n) for n in ("silu_done", "sct_ps", "sct_done", "mod_ps", "mod_done", "modt_ps", "modt_done"))
        w_hi_done, w_lo_done, wr_hi_done, wr_lo_done, fills = (
            sem(n) for n in ("w_hi_done", "w_lo_done", "wr_hi_done", "wr_lo_done", "fills"))
        waits_met = sem("waits_met")
        dve_own, act_own, pool_own = sem("dve_own"), sem("act_own"), sem("pool_own")
        var1, std1_done, xhat_done, ht_ps, h_hi_done, h_lo_done = (
            sem(n) for n in ("var1", "std1_done", "xhat_done", "ht_ps", "h_hi_done", "h_lo_done"))
        pj_ps, pj_act, pj_dve, t2_done, rope_done, k0_done, kc_done, vt_ps, vn_done = (
            sem(n) for n in ("pj_ps", "pj_act", "pj_dve", "t2_done", "rope_done", "k0_done", "kc_done", "vt_ps", "vn_done"))
        sc_ps, sneg_done, exp_done, rinv_done, norm_done, pt_ps, pt_done, pv_ps, ot_done = (
            sem(n) for n in ("sc_ps", "sneg_done", "exp_done", "rinv_done", "norm_done", "pt_ps", "pt_done", "pv_ps", "ot_done"))
        y_ps, yg_done, x1_done, var2, std2_done, xh2_done, h2_done, rms_done, xn_done, base_done = (
            sem(n) for n in ("y_ps", "yg_done", "x1_done", "var2", "std2_done", "xh2_done", "h2_done", "rms_done", "xn_done", "base_done"))
        xnt_ps, xnt_hi_done, xnt_lo_done, lg_ps, z_done, ex_done, chosen_done, pos_ps, sidx_done, route_done = (
            sem(n) for n in ("xnt_ps", "xnt_hi_done", "xnt_lo_done", "lg_ps", "z_done", "ex_done", "chosen_done", "pos_ps", "sidx_done", "route_done"))
        ld_e = [sem(f"ld_e{i}") for i in range(RING)]
        ld_xe = [sem(f"ld_xe{i}") for i in range(RING)]
        st_y = [sem("st_y0"), sem("st_y1")]
        xe_ps, xe_done, gu_ps, sgl_done, hh_done, hh_ps, hht_done, ye_ps, ye_done = (
            sem(n) for n in ("xe_ps", "xe_done", "gu_ps", "sgl_done", "hh_done", "hh_ps", "hht_done", "ye_ps", "ye_done"))
        ld_sw, ld_swd, ld_gb = sem("ld_sw"), sem("ld_swd"), sem("ld_gb")
        ld_xs = [sem("ld_xs0"), sem("ld_xs1")]
        ld_bas = [sem("ld_bas0"), sem("ld_bas1")]
        ld_gat = [sem(f"ld_gat{t}") for t in range(TT)]
        st_out = [sem("st_out0"), sem("st_out1")]
        sw_hi_done, sw_lo_done, sh_ps, sg2_done, hs_done, dn_ps, idx_done, acc_done, fin_done, acc_own = (
            sem(n) for n in ("sw_hi_done", "sw_lo_done", "sh_ps", "sg2_done", "hs_done", "dn_ps", "idx_done", "acc_done", "fin_done", "acc_own"))

        def met(eng):
            eng.sem_inc(waits_met, 1)

        class Chain:

            def __init__(self, eng, own, base=0):
                self.eng, self.own, self.base, self.n = eng, own, base, 0

            def __call__(self, ins, plain=False):
                ins.then_inc(self.own, 1)
                self.n += 1
                self.eng.wait_ge(self.own, self.base + self.n)
                if plain:
                    met(self.eng)

        DVE_PRE, DVE_ROUND = 16, 29
        ACT_PRE, ACT_ROUND = 1, 3
        POOL_ROUND = 4
        W_ORDER = (4, 0, 6, 1, 5, 2, 7, 3)
        WC = QKV // 8

        def x_pair(p):
            return x[bass.ds(p * TOK, TOK), :].rearrange("(t p) h -> p t h", p=PN)

        def rows(ap, row):
            return ap[bass.ds(row, PN), :]

        def both(ap):
            return ap.unsqueeze(1).broadcast_to([PN, 2, S])

        def pair3(ap):
            return ap.rearrange("p (b s) -> p b s", b=2)

        def later(n):
            return not isinstance(n, int) or n > 0

        block = ctx.enter_context(nc.Block())

        @block.sync
        def _(sp):
            sp.dma_start(c_sb[:, :], c_in).then_inc(ld_c, 16)
            sp.dma_start(ident[:, :], ident_t).then_inc(ld_c, 16)
            sp.dma_start(wm[:, :, :], wmod.rearrange("(c p) n -> p c n", p=PN)).then_inc(ld_wm, 16)
            sp.dma_start(xin[:, :, :], x_pair(0)).then_inc(ld_xin, 16)
            for j in W_ORDER:
                sp.dma_start(wraw[:, :, j * WC:(j + 1) * WC],
                             w_pack.rearrange("(c p) n -> p c n", p=PN)[:, :, j * WC:(j + 1) * WC]).then_inc(ld_w[j], 16)
            sp.wait_ge(mod_done, 1)
            sp.dma_start(mod_d, mod[:, :]).then_inc(st_mod, 16)
            sp.wait_ge(fills, 1)
            sp.dma_start(slots_d.rearrange("(a p) h -> p a h", p=PN),
                         vN[:, 0, 0:H].unsqueeze(1).broadcast_to([PN, E, H])).then_inc(st_zero, 16)
            sp.wait_ge(st_mod, 16)

            def pair_loads(p):
                sp.wait_ge(base_done, 2 * p + FREE)
                for b in range(2):
                    sp.dma_start(bcm[:, b, :], mod_d[bass.ds(2 * p + b, 1), 2 * H:6 * H].rearrange("a n -> (a n)")
                                 .partition_broadcast(PN)).then_inc(ld_bcm, 16)
                sp.dma_start(xres[:, :, :], x_pair(p)).then_inc(ld_xres, 16)

            def pair_stores(p):
                for b in range(2):
                    sp.wait_ge(base_done, 2 * p + b + 1 + FREE)
                    sp.dma_start(base_d[bass.ds(p * TOK + b * S, S), :].rearrange("(t p) h -> p t h", p=PN),
                                 h2[:, 2 * b:2 * b + 2, :]).then_inc(st_base, 16)
                    sp.wait_ge(xnt_hi_done, 2 * p + b + 1)
                    sp.dma_start(xnt_d[bass.ds(p, 1), :, 0, :, b * S:(b + 1) * S].rearrange("a p c s -> (a p) c s"),
                                 xnT_hi[:, :, :].bitcast(F32)).then_inc(st_xnt, 16)
                    sp.wait_ge(xnt_lo_done, 2 * p + b + 1 + FREE)
                    sp.dma_start(xnt_d[bass.ds(p, 1), :, 1, :, b * S:(b + 1) * S].rearrange("a p c s -> (a p) c s"),
                                 xnT_lo[:, :, :].bitcast(F32)).then_inc(st_xnt, 16)

            with sp.Fori(0, NPAIR - 1) as p:
                pair_loads(p)
                sp.wait_ge(ht_ps, p + 1)
                sp.dma_start(xin[:, :, :], x_pair(p + 1)).then_inc(ld_xin, 16)
                pair_stores(p)
            pair_loads(NPAIR - 1)
            sp.wait_ge(ht_ps, NPAIR)
            sp.dma_start(xin[:, :, :], x_pair(NPAIR - 1)).then_inc(ld_xin, 16)

            def expert_weights(e, i):
                sp.dma_start(wgu[:, i, :, 0:F], w_gate[bass.ds(e, 1), :, :].rearrange("a (c p) f -> p (a c) f", p=PN))\
                  .then_inc(ld_e[i], 16)
                sp.dma_start(wgu[:, i, :, F:2 * F], w_up[bass.ds(e, 1), :, :].rearrange("a (c p) f -> p (a c) f", p=PN))\
                  .then_inc(ld_e[i], 16)
                sp.dma_start(wd[:, i, :, :], w_down[bass.ds(e, 1), :, :].rearrange("a (c p) h -> p (a c) h", p=FH))\
                  .then_inc(ld_e[i], 16)

            sp.wait_ge(pj_ps, UNITS * NPAIR + 4)
            for e in range(RING):
                expert_weights(e, e)
            sp.dma_start(swd[:, 0:FT - 1, :], sw_down[0:(FT - 1) * PN, :].rearrange("(t p) h -> p t h", p=PN)).then_inc(ld_swd, 16)
            sp.dma_start(swd[0:FS - (FT - 1) * PN, FT - 1, :], sw_down[(FT - 1) * PN:FS, :]).then_inc(ld_swd, 16)
            sp.wait_ge(y_ps, TT * NPAIR + FREE)
            for n, src in enumerate((sw_gate, sw_up)):
                sp.dma_start(swraw[:, :, n * FS:(n + 1) * FS], src.rearrange("(c p) f -> p c f", p=PN)).then_inc(ld_sw, 16)
            pair_stores(NPAIR - 1)

            def slot_rows(e, i):
                sp.dma_start(xe[:, i, :], rows(slots_d, e * CAP)).then_inc(ld_xe[i], 16)

            sp.wait_ge(st_scat, 16 * (NPAIR + 1) * TT * TOPK)
            for e in range(RING):
                slot_rows(e, e)
            with sp.Fori(1, E // RING) as r:
                for i in range(RING):
                    sp.wait_ge(ye_ps, RING * r + (i - RING + 1))
                    expert_weights(RING * r + i, i)
                    slot_rows(RING * r + i, i)

            sp.dma_start(gball[:, :, :], mod_d[:, 5 * H:6 * H].partition_broadcast(PN)).then_inc(ld_gb, 16)
            sp.wait_ge(st_xnt, 64 * NPAIR + FREE)
            sp.wait_ge(st_base, 32 * NPAIR + FREE)

            def shared_inputs(q, j):
                for dst, part in ((xs_hi, 0), (xs_lo, 1)):
                    sp.dma_start(dst[:, j, :, :].bitcast(F32), xnt_d[bass.ds(q, 1), :, part, :, :].rearrange("a p c s -> (a p) c s"))\
                      .then_inc(ld_xs[j], 16)

            def residual(tile, par):
                sp.dma_start(bas[:, par, :], rows(base_d, tile * PN)).then_inc(ld_bas[par], 16)

            for j in range(2):
                shared_inputs(j, j)
                residual(j, j)
            for tile in range(NPAIR * TT):
                sp.wait_ge(fin_done, tile + 1)
                sp.dma_start(rows(out, tile * PN), fin[:, tile % 2, :]).then_inc(st_out[tile % 2], 16)
                if tile + 2 < NPAIR * TT:
                    residual(tile + 2, tile % 2)
                q = tile // TT
                if tile % TT == 0 and 0 < q < NPAIR - 1:
                    sp.wait_ge(sh_ps, FT * q)
                    shared_inputs(q + 1, (q + 1) % 2)
            for par in range(2):
                sp.wait_ge(st_out[par], 16 * NPAIR * TT // 2 + FREE)

        @block.scalar
        def _(act):
            for dst, src in ((cosT[:, :], cos_t), (sinT[:, :], sin_t), (mask[:, :], mask_t), (tri[:, :], tri_t),
                             (ebase[:, :], ebase_t), (wnorm[:, :], w_norm.partition_broadcast(PN)),
                             (cwk[:, :], conv_k.rearrange("g t -> (g t)").partition_broadcast(PN)),
                             (cwv[:, :], conv_v.rearrange("g t -> (g t)").partition_broadcast(PN))):
                act.dma_start(dst, src).then_inc(ld_const, 16)
            act.wait_ge(fills, 2)
            act.dma_start(wr[:, :, 0:E], w_router.rearrange("(c p) e -> p c e", p=PN)).then_inc(ld_const, 16)
            act.dma_start(wr[:, :, E:E + 1], w_sgate.rearrange("(c p) e -> p c e", p=PN), allow_slow_non_contiguous=True).then_inc(ld_const, 16)
            act.dma_start(wo[:, :, :], w_o.rearrange("(n p) h -> p n h", p=PN)).then_inc(ld_wo, 16)
            act.wait_ge(ld_c, 32)
            act.activation(sc[:, :], c_sb[:, :], ACT.Silu).then_inc(silu_done, 1)

            def prepare_norm(p):
                act.wait_ge(var1, p + 1)
                act.activation(std1[:, 0, :], mv1[:, :, 1], ACT.Sqrt, bias=LN_EPS).then_inc(std1_done, 1)

            def prepare_h(p, own):
                act.wait_ge(ht_ps, p + 1)
                act.wait_ge(modt_done, 1)
                if later(p):
                    act.wait_ge(rope_done, ROPES * p)
                for c in range(HC):
                    for b in range(2):
                        last = act.activation(qsw[:, c, b * S:(b + 1) * S], PT[c][:, b * S:(b + 1) * S], ACT.Identity,
                                              scale=modT[:, 2 + c, bass.ds(2 * p + b, 1)],
                                              bias=modT[:, c, bass.ds(2 * p + b, 1)])
                own(last)
                if later(p):
                    act.wait_ge(pj_ps, UNITS * p)
                act.activation(hT_hi[:, :, :], qsw[:, :, :], ACT.Copy).then_inc(h_hi_done, 1)

            def project(p, m):
                g, r = m // 4, m % 4
                bank = PJ[m % 2]
                act.wait_ge(pj_ps, UNITS * p + (m + 1))
                if r == 2:
                    if m >= 4 or later(p):
                        act.wait_ge(pj_dve, UNITS * p + (m - 3))
                    act.activation(v0[:, :, 1:S + 1], pair3(bank[:, :]), ACT.Copy,
                                   scale=cwv[:, 2 * g:2 * g + 1]).then_inc(pj_act, 1)
                    return
                rope = 3 * g + ROPE_OF[r]
                if rope >= 2 or later(p):
                    act.wait_ge(rope_done, ROPES * p + (rope - 1))
                half = HD // 2
                act.activation(qsw[0:half, rope % 2, :], bank[half:HD, :], ACT.Copy)
                act.activation(qsw[half:HD, rope % 2, :], bank[0:half, :], ACT.Copy).then_inc(pj_act, 1)

            def k_tap(p, g):
                if g >= 1 or later(p):
                    act.wait_ge(kc_done, GROUPS * p + g)
                act.wait_ge(rope_done, ROPES * p + (3 * g + 1))
                act.activation(k0[:, :, 1:S + 1], pair3(kr[:, :]), ACT.Copy,
                               scale=cwk[:, 2 * g:2 * g + 1]).then_inc(k0_done, 1)

            def exps_of(p, n):
                act.wait_ge(sneg_done, UNITS * p + (n + 1))
                if n >= 3:
                    act.wait_ge(pt_ps, UNITS * p + (n - 2))
                for j, (a, z) in enumerate(((0, PN), (PN, 3 * PN))):
                    last = act.activation(prob[:, n % 3, a:z], sneg[:, n % 2, a:z], ACT.Exp, scale=-1.0,
                                          bias=nmax[:, n % 4, j:j + 1], accum_out=rsum[:, n % 4, j:j + 1])
                last.then_inc(exp_done, 1)

            def v_rows(p, g):
                act.wait_ge(vt_ps, GROUPS * p + (g + 1))
                act.activation(vN[:, g % 2, :], XB[:, :], ACT.Copy).then_inc(vn_done, 1)

            def head_out(p, n):
                g, h, b = n // 4, (n % 4) // 2, n % 2
                act.wait_ge(pv_ps, UNITS * p + (n + 1))
                if n == 0:
                    act.wait_ge(y_ps, TT * p + FREE)
                act.activation(oT[:, 2 * g + h, b * S:(b + 1) * S], OB[:, (n % 2) * S:(n % 2 + 1) * S],
                               ACT.Copy).then_inc(ot_done, 1)

            def slot(p, n):
                m = n + 4
                if m < UNITS:
                    if m % 4 == 2:
                        k_tap(p, m // 4)
                    project(p, m)
                if n < UNITS:
                    exps_of(p, n)
                    if n % 4 == 0:
                        v_rows(p, n // 4)
                if n >= PV_LAG:
                    head_out(p, n - PV_LAG)

            def first_group(p):
                project(p, 0)
                project(p, 1)
                k_tap(p, 0)
                project(p, 2)
                project(p, 3)

            prepare_norm(0)
            for n, j in enumerate(W_ORDER):
                act.wait_ge(ld_w[j], 16)
                act.activation(w_hi[:, :, j * WC:(j + 1) * WC], wraw[:, :, j * WC:(j + 1) * WC], ACT.Copy).then_inc(w_hi_done, 1)
                if n == 0:
                    own = Chain(act, act_own)
                    prepare_h(0, own)
                    assert own.n == ACT_PRE
            act.wait_ge(ld_const, 160)
            act.activation(wr_hi[:, :, :], wr[:, :, :], ACT.Copy).then_inc(wr_hi_done, 1)
            act.wait_ge(fills, 4)
            first_group(0)
            act.wait_ge(st_zero, 16)
            act.wait_ge(w_lo_done, 8)

            with act.Fori(0, NPAIR) as p:
                own = Chain(act, act_own, ACT_PRE + ACT_ROUND * p)
                for n in range(UNITS):
                    slot(p, n)
                    if n == UNITS - 2:
                        prepare_norm(p + 1)
                for n in range(UNITS, UNITS + PV_LAG):
                    slot(p, n)
                prepare_h(p + 1, own)
                for b in range(2):
                    act.wait_ge(var2, 2 * p + (b + 1))
                    act.activation(std2[:, 0, 2 * b:2 * b + 2], mv2[:, 2 * b:2 * b + 2, 1], ACT.Sqrt,
                                   bias=LN_EPS).then_inc(std2_done, 1)
                for b in range(2):
                    act.wait_ge(h2_done, 2 * p + (b + 1))
                    for t in range(2 * b, 2 * b + 2):
                        last = act.activation(xn[:, t, :], h2[:, t, :], ACT.Square, accum_out=rms[:, 0, t:t + 1])
                    own(last)
                    act.activation(rms[:, 1, 2 * b:2 * b + 2], rms[:, 0, 2 * b:2 * b + 2], ACT.Sqrt, scale=1.0 / H,
                                   bias=RMS_EPS).then_inc(rms_done, 1)
                first_group(p + 1)
                for b in range(2):
                    act.wait_ge(xnt_ps, 2 * p + (b + 1))
                    act.wait_ge(st_xnt, 64 * p + 32 * b + FREE)
                    act.wait_ge(lg_ps, 2 * p + b + FREE)
                    for c in range(HC):
                        last = act.activation(xnT_hi[:, c, :], PT[c][:, b * S:(b + 1) * S], ACT.Copy)
                    last.then_inc(xnt_hi_done, 1)
                act.wait_ge(z_done, p + 1)
                act.activation(red[:, 2, :], XB[:, 0:TT * LCOL].rearrange("p (t c) -> p t c", c=LCOL)[:, :, E], ACT.Exp, scale=-1.0)
                act.activation(ex[:, :, :], zz[:, :, 0:E], ACT.Exp).then_inc(ex_done, 1)
                assert own.n == ACT_ROUND, own.n

            act.wait_ge(ld_sw, 32)
            act.activation(sw_hi[:, :, :], swraw[:, :, :], ACT.Copy).then_inc(sw_hi_done, 1)

            def expert_slot(base, n, lo=0, hi=10 ** 9):
                if lo <= n - 1 < hi:
                    act.wait_ge(gu_ps, base + n)
                    if n - 1 >= 2 or later(base):
                        act.wait_ge(hh_done, base + (n - 2))
                    act.activation(sgl[:, (n - 1) % 2, :], SC[(n - 1) % 2][:, 0:F], ACT.Silu).then_inc(sgl_done, 1)
                if lo <= n - 2 < hi:
                    act.wait_ge(hh_ps, base + (n - 1))
                    if n - 2 >= 2 or later(base):
                        act.wait_ge(ye_ps, base + (n - 3))
                    act.activation(hhT[:, (n - 2) % 2, :], PT[(n - 2) % 2][0:FH, 0:2 * PN], ACT.Copy).then_inc(hht_done, 1)
                if lo <= n - 3 < hi:
                    act.wait_ge(ye_done, base + (n - 2))
                    act.dma_start(rows(y_d, (base + (n - 3)) * CAP), ye[:, (n - 3) % 2, :]).then_inc(st_y[(n - 3) % 2], 16)

            for n in range(RING):
                expert_slot(0, n)
            with act.Fori(1, E // RING) as r:
                for n in range(RING):
                    expert_slot(RING * r, n, lo=-RING)
            for n in range(RING - 1):
                expert_slot(E, n, lo=-RING, hi=0)

            with act.Fori(0, NPAIR // 2) as r:
                for j in range(2):
                    for f in range(FT):
                        fw = min(PN, FS - f * PN)
                        k = FT * j + f
                        act.wait_ge(sh_ps, 2 * FT * r + (k + 1))
                        if k >= 2:
                            act.wait_ge(hs_done, 2 * FT * r + (k - 1) + FREE)
                        act.activation(sg2[0:fw, f % 2, :], PJ[f % 2][0:fw, :], ACT.Silu).then_inc(sg2_done, 1)

        @block.gpsimd
        def _(pool):
            for start in (y_ps, yg_done, route_done, xnt_lo_done, lg_ps, base_done, hs_done, acc_done, dn_ps,
                          st_xnt, st_base, st_out[0], st_out[1]):
                pool.sem_inc(start, FREE)
            pool.memset(vN[:, :, :], 0.0).then_inc(fills, 1)
            pool.memset(wr[:, :, :], 0.0).then_inc(fills, 1)
            pool.memset(k0[:, :, 0:1], 0.0).then_inc(fills, 1)
            pool.memset(v0[:, :, 0:1], 0.0).then_inc(fills, 1)
            pool.memset(ones[:, :], 1.0).then_inc(fills, 1)
            pool.memset(carry[:, :, :], 0.0).then_inc(fills, 1)
            pool.memset(modT[:, :, B:B + 2], 0.0).then_inc(fills, 1)

            def rope_sin(p, m):
                g, r = m // 4, m % 4
                if r == 2:
                    return
                rope = 3 * g + ROPE_OF[r]
                pool.wait_ge(pj_act, UNITS * p + (m + 1))
                pool.tensor_tensor(pair3(qsw[:, rope % 2, :]), pair3(qsw[:, rope % 2, :]), both(sinT[:, :]),
                                   ALU.mult).then_inc(t2_done, 1)

            def normalise(p, n):
                pool.wait_ge(rinv_done, UNITS * p + (n + 1))
                met(pool)
                for j, (a, z) in enumerate(((0, PN), (PN, 3 * PN))):
                    last = pool.tensor_scalar(prob[:, n % 3, a:z], prob[:, n % 3, a:z], rinv[:, n % 4, j:j + 1], None, ALU.mult)
                last.then_inc(norm_done, 1)

            def scatter(c):
                pool.indirect_dma_start(out=slots_d, out_offset=bass.IndirectOffsetOnAxis(ap=sidx[:, c:c + 1], axis=0),
                                        in_=xn[:, c // TOPK, :], in_offset=None, bounds_check=E * CAP - 1,
                                        oob_is_err=False).then_inc(st_scat, 16)

            pool.wait_ge(ld_const, 160)
            for m in range(4):
                rope_sin(0, m)
            pool.wait_ge(modt_done, 1)
            pool.wait_ge(st_mod, 16)
            pool.memset(sidx[:, :], SKIP).then_inc(fills, 1)
            pool.memset(xn[:, :, :], 0.0).then_inc(fills, 1)
            pool.wait_ge(fills, 9)
            pool.wait_ge(st_zero, 16)
            with pool.Fori(0, NPAIR) as p:
                own = Chain(pool, pool_own, POOL_ROUND * p)
                for n in range(UNITS + 1):
                    if n + 4 < UNITS:
                        rope_sin(p, n + 4)
                    if n >= 1:
                        normalise(p, n - 1)
                    if n < TT * TOPK:
                        if n == 0:
                            pool.wait_ge(route_done, p + FREE)
                            met(pool)
                        scatter(n)
                pool.wait_ge(ld_xres, 16 * (p + 1))
                for b in range(2):
                    t = slice(2 * b, 2 * b + 2)
                    pool.wait_ge(yg_done, 2 * p + (b + 1) + FREE)
                    pool.tensor_tensor(xres[:, t, :], xres[:, t, :], yg[:, b, :, :], ALU.add).then_inc(x1_done, 1)
                for b in range(2):
                    t = slice(2 * b, 2 * b + 2)
                    pool.wait_ge(xh2_done, 2 * p + (b + 1))
                    own(pool.tensor_tensor(h2[:, t, :], h2[:, t, :],
                                           bcm[:, b, 2 * H:3 * H].unsqueeze(1).broadcast_to([PN, 2, H]), ALU.mult))
                    pool.tensor_tensor(h2[:, t, :], h2[:, t, :],
                                       bcm[:, b, H:2 * H].unsqueeze(1).broadcast_to([PN, 2, H]), ALU.add).then_inc(h2_done, 1)
                for m in range(4):
                    rope_sin(p + 1, m)
                for b in range(2):
                    t = slice(2 * b, 2 * b + 2)
                    pool.wait_ge(xn_done, 2 * p + (b + 1))
                    pool.wait_ge(rms_done, 2 * p + (b + 1))
                    own(pool.tensor_tensor(h2[:, t, :], h2[:, t, :],
                                           bcm[:, b, 3 * H:4 * H].unsqueeze(1).broadcast_to([PN, 2, H]), ALU.mult))
                    pool.tensor_tensor(h2[:, t, :], h2[:, t, :], xres[:, t, :], ALU.add).then_inc(base_done, 1)
                assert own.n == POOL_ROUND, own.n

            for c in range(TT * TOPK):
                if c == 0:
                    pool.wait_ge(sidx_done, NPAIR)
                scatter(c)

            for par in range(2):
                pool.wait_ge(st_y[par], 16 * E // 2)
            with pool.Fori(0, NPAIR // 2) as r:
                for j in range(2):
                    for t in range(TT):
                        pool.wait_ge(idx_done, 2 * r + (j + 1))
                        pool.wait_ge(acc_done, (2 * TT * r + (t + 1 if j else 0)) + FREE)
                        met(pool)
                        for k in range(TOPK):
                            c = t * TOPK + k
                            pool.indirect_dma_start(out=gat[:, t, k, :], out_offset=None, in_=y_d,
                                                    in_offset=bass.IndirectOffsetOnAxis(ap=idxc[:, j, c:c + 1], axis=0))\
                                .then_inc(ld_gat[t], 16)

        @block.vector
        def _(dve):
            pre = Chain(dve, dve_own)
            dve.wait_ge(sct_ps, 1)
            dve.tensor_copy(scT[:, :, :], PT[0][:, 0:HC * B].rearrange("p (c b) -> p c b", b=B)).then_inc(sct_done, 1)
            dve.wait_ge(mod_ps, 1)
            for j, bk in enumerate((PJ[0], PJ[1], SC[0])):
                pre(dve.tensor_copy(mod[:, j * 512:(j + 1) * 512], bk[0:B, :]))
            for part in (1, 4):
                pre(dve.tensor_scalar(mod[:, part * H:(part + 1) * H], mod[:, part * H:(part + 1) * H], 1.0, None, ALU.add))
            for part in (2, 5):
                gate = mod[:, part * H:(part + 1) * H]
                pre(dve.scalar_tensor_tensor(gabs[:, :], gate, -1.0, gate, ALU.mult, ALU.max))
                pre(dve.tensor_scalar(gabs[:, :], gabs[:, :], 0.25, None, ALU.max))
                pre(dve.tensor_scalar(gsgn[:, :], gate, 0.0, 2.0, ALU.is_ge, ALU.mult))
                pre(dve.scalar_tensor_tensor(gate, gsgn[:, :], -1.0, gabs[:, :], ALU.add, ALU.mult))
            dve.tensor_copy(gsgn[:, 0:1], gabs[:, 0:1]).then_inc(mod_done, 1)
            dve.wait_ge(modt_ps, 1)
            dve.tensor_copy(modT[:, :, 0:B], PT[0][:, 64:64 + 4 * B].rearrange("p (k b) -> p k b", b=B)).then_inc(modt_done, 1)

            def prepare_norm(p, own):
                dve.wait_ge(ld_xin, 16 * (p + 1))
                for t in range(TT):
                    last = dve.bn_stats(st1[:, t, :], xin[:, t, :])
                own(last, plain=True)
                for t in range(TT):
                    last = dve.bn_aggr(mv1[:, t, :], st1[:, t, :])
                last.then_inc(var1, 1)
                dve.wait_ge(std1_done, p + 1)
                own(dve.reciprocal(std1[:, 1, :], std1[:, 0, :]))
                for t in range(TT):
                    last = dve.tensor_scalar(xin[:, t, :], xin[:, t, :], mv1[:, t, 0:1], std1[:, 1, t:t + 1],
                                             ALU.subtract, ALU.mult)
                last.then_inc(xhat_done, 1)

            def prepare_lo(p):
                dve.wait_ge(h_hi_done, p + 1)
                dve.tensor_tensor(hT_lo[:, :, :], qsw[:, :, :], hT_hi[:, :, :].bitcast(F32), ALU.subtract).then_inc(h_lo_done, 1)

            def rope_buffer(m):
                g, r = m // 4, m % 4
                return kr[:, :] if r == 0 else qr[:, 0 if r == 1 else 1, g % 2, :]

            def project(p, m):
                g, r = m // 4, m % 4
                dve.wait_ge(pj_act, UNITS * p + (m + 1))
                if r == 2:
                    if g >= 1 or later(p):
                        dve.wait_ge(vt_ps, GROUPS * p + g)
                    dve.scalar_tensor_tensor(pair3(vT[:, :]), pair3(PJ[m % 2][:, :]), cwv[:, 2 * g + 1:2 * g + 2],
                                             v0[:, :, 0:S], ALU.mult, ALU.add).then_inc(pj_dve, 1)
                    return
                dve.tensor_tensor(pair3(rope_buffer(m)), pair3(PJ[m % 2][:, :]), both(cosT[:, :]), ALU.mult).then_inc(pj_dve, 1)

            def rope_add(p, m):
                g, r = m // 4, m % 4
                if r == 2:
                    return
                rope = 3 * g + ROPE_OF[r]
                dve.wait_ge(t2_done, ROPES * p + (rope + 1))
                dve.wait_ge(pj_dve, UNITS * p + (m + 1))
                dve.tensor_tensor(rope_buffer(m), rope_buffer(m), qsw[:, rope % 2, :], ALU.add).then_inc(rope_done, 1)

            def k_conv(p, g):
                dve.wait_ge(k0_done, GROUPS * p + (g + 1))
                dve.scalar_tensor_tensor(pair3(kc[:, g % 2, :]), pair3(kr[:, :]), cwk[:, 2 * g + 1:2 * g + 2],
                                         k0[:, :, 0:S], ALU.mult, ALU.add).then_inc(kc_done, 1)

            def first_group(p):
                project(p, 0)
                project(p, 1)
                rope_add(p, 0)
                project(p, 2)
                k_conv(p, 0)
                rope_add(p, 1)
                project(p, 3)

            def scores(p, n):
                dve.wait_ge(sc_ps, UNITS * p + (n + 1))
                if n >= 2:
                    dve.wait_ge(exp_done, UNITS * p + (n - 1))
                met(dve)
                for j, (a, z) in enumerate(((0, PN), (PN, 3 * PN))):
                    last = dve.tensor_tensor_reduce(out=sneg[:, n % 2, a:z], in0=SC[n % 2][:, a:z], in1=mask[:, a:z],
                                                    scale=-float(HD) ** -0.5, scalar=3.4e38, op0=ALU.add, op1=ALU.min,
                                                    accum_out=nmax[:, n % 4, j:j + 1])
                last.then_inc(sneg_done, 1)

            def row_sums(p, n):
                dve.wait_ge(exp_done, UNITS * p + (n + 1))
                dve.reciprocal(rinv[:, n % 4, :], rsum[:, n % 4, :]).then_inc(rinv_done, 1)

            def transposed(p, n):
                dve.wait_ge(pt_ps, UNITS * p + (n + 1))
                if n >= 2:
                    dve.wait_ge(pv_ps, UNITS * p + (n - 1))
                dve.tensor_copy(pT[:, n % 2, :], PT[n % 2][:, 0:3 * PN]).then_inc(pt_done, 1)

            def slot(p, n):
                m = n + 4
                if m < UNITS:
                    project(p, m)
                if n < UNITS:
                    scores(p, n)
                if 0 < n <= UNITS:
                    row_sums(p, n - 1)
                if m - 1 < UNITS:
                    rope_add(p, m - 1)
                if m < UNITS and m % 4 == 2:
                    k_conv(p, m // 4)
                if T_LAG <= n < UNITS + T_LAG:
                    transposed(p, n - T_LAG)

            prepare_norm(0, pre)
            for n, j in enumerate(W_ORDER):
                dve.wait_ge(w_hi_done, n + 1)
                dve.tensor_tensor(w_lo[:, :, j * WC:(j + 1) * WC], wraw[:, :, j * WC:(j + 1) * WC],
                                  w_hi[:, :, j * WC:(j + 1) * WC].bitcast(F32), ALU.subtract).then_inc(w_lo_done, 1)
                if n == 0:
                    prepare_lo(0)
            dve.wait_ge(wr_hi_done, 1)
            dve.tensor_tensor(wr_lo[:, :, :], wr[:, :, :], wr_hi[:, :, :].bitcast(F32), ALU.subtract).then_inc(wr_lo_done, 1)
            dve.wait_ge(fills, 7)
            dve.wait_ge(ld_const, 160)
            first_group(0)
            dve.wait_ge(st_mod, 16)
            pre(dve.memset(zz[:, :, E:E + TOPK], SENTINEL))
            assert pre.n == DVE_PRE, pre.n

            with dve.Fori(0, NPAIR) as p:
                own = Chain(dve, dve_own, DVE_PRE + DVE_ROUND * p)
                for n in range(UNITS + T_LAG):
                    slot(p, n)
                    if n == UNITS - 2:
                        prepare_norm(p + 1, own)
                dve.wait_ge(ld_bcm, 32 * (p + 1))
                dve.wait_ge(st_base, 32 * p + FREE)
                dve.wait_ge(st_scat, 16 * TT * TOPK * (p + 1))
                prepare_lo(p + 1)
                for b in range(2):
                    dve.wait_ge(y_ps, TT * p + (2 * b + 2) + FREE)
                    dve.tensor_tensor(yg[:, b, :, :], SC[b][:, :].rearrange("p (t h) -> p t h", h=H),
                                      bcm[:, b, 0:H].unsqueeze(1).broadcast_to([PN, 2, H]), ALU.mult).then_inc(yg_done, 1)
                for b in range(2):
                    dve.wait_ge(x1_done, 2 * p + (b + 1))
                    for t in range(2 * b, 2 * b + 2):
                        last = dve.bn_stats(st2[:, t, :], xres[:, t, :])
                    own(last, plain=True)
                    for t in range(2 * b, 2 * b + 2):
                        last = dve.bn_aggr(mv2[:, t, :], st2[:, t, :])
                    last.then_inc(var2, 1)
                for b in range(2):
                    dve.wait_ge(std2_done, 2 * p + (b + 1))
                    own(dve.reciprocal(std2[:, 1, 2 * b:2 * b + 2], std2[:, 0, 2 * b:2 * b + 2]))
                    for t in range(2 * b, 2 * b + 2):
                        last = dve.tensor_scalar(h2[:, t, :], xres[:, t, :], mv2[:, t, 0:1], std2[:, 1, t:t + 1],
                                                 ALU.subtract, ALU.mult)
                    last.then_inc(xh2_done, 1)
                for b in range(2):
                    dve.wait_ge(rms_done, 2 * p + (b + 1))
                    own(dve.reciprocal(rms[:, 2, 2 * b:2 * b + 2], rms[:, 1, 2 * b:2 * b + 2]))
                    for t in range(2 * b, 2 * b + 2):
                        last = dve.scalar_tensor_tensor(xn[:, t, :], h2[:, t, :], rms[:, 2, t:t + 1], wnorm[:, :],
                                                        ALU.mult, ALU.mult)
                    last.then_inc(xn_done, 1)
                first_group(p + 1)
                for b in range(2):
                    dve.wait_ge(xnt_hi_done, 2 * p + (b + 1))
                    dve.wait_ge(st_xnt, 64 * p + 32 * b + FREE)
                    for c in range(HC):
                        last = dve.tensor_tensor(xnT_lo[:, c, :], PT[c][:, b * S:(b + 1) * S],
                                                 xnT_hi[:, c, :].bitcast(F32), ALU.subtract)
                    last.then_inc(xnt_lo_done, 1)
                logits = XB[:, 0:TT * LCOL].rearrange("p (t c) -> p t c", c=LCOL)[:, :, 0:E]
                dve.wait_ge(lg_ps, 2 * p + 2 + FREE)
                own(dve.tensor_reduce(red[:, 0, :], logits, AXX, ALU.max))
                own(dve.tensor_tensor(zz[:, :, 0:E], logits, red[:, 0, :].unsqueeze(2).broadcast_to([PN, TT, E]), ALU.subtract))
                dve.tensor_scalar(zz[:, :, 0:E], zz[:, :, 0:E], PROB_FLOOR, None, ALU.max).then_inc(z_done, 1)
                dve.wait_ge(z_done, p + 1)
                met(dve)
                for t in range(TT):
                    last = dve.max(top8[:, t, :], zz[:, t, :])
                own(last, plain=True)
                for t in range(TT):
                    last = dve.match_replace(zz2[:, t, :], top8[:, t, :], zz[:, t, :], TAKEN)
                own(last)
                dve.tensor_scalar(chosen[:, :, :], zz2[:, :, 0:E], TAKEN / 2, None, ALU.is_lt).then_inc(chosen_done, 1)
                dve.wait_ge(ex_done, p + 1)
                own(dve.tensor_reduce(red[:, 1, :], ex[:, :, :], AXX, ALU.add))
                own(dve.reciprocal(red[:, 3, :], red[:, 1, :]))
                own(dve.tensor_tensor(ex[:, :, :], ex[:, :, :], red[:, 3, :].unsqueeze(2).broadcast_to([PN, TT, E]), ALU.mult))
                own(dve.tensor_scalar(red[:, 2, :], red[:, 2, :], 1.0, None, ALU.add))
                own(dve.reciprocal(sgate[:, bass.ds(p, 1), :].rearrange("p a t -> p (a t)"), red[:, 2, :]))
                dve.wait_ge(pos_ps, p + 1)
                pos = XB[:, 256:256 + TT * E].rearrange("p (t e) -> p t e", e=E)
                own(dve.scalar_tensor_tensor(kept[:, :, :], pos, float(CAP), chosen[:, :, :], ALU.is_lt, ALU.mult))
                own(dve.tensor_tensor(key[:, :, :], pos, ebase[:, :].unsqueeze(1).broadcast_to([PN, TT, E]), ALU.add))
                own(dve.tensor_tensor(key[:, :, :], key[:, :, :], kept[:, :, :], ALU.mult))
                own(dve.tensor_tensor(ex[:, :, :], ex[:, :, :], kept[:, :, :], ALU.mult), plain=True)
                for t in range(TT):
                    last = dve.max(key8[:, t, :], key[:, t, :])
                own(last)
                own(dve.tensor_scalar(late[:, :, :], key8[:, :, 0:TOPK], 0.0, float(SKIP), ALU.is_equal, ALU.mult))
                dve.scalar_tensor_tensor(sidx[:, :].rearrange("p (t k) -> p t k", k=TOPK), key8[:, :, 0:TOPK], -1.0,
                                         late[:, :, :], ALU.add, ALU.add).then_inc(sidx_done, 1)
                own(dve.tensor_scalar(gidx[:, bass.ds(p, 1), :].rearrange("p a (t k) -> p (a t) k", k=TOPK),
                                      key8[:, :, 0:TOPK], -1.0, 0.0, ALU.add, ALU.max))
                own(dve.tensor_tensor(eq[:, :, :, :], key[:, :, :].unsqueeze(2).broadcast_to([PN, TT, TOPK, E]),
                                      key8[:, :, 0:TOPK].unsqueeze(3).broadcast_to([PN, TT, TOPK, E]), ALU.is_equal))
                own(dve.tensor_tensor(eq[:, :, :, :], eq[:, :, :, :],
                                      ex[:, :, :].unsqueeze(2).broadcast_to([PN, TT, TOPK, E]), ALU.mult))
                own(dve.tensor_reduce(wsel[:, bass.ds(p, 1), :].rearrange("p a (t k) -> p (a t) k", k=TOPK),
                                      eq[:, :, :, :], AXX, ALU.add))
                own(dve.tensor_reduce(carry[:, 1, :], chosen[:, :, :].rearrange("p t e -> p e t"), AXX, ALU.add))
                own(dve.tensor_tensor(carry[:, 0, :], carry[:, 0, :], carry[:, 1, :], ALU.add))
                assert own.n == DVE_ROUND, own.n
                dve.tensor_copy(carry[:, 1, 0:1], carry[:, 0, 0:1]).then_inc(route_done, 1)

            dve.wait_ge(sw_hi_done, 1)
            dve.tensor_tensor(sw_lo[:, :, :], swraw[:, :, :], sw_hi[:, :, :].bitcast(F32), ALU.subtract).then_inc(sw_lo_done, 1)

            def expert_slot(base, n, lo=0, hi=10 ** 9):
                if lo <= n < hi:
                    dve.wait_ge(xe_ps, base + (n + 1))
                    if n >= 2 or later(base):
                        dve.wait_ge(gu_ps, base + (n - 1))
                    dve.tensor_copy(xeT[:, n % 2, :], PJ[n % 2][:, 0:H]).then_inc(xe_done, 1)
                if lo <= n - 1 < hi:
                    dve.wait_ge(sgl_done, base + n)
                    if n - 1 >= 2 or later(base):
                        dve.wait_ge(hh_ps, base + (n - 2))
                    dve.tensor_tensor(hh[:, (n - 1) % 2, :], SC[(n - 1) % 2][:, F:2 * F], sgl[:, (n - 1) % 2, :],
                                      ALU.mult).then_inc(hh_done, 1)
                if lo <= n - 3 < hi:
                    dve.wait_ge(ye_ps, base + (n - 2))
                    if n - 3 >= 2 or later(base):
                        dve.wait_ge(st_y[(n - 3) % 2], st_count(base, n - 3))
                    bk = (OB, XB)[(n - 3) % 2]
                    dve.tensor_copy(ye[:, (n - 3) % 2, :], bk[:, 0:H]).then_inc(ye_done, 1)

            def st_count(base, e):
                return 8 * base + 16 * (e // 2)

            for n in range(RING):
                expert_slot(0, n)
            with dve.Fori(1, E // RING) as r:
                for n in range(RING):
                    expert_slot(RING * r, n, lo=-RING)
            for n in range(RING - 1):
                expert_slot(E, n, lo=-RING, hi=0)

            dve.wait_ge(ld_gb, 16)
            with dve.Fori(0, NPAIR // 2) as r:
                for j in range(2):
                    dve.tensor_copy(idxc[:, j, :], gidx[:, bass.ds(2 * r + j, 1), :].rearrange("p a k -> p (a k)"))\
                       .then_inc(idx_done, 1)
                for j in range(2):
                    for f in range(FT):
                        fw = min(PN, FS - f * PN)
                        k = FT * j + f
                        dve.wait_ge(sg2_done, 2 * FT * r + (k + 1))
                        if f == 0:
                            dve.wait_ge(dn_ps, 2 * TT * r + FREE)
                        dve.tensor_tensor(hs[0:fw, j, f, :], SC[f % 2][0:fw, :], sg2[0:fw, f % 2, :], ALU.mult).then_inc(hs_done, 1)
                    for t in range(TT):
                        n = TT * j + t
                        own = Chain(dve, acc_own, 5 * (2 * TT * r + n))
                        bk = (OB, XB)[t % 2]
                        dve.wait_ge(dn_ps, 2 * TT * r + (n + 1) + FREE)
                        if n >= 2:
                            dve.wait_ge(fin_done, 2 * TT * r + (n - 1))
                        own(dve.tensor_scalar(acc[:, t % 2, :], bk[:, 0:H],
                                              sgate[:, bass.ds(2 * r + j, 1), t:t + 1].rearrange("p a t -> p (a t)"), None, ALU.mult))
                        dve.wait_ge(ld_gat[t], 16 * TOPK * 2 * r + 16 * TOPK * (j + 1))
                        for k in range(TOPK):
                            ins = dve.scalar_tensor_tensor(
                                acc[:, t % 2, :], gat[:, t, k, :],
                                wsel[:, bass.ds(2 * r + j, 1), t * TOPK + k:t * TOPK + k + 1].rearrange("p a t -> p (a t)"),
                                acc[:, t % 2, :], ALU.mult, ALU.add)
                            own(ins)
                        dve.wait_ge(st_out[t % 2], 16 * TT * r + 16 * (n // 2) + FREE)
                        dve.tensor_tensor(fin[:, t % 2, :], acc[:, t % 2, :],
                                          gball[:, bass.ds(4 * r + 2 * j + t // 2, 1), :].rearrange("p a h -> p (a h)"),
                                          ALU.mult).then_inc(acc_done, 1)
                        dve.wait_ge(acc_done, 2 * TT * r + (n + 1) + FREE)
                        dve.wait_ge(ld_bas[t % 2], 16 * TT * r + 16 * (n // 2 + 1))
                        dve.tensor_tensor(fin[:, t % 2, :], fin[:, t % 2, :], bas[:, t % 2, :], ALU.add).then_inc(fin_done, 1)

        @block.tensor
        def _(pe):
            def halves(out_ap, pieces, hi_lo):
                (w1, w2), (x1, x2) = hi_lo
                steps = [(c, a, b_) for c in range(pieces) for a, b_ in ((w1, x1), (w1, x2), (w2, x1))]
                for n, (c, a, b_) in enumerate(steps):
                    last = pe.matmul(out_ap, a(c), b_(c), start=(n == 0), stop=(n == len(steps) - 1))
                return last

            pe.wait_ge(silu_done, 1)
            for c in range(HC):
                last = pe.transpose(PT[0][:, c * B:(c + 1) * B], sc[:, c * PN:(c + 1) * PN], ident[0:B, 0:B])
            last.then_inc(sct_ps, 1)
            pe.wait_ge(sct_done, 1)
            pe.wait_ge(ld_wm, 16)
            for j, bk in enumerate((PJ[0], PJ[1], SC[0])):
                for c in range(HC):
                    last = pe.matmul(bk[0:B, :], scT[:, c, :], wm[:, c, j * 512:(j + 1) * 512], start=(c == 0), stop=(c == HC - 1))
            last.then_inc(mod_ps, 1)
            pe.wait_ge(mod_done, 1)
            for k in range(4):
                last = pe.transpose(PT[0][:, 64 + k * B:64 + (k + 1) * B], mod[:, k * PN:(k + 1) * PN], ident[0:B, 0:B])
            last.then_inc(modt_ps, 1)
            pe.wait_ge(modt_done, 1)

            def prepare_t(p):
                pe.wait_ge(xhat_done, p + 1)
                for c in range(HC):
                    for t in range(TT):
                        last = pe.transpose(PT[c][:, t * PN:(t + 1) * PN], xin[:, t, c * PN:(c + 1) * PN], ident[:, :])
                last.then_inc(ht_ps, 1)

            def project(p, m):
                g, r = m // 4, m % 4
                head = {0: NH + g, 1: 2 * g, 2: NH + NKV + g, 3: 2 * g + 1}[r]
                cols = slice(head * HD, (head + 1) * HD)
                if m == 0:
                    pe.wait_ge(h_lo_done, p + 1)
                if m >= 2 or later(p):
                    pe.wait_ge(pj_act, UNITS * p + (m - 1))
                    pe.wait_ge(pj_dve, UNITS * p + (m - 1))
                halves(PJ[m % 2][:, :], HC,
                       ((lambda c: w_hi[:, c, cols], lambda c: w_lo[:, c, cols]),
                        (lambda c: hT_hi[:, c, :], lambda c: hT_lo[:, c, :]))).then_inc(pj_ps, 1)

            def scores(p, n):
                g, h, b = n // 4, (n % 4) // 2, n % 2
                if n == 0:
                    pe.wait_ge(yg_done, 2 * p + FREE)
                if n >= 2:
                    pe.wait_ge(sneg_done, UNITS * p + (n - 1))
                if n % 4 == 0:
                    pe.wait_ge(kc_done, GROUPS * p + (g + 1))
                if n % 2 == 0:
                    pe.wait_ge(rope_done, ROPES * p + (3 * g + h + 2))
                q = qr[:, h, g % 2, b * S:(b + 1) * S]
                k = kc[:, g % 2, b * S:(b + 1) * S]
                pe.matmul(SC[n % 2][:, 0:PN], q[:, 0:PN], k[:, 0:PN], start=True, stop=True)
                pe.matmul(SC[n % 2][:, PN:3 * PN], q[:, PN:S], k, start=True, stop=True).then_inc(sc_ps, 1)

            def v_transpose(p, g):
                pe.wait_ge(pj_dve, UNITS * p + (4 * g + 3))
                if g >= 1:
                    pe.wait_ge(vn_done, GROUPS * p + g)
                else:
                    pe.wait_ge(route_done, p + FREE)
                for j in range(TT):
                    last = pe.transpose(XB[:, j * PN:(j + 1) * PN], vT[:, j * PN:(j + 1) * PN], ident[:, :])
                last.then_inc(vt_ps, 1)

            def p_transpose(p, n):
                pe.wait_ge(norm_done, UNITS * p + (n + 1))
                if n >= 2:
                    pe.wait_ge(pt_done, UNITS * p + (n - 1))
                elif n == 0:
                    pe.wait_ge(xnt_lo_done, 2 * p + FREE)
                for j in range(3):
                    last = pe.transpose(PT[n % 2][:, j * PN:(j + 1) * PN], prob[:, n % 3, j * PN:(j + 1) * PN], ident[:, :])
                last.then_inc(pt_ps, 1)

            def weighted_v(p, n):
                g, b = n // 4, n % 2
                pe.wait_ge(pt_done, UNITS * p + (n + 1))
                if n >= 1:
                    pe.wait_ge(ot_done, UNITS * p + n)
                if n % 4 == 0:
                    pe.wait_ge(vn_done, GROUPS * p + (g + 1))
                o = OB[:, (n % 2) * S:(n % 2 + 1) * S]
                v = vN[:, g % 2, b * S:(b + 1) * S]
                pe.matmul(o, v[:, 0:PN], pT[:, n % 2, 0:S], start=True, stop=False)
                pe.matmul(o[:, PN:S], v[:, PN:S], pT[:, n % 2, S:S + PN], start=False, stop=True).then_inc(pv_ps, 1)

            prepare_t(0)
            for m in range(4):
                if m in (0, 1, 2):
                    pe.wait_ge(w_lo_done, m + 1)
                project(0, m)
            pe.wait_ge(w_lo_done, 8)
            pe.wait_ge(ld_wo, 16)
            pe.wait_ge(wr_lo_done, 1)
            pe.wait_ge(fills, 7)
            pe.wait_ge(ld_const, 160)

            with pe.Fori(0, NPAIR) as p:
                for n in range(UNITS + PV_LAG):
                    if n + 4 < UNITS:
                        project(p, n + 4)
                    if n < UNITS:
                        scores(p, n)
                        if n % 4 == 0:
                            v_transpose(p, n // 4)
                    if T_LAG <= n < UNITS + T_LAG:
                        p_transpose(p, n - T_LAG)
                    if n >= PV_LAG:
                        weighted_v(p, n - PV_LAG)
                pe.wait_ge(pt_done, UNITS * (p + 1))
                prepare_t(p + 1)
                pe.wait_ge(ot_done, UNITS * (p + 1))
                for t in range(TT):
                    for h in range(NH):
                        last = pe.matmul(SC[t // 2][:, (t % 2) * H:(t % 2 + 1) * H], oT[:, h, t * PN:(t + 1) * PN],
                                         wo[:, h, :], start=(h == 0), stop=(h == NH - 1))
                    last.then_inc(y_ps, 1)
                for m in range(4):
                    project(p + 1, m)
                pe.wait_ge(h_hi_done, p + 2)
                for b in range(2):
                    pe.wait_ge(xn_done, 2 * p + (b + 1))
                    for c in range(HC):
                        for t in range(2 * b, 2 * b + 2):
                            last = pe.transpose(PT[c][:, t * PN:(t + 1) * PN], xn[:, t, c * PN:(c + 1) * PN], ident[:, :])
                    last.then_inc(xnt_ps, 1)
                    pe.wait_ge(xnt_lo_done, 2 * p + (b + 1) + FREE)
                    for t in range(2 * b, 2 * b + 2):
                        tk = slice((t % 2) * PN, (t % 2 + 1) * PN)
                        last = halves(XB[:, t * LCOL:t * LCOL + E + 2], HC,
                                      ((lambda c: xnT_hi[:, c, tk], lambda c: xnT_lo[:, c, tk]),
                                       (lambda c: wr_hi[:, c, :], lambda c: wr_lo[:, c, :])))
                    last.then_inc(lg_ps, 1)
                pe.wait_ge(chosen_done, p + 1)
                pe.wait_ge(ex_done, p + 1)
                for t in range(TT):
                    o = XB[:, 256 + t * E:256 + (t + 1) * E]
                    pe.matmul(o, ones[:, :], carry[:, 0, :], start=True, stop=False)
                    for u in range(t):
                        pe.matmul(o, ones[:, :], chosen[:, u, :], start=False, stop=False)
                    last = pe.matmul(o, tri[:, :], chosen[:, t, :], start=False, stop=True)
                last.then_inc(pos_ps, 1)

            def expert_slot(base, n, rnd, lo=0, hi=10 ** 9):
                if lo <= n < hi:
                    pe.wait_ge(ld_xe[n % RING], 16 * rnd)
                    if n >= 2 or later(base):
                        pe.wait_ge(xe_done, base + (n - 1))
                    for c in range(HC):
                        last = pe.transpose(PJ[n % 2][:, c * PN:(c + 1) * PN], xe[:, n % RING, c * PN:(c + 1) * PN], ident[:, :])
                    last.then_inc(xe_ps, 1)
                if lo <= n - 1 < hi:
                    e, i = n - 1, (n - 1) % RING
                    pe.wait_ge(xe_done, base + (e + 1))
                    pe.wait_ge(ld_e[i], 48 * (rnd if e >= 0 else rnd - 1))
                    if e >= 2 or later(base):
                        pe.wait_ge(hh_done, base + (e - 1))
                    for c in range(HC):
                        last = pe.matmul(SC[e % 2][:, 0:2 * F], xeT[:, e % 2, c * PN:(c + 1) * PN], wgu[:, i, c, :],
                                         start=(c == 0), stop=(c == HC - 1))
                    last.then_inc(gu_ps, 1)
                if lo <= n - 2 < hi:
                    e = n - 2
                    pe.wait_ge(hh_done, base + (e + 1))
                    if e >= 2 or later(base):
                        pe.wait_ge(hht_done, base + (e - 1))
                    for c in range(2):
                        last = pe.transpose(PT[e % 2][0:FH, c * PN:(c + 1) * PN], hh[:, e % 2, c * FH:(c + 1) * FH], ident[:, :])
                    last.then_inc(hh_ps, 1)
                if lo <= n - 3 < hi:
                    e, i = n - 3, (n - 3) % RING
                    pe.wait_ge(hht_done, base + (e + 1))
                    if e >= 2 or later(base):
                        pe.wait_ge(ye_done, base + (e - 1))
                    bk = (OB, XB)[e % 2]
                    for c in range(2):
                        last = pe.matmul(bk[:, 0:H], hhT[:, e % 2, c * PN:(c + 1) * PN], wd[:, i, c, :],
                                         start=(c == 0), stop=(c == 1))
                    last.then_inc(ye_ps, 1)

            pe.wait_ge(route_done, NPAIR + FREE)
            for n in range(RING):
                expert_slot(0, n, 1)
            with pe.Fori(1, E // RING) as r:
                for n in range(RING):
                    expert_slot(RING * r, n, r + 1, lo=-RING)
            for n in range(RING - 1):
                expert_slot(E, n, E // RING + 1, lo=-RING, hi=0)

            pe.wait_ge(sw_lo_done, 1)
            pe.wait_ge(ld_swd, 32)
            pe.wait_ge(ye_done, E)
            with pe.Fori(0, NPAIR // 2) as r:
                for j in range(2):
                    pe.wait_ge(ld_xs[j], 32 * (r + 1))
                    for f in range(FT):
                        fw = min(PN, FS - f * PN)
                        k = FT * j + f
                        pe.wait_ge(hs_done, (2 * FT * r + (k - 1) if k >= 2 else 2 * FT * r) + FREE)
                        for off, bk in ((0, PJ[f % 2]), (FS, SC[f % 2])):
                            cols = slice(off + f * PN, off + f * PN + fw)
                            last = halves(bk[0:fw, :], HC,
                                          ((lambda c: sw_hi[:, c, cols], lambda c: sw_lo[:, c, cols]),
                                           (lambda c: xs_hi[:, j, c, :], lambda c: xs_lo[:, j, c, :])))
                        last.then_inc(sh_ps, 1)
                    pe.wait_ge(hs_done, 2 * FT * r + FT * (j + 1) + FREE)
                    for t in range(TT):
                        n = TT * j + t
                        if n >= 2:
                            pe.wait_ge(acc_done, 2 * TT * r + (n - 1) + FREE)
                        bk = (OB, XB)[t % 2]
                        for f in range(FT):
                            fw = min(PN, FS - f * PN)
                            last = pe.matmul(bk[:, 0:H], hs[0:fw, j, f, t * PN:(t + 1) * PN], swd[0:fw, f, :],
                                             start=(f == 0), stop=(f == FT - 1))
                        last.then_inc(dn_ps, 1)


_INS = ['L0_attn_hidden', 'L0_attn_W_pack', 'L0_attn_W_o', 'L0_attn_conv_k', 'L0_attn_conv_v', 'L0_ffn_w_norm',
        'L0_ffn_w_router', 'L0_ffn_w_gate', 'L0_ffn_w_up', 'L0_ffn_w_down', 'L0_ffn_sw_gate', 'L0_ffn_sw_up',
        'L0_ffn_sw_down', 'L0_ffn_w_shared_gate', 'L0_c', 'L0_wmod']
_OUTS = [((B, S, H), 'float32')]


def _constants():
    import numpy as _np
    f = _np.float32
    inv_freq = f(1.0) / f(100000.0) ** (_np.arange(0, HD, 2, dtype=f) / f(HD))
    freqs = _np.outer(_np.arange(S, dtype=f), inv_freq).astype(f).T
    cos, sin = _np.cos(freqs).astype(f), _np.sin(freqs).astype(f)
    i, j = _np.arange(PN)[:, None], _np.arange(PN)[None, :]
    causal, window = j <= i, j > i
    allowed = _np.concatenate([causal, window, causal], axis=1)
    return [_np.concatenate([cos, cos], axis=0), _np.concatenate([-sin, sin], axis=0),
            _np.where(allowed, f(0.0), f(-3.0e38)).astype(f), _np.eye(PN, dtype=f), (i < j).astype(f),
            _np.tile((_np.arange(E) * CAP + 1).astype(f), (PN, 1))]


def kernel(**inputs):
    import numpy as _np
    import concourse.bacc as _bacc
    from concourse import mybir as _mybir
    from concourse.bass_utils import run_bass_kernel_spmd as _run

    nc = _bacc.Bacc("TRN2", target_bir_lowering=False, num_devices=1)
    arrays, args = {}, []
    host = [_np.ascontiguousarray(inputs[name]) for name in _INS] + _constants()
    for n, a in enumerate(host):
        if n == 0:
            a = a.reshape(B * S, H)
        name = f"in_{n}_dram"
        arrays[name] = a
        args.append(nc.dram_tensor(name, a.shape, _mybir.dt.from_np(a.dtype), kind="ExternalInput").ap())
    out = nc.dram_tensor("out_0_dram", (B * S, H), _mybir.dt.float32, kind="ExternalOutput").ap()
    adaln_block(nc, *args, out)
    r = _run(nc, [arrays], core_ids=[0])
    return r.results[0]["out_0_dram"].reshape(B, S, H)
```

```python
from contextlib import ExitStack

import concourse.bass as bass
from concourse import mybir

F32 = mybir.dt.float32
F32R = mybir.dt.float32r
I32 = mybir.dt.int32
ALU = mybir.AluOpType
ACT = mybir.ActivationFunctionType
AXX = mybir.AxisListType.X

PN = 128
B, S, H = 8, 256, 256
HC = H // PN
NH, NKV, HD = 16, 8, 128
E, TOPK, F, CAP = 32, 4, 176, 128
FH = F // 2
FS = 704
FT = -(-FS // PN)
NPAIR = B // 2
TOK = 2 * S
TT = TOK // PN
GROUPS = NKV
UNITS = 4 * GROUPS
ROPES = 3 * GROUPS
QKV = (NH + 2 * NKV) * HD
LN_EPS, RMS_EPS = 1e-5, 1e-6
ROPE_OF = {0: 0, 1: 1, 3: 2}
T_LAG, PV_LAG = 2, 3
PROB_FLOOR = -87.34
SENTINEL, TAKEN = 1.0, -1000.0
SKIP = 2 * E * CAP
RING = 8
HALF = RING // 2
FREE = 1
LCOL = 64


def adaln_block(nc, x, w_pack, w_o, conv_k, conv_v, w_norm, w_router, w_gate, w_up, w_down, sw_gate, sw_up,
                sw_down, w_sgate, c_in, wmod, cos_t, sin_t, mask_t, ident_t, tri_t, ebase_t, out):
    ctx = ExitStack()
    with ctx:
        def sb(name, shape, dt=F32, where=ctx):
            return where.enter_context(nc.sbuf_tensor(name, shape, dt))

        def sem(name):
            return ctx.enter_context(nc.semaphore(name))

        mod_d = nc.dram_tensor("mod_rows", [B, 6 * H], F32, kind="Internal").ap()
        slots_d = nc.dram_tensor("slot_rows", [E * CAP, H], F32, kind="Internal").ap()
        y_d = nc.dram_tensor("expert_rows", [E * CAP, H], F32, kind="Internal").ap()
        base_d = nc.dram_tensor("residual_rows", [B * S, H], F32, kind="Internal").ap()
        xnt_d = nc.dram_tensor("xn_transposed", [NPAIR, PN, 2, HC, TOK], F32, kind="Internal").ap()

        cosT = sb("cosT", [PN, S])
        sinT = sb("sinT", [PN, S])
        mask = sb("mask", [PN, 3 * PN])
        ident = sb("ident", [PN, PN])
        tri = sb("tri", [PN, PN])
        ones = sb("ones", [PN, PN])
        ebase = sb("ebase", [PN, E])
        wnorm = sb("wnorm", [PN, H])
        cwk = sb("cwk", [PN, 2 * NKV])
        cwv = sb("cwv", [PN, 2 * NKV])
        modT = sb("modT", [PN, 4, B + 2])
        scT = sb("scT", [PN, HC, B])
        wr = sb("wr", [PN, HC, E + 2])
        wr_hi = sb("wr_hi", [PN, HC, E + 2], F32R)
        wr_lo = sb("wr_lo", [PN, HC, E + 2], F32R)
        gidx = sb("gidx", [PN, NPAIR, TT * TOPK], I32)
        wsel = sb("wsel", [PN, NPAIR, TT * TOPK])
        sgate = sb("sgate", [PN, NPAIR, TT])
        carry = sb("carry", [PN, 2, E])

        att = ExitStack()
        hT_hi = sb("hT_hi", [PN, HC, TOK], F32R, att)
        hT_lo = sb("hT_lo", [PN, HC, TOK], F32R, att)
        bcm = sb("bcm", [PN, 2, 4 * H], F32, att)
        xin = sb("xin", [PN, TT, H], F32, att)
        xres = sb("xres", [PN, TT, H], F32, att)
        qsw = sb("qsw", [PN, 2, TOK], F32, att)
        qr = sb("qr", [PN, 2, 2, TOK], F32, att)
        kr = sb("kr", [PN, TOK], F32, att)
        k0 = sb("k0", [PN, 2, S + 1], F32, att)
        v0 = sb("v0", [PN, 2, S + 1], F32, att)
        kc = sb("kc", [PN, 2, TOK], F32, att)
        vT = sb("vT", [PN, TOK], F32, att)
        vN = sb("vN", [PN, 2, TOK], F32, att)
        rows8 = ExitStack()
        c_sb = sb("c_sb", [B, H], F32, rows8)
        sc = sb("sc", [B, H], F32, rows8)
        gabs = sb("gabs", [B, H], F32, rows8)
        gsgn = sb("gsgn", [B, H], F32, rows8)
        rows8.close()
        sneg = sb("sneg", [PN, 2, 3 * PN], F32, att)
        nmax = sb("nmax", [PN, 4, 2], F32, att)
        prob = sb("prob", [PN, 3, 3 * PN], F32, att)
        rsum = sb("rsum", [PN, 4, 2], F32, att)
        rinv = sb("rinv", [PN, 4, 2], F32, att)
        pT = sb("pT", [PN, 2, 3 * PN], F32, att)
        wo = sb("wo", [PN, NH, H], F32, att)
        st1 = sb("st1", [PN, TT, 6], F32, att)
        mv1 = sb("mv1", [PN, TT, 2], F32, att)
        std1 = sb("std1", [PN, 2, TT], F32, att)
        mods = ExitStack()
        wm = sb("wm", [PN, HC, 6 * H], F32, mods)
        mod = sb("mod", [B, 6 * H], F32, mods)
        mods.close()
        xnT_hi = sb("xnT_hi", [PN, HC, S], F32R, att)
        xnT_lo = sb("xnT_lo", [PN, HC, S], F32R, att)
        yg = sb("yg", [PN, 2, 2, H], F32, att)
        h2 = sb("h2", [PN, TT, H], F32, att)
        xn = sb("xn", [PN, TT, H], F32, att)
        st2 = sb("st2", [PN, TT, 6], F32, att)
        mv2 = sb("mv2", [PN, TT, 2], F32, att)
        std2 = sb("std2", [PN, 2, TT], F32, att)
        rms = sb("rms", [PN, 3, TT], F32, att)
        zz = sb("zz", [PN, TT, E + TOPK], F32, att)
        zz2 = sb("zz2", [PN, TT, E + TOPK], F32, att)
        top8 = sb("top8", [PN, TT, 8], F32, att)
        key8 = sb("key8", [PN, TT, 8], F32, att)
        red = sb("red", [PN, 4, TT], F32, att)
        ex = sb("ex", [PN, TT, E], F32, att)
        chosen = sb("chosen", [PN, TT, E], F32, att)
        kept = sb("kept", [PN, TT, E], F32, att)
        key = sb("key", [PN, TT, E], F32, att)
        late = sb("late", [PN, TT, TOPK], F32, att)
        sidx = sb("sidx", [PN, TT * TOPK], I32, att)
        eq = sb("eq", [PN, TT, TOPK, E], F32, att)
        raws = ExitStack()
        wraw = sb("wraw", [PN, HC, QKV], F32, raws)
        raws.close()
        outs = ExitStack()
        oT = sb("oT", [PN, NH, TOK], F32, outs)
        proj_w = ExitStack()
        w_hi = sb("w_hi", [PN, HC, QKV], F32R, proj_w)
        w_lo = sb("w_lo", [PN, HC, QKV], F32R, proj_w)
        proj_w.close()

        exps = ExitStack()
        wgu = sb("wgu", [PN, RING, HC, 2 * F], F32, exps)
        wd = sb("wd", [FH, RING, 2, H], F32, exps)
        sw_hi = sb("sw_hi", [PN, HC, 2 * FS], F32R, exps)
        sw_lo = sb("sw_lo", [PN, HC, 2 * FS], F32R, exps)
        exps.close()
        outs.close()
        shar = ExitStack()
        swraw = sb("swraw", [PN, HC, 2 * FS], F32, shar)
        swd = sb("swd", [PN, FT, H], F32, shar)
        xs_hi = sb("xs_hi", [PN, HC, TOK], F32R, shar)
        xs_lo = sb("xs_lo", [PN, HC, TOK], F32R, shar)
        shar.close()
        att.close()
        hs = sb("hs", [PN, FT, TOK])
        sg2 = sb("sg2", [PN, 2, TOK])
        gat = sb("gat", [PN, TT, TOPK, H])
        gball = sb("gball", [PN, B, H])
        bas = sb("bas", [PN, 2, H])
        acc = sb("acc", [PN, 2, H])
        fin = sb("fin", [PN, 2, H])
        shrow = sb("shrow", [PN, NPAIR * TT, H])
        xe = sb("xe", [PN, RING, H])
        xeT = sb("xeT", [PN, 2, H])
        sgl = sb("sgl", [PN, 2, F])
        hh = sb("hh", [PN, 2, F])
        hhT = sb("hhT", [FH, 2, 2 * PN])
        ye = sb("ye", [PN, 4, H])

        def bank(name):
            return ctx.enter_context(nc.psum_tensor(name, [PN, 512], F32))

        PJ = [bank("PJ0"), bank("PJ1")]
        SC = [bank("SC0"), bank("SC1")]
        PT = [bank("PT0"), bank("PT1")]
        OB = bank("OB")
        XB = bank("XB")

        ld_c, ld_wm, ld_xin, ld_xres, ld_bcm = sem("ld_c"), sem("ld_wm"), sem("ld_xin"), sem("ld_xres"), sem("ld_bcm")
        ld_const, ld_wo = sem("ld_const"), sem("ld_wo")
        ld_w = [sem(f"ld_w{j}") for j in range(8)]
        st_mod, st_zero, st_base, st_xnt, st_scat = sem("st_mod"), sem("st_zero"), sem("st_base"), sem("st_xnt"), sem("st_scat")
        silu_done, sct_ps, sct_done, mod_ps, mod_done, modt_ps, modt_done = (
            sem(n) for n in ("silu_done", "sct_ps", "sct_done", "mod_ps", "mod_done", "modt_ps", "modt_done"))
        w_hi_done, w_lo_done, wr_hi_done, wr_lo_done, fills = (
            sem(n) for n in ("w_hi_done", "w_lo_done", "wr_hi_done", "wr_lo_done", "fills"))
        waits_met = sem("waits_met")
        dve_own, act_own, pool_own = sem("dve_own"), sem("act_own"), sem("pool_own")
        var1, std1_done, xhat_done, ht_ps, h_hi_done, h_lo_done = (
            sem(n) for n in ("var1", "std1_done", "xhat_done", "ht_ps", "h_hi_done", "h_lo_done"))
        pj_ps, pj_act, pj_dve, t2_done, rope_done, k0_done, kc_done, vt_ps, vn_done = (
            sem(n) for n in ("pj_ps", "pj_act", "pj_dve", "t2_done", "rope_done", "k0_done", "kc_done", "vt_ps", "vn_done"))
        sc_ps, sneg_done, exp_done, rinv_done, norm_done, pt_ps, pt_done, pv_ps, ot_done = (
            sem(n) for n in ("sc_ps", "sneg_done", "exp_done", "rinv_done", "norm_done", "pt_ps", "pt_done", "pv_ps", "ot_done"))
        y_ps, yg_done, x1_done, var2, std2_done, xh2_done, h2_done, rms_done, xn_done, base_done = (
            sem(n) for n in ("y_ps", "yg_done", "x1_done", "var2", "std2_done", "xh2_done", "h2_done", "rms_done", "xn_done", "base_done"))
        xnt_ps, xnt_hi_done, xnt_lo_done, lg_ps, z_done, ex_done, chosen_done, pos_ps, sidx_done, route_done = (
            sem(n) for n in ("xnt_ps", "xnt_hi_done", "xnt_lo_done", "lg_ps", "z_done", "ex_done", "chosen_done", "pos_ps", "sidx_done", "route_done"))
        ld_e = [sem(f"ld_e{i}") for i in range(HALF)]
        ld_xe = [sem(f"ld_xe{i}") for i in range(HALF)]
        st_y = [sem("st_y0"), sem("st_y1")]
        xe_ps, xe_done, gu_ps, sgl_done, hh_done, hh_ps, hht_done, ye_ps, ye_done = (
            sem(n) for n in ("xe_ps", "xe_done", "gu_ps", "sgl_done", "hh_done", "hh_ps", "hht_done", "ye_ps", "ye_done"))
        ld_sw, ld_swd, ld_gb = sem("ld_sw"), sem("ld_swd"), sem("ld_gb")
        ld_xs = sem("ld_xs")
        ld_bas = [sem("ld_bas0"), sem("ld_bas1")]
        ld_gat = [sem(f"ld_gat{t}") for t in range(TT)]
        st_out = [sem("st_out0"), sem("st_out1")]
        st_all = sem("st_all")
        sw_hi_done, sw_lo_done, sh_ps, sg2_done, hs_done, dn_ps, shrow_done, acc_done, fin_done, acc_own = (
            sem(n) for n in ("sw_hi_done", "sw_lo_done", "sh_ps", "sg2_done", "hs_done", "dn_ps", "shrow_done", "acc_done", "fin_done", "acc_own"))

        def met(eng):
            eng.sem_inc(waits_met, 1)

        class Chain:

            def __init__(self, eng, own, base=0):
                self.eng, self.own, self.base, self.n = eng, own, base, 0

            def __call__(self, ins, plain=False):
                ins.then_inc(self.own, 1)
                self.n += 1
                self.eng.wait_ge(self.own, self.base + self.n)
                if plain:
                    met(self.eng)

        DVE_PRE, DVE_ROUND = 16, 29
        ACT_PRE, ACT_ROUND = 1, 3
        POOL_ROUND = 4
        W_ORDER = (4, 0, 6, 1, 5, 2, 7, 3)
        WC = QKV // 8

        def x_pair(p):
            return x[bass.ds(p * TOK, TOK), :].rearrange("(t p) h -> p t h", p=PN)

        def rows(ap, row):
            return ap[bass.ds(row, PN), :]

        def both(ap):
            return ap.unsqueeze(1).broadcast_to([PN, 2, S])

        def pair3(ap):
            return ap.rearrange("p (b s) -> p b s", b=2)

        def rope_buffer(m):
            g, r = m // 4, m % 4
            return kr[:, :] if r == 0 else qr[:, 0 if r == 1 else 1, g % 2, :]

        def later(n):
            return not isinstance(n, int) or n > 0

        block = ctx.enter_context(nc.Block())

        @block.sync
        def _(sp):
            sp.dma_start(c_sb[:, :], c_in).then_inc(ld_c, 16)
            sp.dma_start(ident[:, :], ident_t).then_inc(ld_c, 16)
            sp.dma_start(wm[:, :, :], wmod.rearrange("(c p) n -> p c n", p=PN)).then_inc(ld_wm, 16)
            sp.dma_start(xin[:, :, :], x_pair(0)).then_inc(ld_xin, 16)
            for j in W_ORDER:
                sp.dma_start(wraw[:, :, j * WC:(j + 1) * WC],
                             w_pack.rearrange("(c p) n -> p c n", p=PN)[:, :, j * WC:(j + 1) * WC]).then_inc(ld_w[j], 16)
            sp.wait_ge(mod_done, 1)
            sp.dma_start(mod_d, mod[:, :]).then_inc(st_mod, 16)
            sp.wait_ge(fills, 1)
            sp.dma_start(slots_d.rearrange("(a p) h -> p a h", p=PN),
                         vN[:, 0, 0:H].unsqueeze(1).broadcast_to([PN, E, H])).then_inc(st_zero, 16)
            sp.wait_ge(st_mod, 16)

            def pair_loads(p):
                sp.wait_ge(base_done, 2 * p + FREE)
                for b in range(2):
                    sp.dma_start(bcm[:, b, :], mod_d[bass.ds(2 * p + b, 1), 2 * H:6 * H].rearrange("a n -> (a n)")
                                 .partition_broadcast(PN)).then_inc(ld_bcm, 16)
                sp.dma_start(xres[:, :, :], x_pair(p)).then_inc(ld_xres, 16)

            def pair_stores(p):
                for b in range(2):
                    sp.wait_ge(base_done, 2 * p + b + 1 + FREE)
                    sp.dma_start(base_d[bass.ds(p * TOK + b * S, S), :].rearrange("(t p) h -> p t h", p=PN),
                                 h2[:, 2 * b:2 * b + 2, :]).then_inc(st_base, 16)
                    sp.wait_ge(xnt_hi_done, 2 * p + b + 1)
                    sp.dma_start(xnt_d[bass.ds(p, 1), :, 0, :, b * S:(b + 1) * S].rearrange("a p c s -> (a p) c s"),
                                 xnT_hi[:, :, :].bitcast(F32)).then_inc(st_xnt, 16)
                    sp.wait_ge(xnt_lo_done, 2 * p + b + 1 + FREE)
                    sp.dma_start(xnt_d[bass.ds(p, 1), :, 1, :, b * S:(b + 1) * S].rearrange("a p c s -> (a p) c s"),
                                 xnT_lo[:, :, :].bitcast(F32)).then_inc(st_xnt, 16)

            with sp.Fori(0, NPAIR - 1) as p:
                pair_loads(p)
                sp.wait_ge(ht_ps, p + 1)
                sp.dma_start(xin[:, :, :], x_pair(p + 1)).then_inc(ld_xin, 16)
                pair_stores(p)
            pair_loads(NPAIR - 1)
            sp.wait_ge(ht_ps, NPAIR)
            sp.dma_start(xin[:, :, :], x_pair(NPAIR - 1)).then_inc(ld_xin, 16)

            def expert_weights(e, i):
                two = slice(2 * i, 2 * i + 2)
                for dst, src in ((wgu[:, two, :, 0:F], w_gate), (wgu[:, two, :, F:2 * F], w_up)):
                    sp.dma_start(dst.rearrange("p e c f -> p (e c) f"),
                                 src[bass.ds(e, 2), :, :].rearrange("a (c p) f -> p (a c) f", p=PN)).then_inc(ld_e[i], 16)
                sp.dma_start(wd[:, two, :, :].rearrange("p e c h -> p (e c) h"),
                             w_down[bass.ds(e, 2), :, :].rearrange("a (c p) h -> p (a c) h", p=FH)).then_inc(ld_e[i], 16)

            sp.wait_ge(pj_ps, UNITS * NPAIR + 4)
            for i in range(HALF):
                expert_weights(2 * i, i)
            sp.wait_ge(y_ps, TT * NPAIR + FREE)
            for n, src in enumerate((sw_gate, sw_up)):
                sp.dma_start(swraw[:, :, n * FS:(n + 1) * FS], src.rearrange("(c p) f -> p c f", p=PN)).then_inc(ld_sw, 16)
            sp.dma_start(swd[:, 0:FT - 1, :], sw_down[0:(FT - 1) * PN, :].rearrange("(t p) h -> p t h", p=PN)).then_inc(ld_swd, 16)
            sp.dma_start(swd[0:FS - (FT - 1) * PN, FT - 1, :], sw_down[(FT - 1) * PN:FS, :]).then_inc(ld_swd, 16)
            pair_stores(NPAIR - 1)

            def slot_rows(e, i):
                sp.dma_start(xe[:, 2 * i:2 * i + 2, :], slots_d[bass.ds(e * CAP, 2 * CAP), :].rearrange("(a p) h -> p a h", p=PN))\
                  .then_inc(ld_xe[i], 16)

            sp.wait_ge(st_xnt, 64 * NPAIR + FREE)
            sp.wait_ge(st_base, 32 * NPAIR + FREE)
            sp.sem_inc(st_all, 1)
            sp.wait_ge(st_scat, 16 * (NPAIR + 1) * TT * TOPK)
            for i in range(HALF):
                slot_rows(2 * i, i)
            sp.dma_start(gball[:, :, :], mod_d[:, 5 * H:6 * H].partition_broadcast(PN)).then_inc(ld_gb, 16)

            def residual(tile, par):
                sp.dma_start(bas[:, par, :], rows(base_d, tile * PN)).then_inc(ld_bas[par], 16)

            for j in range(2):
                residual(j, j)
            with sp.Fori(1, E // RING) as r:
                for i in range(HALF):
                    sp.wait_ge(ye_ps, RING * r + (2 * i + 2 - RING))
                    slot_rows(RING * r + 2 * i, i)
                    expert_weights(RING * r + 2 * i, i)

            for tile in range(NPAIR * TT):
                sp.wait_ge(fin_done, tile + 1)
                sp.dma_start(rows(out, tile * PN), fin[:, tile % 2, :]).then_inc(st_out[tile % 2], 16)
                if tile + 2 < NPAIR * TT:
                    residual(tile + 2, tile % 2)
            for par in range(2):
                sp.wait_ge(st_out[par], 16 * NPAIR * TT // 2 + FREE)

        @block.scalar
        def _(act):
            for dst, src in ((cosT[:, :], cos_t), (sinT[:, :], sin_t), (mask[:, :], mask_t), (tri[:, :], tri_t),
                             (ebase[:, :], ebase_t), (wnorm[:, :], w_norm.partition_broadcast(PN)),
                             (cwk[:, :], conv_k.rearrange("g t -> (g t)").partition_broadcast(PN)),
                             (cwv[:, :], conv_v.rearrange("g t -> (g t)").partition_broadcast(PN))):
                act.dma_start(dst, src).then_inc(ld_const, 16)
            act.wait_ge(fills, 2)
            act.dma_start(wr[:, :, 0:E], w_router.rearrange("(c p) e -> p c e", p=PN)).then_inc(ld_const, 16)
            act.dma_start(wr[:, :, E:E + 1], w_sgate.rearrange("(c p) e -> p c e", p=PN), allow_slow_non_contiguous=True).then_inc(ld_const, 16)
            act.dma_start(wo[:, :, :], w_o.rearrange("(n p) h -> p n h", p=PN)).then_inc(ld_wo, 16)
            act.wait_ge(ld_c, 32)
            act.activation(sc[:, :], c_sb[:, :], ACT.Silu).then_inc(silu_done, 1)

            def prepare_norm(p):
                act.wait_ge(var1, p + 1)
                act.activation(std1[:, 0, :], mv1[:, :, 1], ACT.Sqrt, bias=LN_EPS).then_inc(std1_done, 1)

            def prepare_h(p, own):
                act.wait_ge(ht_ps, p + 1)
                act.wait_ge(modt_done, 1)
                if later(p):
                    act.wait_ge(rope_done, ROPES * p)
                for c in range(HC):
                    for b in range(2):
                        last = act.activation(qsw[:, c, b * S:(b + 1) * S], PT[c][:, b * S:(b + 1) * S], ACT.Identity,
                                              scale=modT[:, 2 + c, bass.ds(2 * p + b, 1)],
                                              bias=modT[:, c, bass.ds(2 * p + b, 1)])
                own(last)
                if later(p):
                    act.wait_ge(pj_ps, UNITS * p)
                act.activation(hT_hi[:, :, :], qsw[:, :, :], ACT.Copy).then_inc(h_hi_done, 1)

            def project(p, m):
                g, r = m // 4, m % 4
                bank = PJ[m % 2]
                act.wait_ge(pj_ps, UNITS * p + (m + 1))
                if r == 2:
                    if m >= 4 or later(p):
                        act.wait_ge(pj_dve, UNITS * p + (m - 3))
                    act.activation(v0[:, :, 1:S + 1], pair3(bank[:, :]), ACT.Copy,
                                   scale=cwv[:, 2 * g:2 * g + 1]).then_inc(pj_act, 1)
                    return
                rope = 3 * g + ROPE_OF[r]
                if rope >= 2 or later(p):
                    act.wait_ge(rope_done, ROPES * p + (rope - 1))
                half = HD // 2
                act.activation(qsw[0:half, rope % 2, :], bank[half:HD, :], ACT.Copy)
                act.activation(qsw[half:HD, rope % 2, :], bank[0:half, :], ACT.Copy).then_inc(pj_act, 1)

            def k_tap(p, g):
                if g >= 1 or later(p):
                    act.wait_ge(kc_done, GROUPS * p + g)
                act.wait_ge(rope_done, ROPES * p + (3 * g + 1))
                act.activation(k0[:, :, 1:S + 1], pair3(kr[:, :]), ACT.Copy,
                               scale=cwk[:, 2 * g:2 * g + 1]).then_inc(k0_done, 1)

            def exps_of(p, n):
                act.wait_ge(sneg_done, UNITS * p + (n + 1))
                if n >= 3:
                    act.wait_ge(pt_ps, UNITS * p + (n - 2))
                for j, (a, z) in enumerate(((0, PN), (PN, 3 * PN))):
                    last = act.activation(prob[:, n % 3, a:z], sneg[:, n % 2, a:z], ACT.Exp, scale=-1.0,
                                          bias=nmax[:, n % 4, j:j + 1], accum_out=rsum[:, n % 4, j:j + 1])
                last.then_inc(exp_done, 1)

            def v_rows(p, g):
                act.wait_ge(vt_ps, GROUPS * p + (g + 1))
                act.activation(vN[:, g % 2, :], XB[:, :], ACT.Copy).then_inc(vn_done, 1)

            def head_out(p, n):
                g, h, b = n // 4, (n % 4) // 2, n % 2
                act.wait_ge(pv_ps, UNITS * p + (n + 1))
                if n == 0:
                    act.wait_ge(y_ps, TT * p + FREE)
                act.activation(oT[:, 2 * g + h, b * S:(b + 1) * S], OB[:, (n % 2) * S:(n % 2 + 1) * S],
                               ACT.Copy).then_inc(ot_done, 1)

            def slot(p, n):
                m = n + 4
                if m < UNITS:
                    if m % 4 == 2:
                        k_tap(p, m // 4)
                    project(p, m)
                if n < UNITS:
                    exps_of(p, n)
                    if n % 4 == 0:
                        v_rows(p, n // 4)
                if n >= PV_LAG:
                    head_out(p, n - PV_LAG)

            def first_group(p):
                project(p, 0)
                project(p, 1)
                k_tap(p, 0)
                project(p, 2)
                project(p, 3)

            prepare_norm(0)
            for n, j in enumerate(W_ORDER):
                act.wait_ge(ld_w[j], 16)
                act.activation(w_hi[:, :, j * WC:(j + 1) * WC], wraw[:, :, j * WC:(j + 1) * WC], ACT.Copy).then_inc(w_hi_done, 1)
                if n == 0:
                    own = Chain(act, act_own)
                    prepare_h(0, own)
                    assert own.n == ACT_PRE
            act.wait_ge(ld_const, 160)
            act.activation(wr_hi[:, :, :], wr[:, :, :], ACT.Copy).then_inc(wr_hi_done, 1)
            act.wait_ge(fills, 4)
            first_group(0)
            act.wait_ge(st_zero, 16)
            act.wait_ge(w_lo_done, 8)

            with act.Fori(0, NPAIR) as p:
                own = Chain(act, act_own, ACT_PRE + ACT_ROUND * p)
                for n in range(UNITS):
                    slot(p, n)
                    if n == UNITS - 2:
                        prepare_norm(p + 1)
                for n in range(UNITS, UNITS + PV_LAG):
                    slot(p, n)
                prepare_h(p + 1, own)
                for b in range(2):
                    act.wait_ge(var2, 2 * p + (b + 1))
                    act.activation(std2[:, 0, 2 * b:2 * b + 2], mv2[:, 2 * b:2 * b + 2, 1], ACT.Sqrt,
                                   bias=LN_EPS).then_inc(std2_done, 1)
                for b in range(2):
                    act.wait_ge(h2_done, 2 * p + (b + 1))
                    for t in range(2 * b, 2 * b + 2):
                        last = act.activation(xn[:, t, :], h2[:, t, :], ACT.Square, accum_out=rms[:, 0, t:t + 1])
                    own(last)
                    act.activation(rms[:, 1, 2 * b:2 * b + 2], rms[:, 0, 2 * b:2 * b + 2], ACT.Sqrt, scale=1.0 / H,
                                   bias=RMS_EPS).then_inc(rms_done, 1)
                first_group(p + 1)
                for b in range(2):
                    act.wait_ge(xnt_ps, 2 * p + (b + 1))
                    act.wait_ge(st_xnt, 64 * p + 32 * b + FREE)
                    act.wait_ge(lg_ps, 2 * p + b + FREE)
                    for c in range(HC):
                        last = act.activation(xnT_hi[:, c, :], PT[c][:, b * S:(b + 1) * S], ACT.Copy)
                    last.then_inc(xnt_hi_done, 1)
                act.wait_ge(z_done, p + 1)
                act.activation(red[:, 2, :], XB[:, 0:TT * LCOL].rearrange("p (t c) -> p t c", c=LCOL)[:, :, E], ACT.Exp, scale=-1.0)
                act.activation(ex[:, :, :], zz[:, :, 0:E], ACT.Exp).then_inc(ex_done, 1)
                assert own.n == ACT_ROUND, own.n

            act.wait_ge(ld_sw, 32)
            act.activation(sw_hi[:, :, :], swraw[:, :, :], ACT.Copy).then_inc(sw_hi_done, 1)

            def expert_slot(base, n, lo=0, hi=10 ** 9):
                if lo <= n - 1 < hi:
                    act.wait_ge(gu_ps, base + n)
                    if n - 1 >= 2 or later(base):
                        act.wait_ge(hh_done, base + (n - 2))
                    act.activation(sgl[:, (n - 1) % 2, :], SC[(n - 1) % 2][:, 0:F], ACT.Silu).then_inc(sgl_done, 1)
                if lo <= n - 2 < hi:
                    act.wait_ge(hh_ps, base + (n - 1))
                    if n - 2 >= 2 or later(base):
                        act.wait_ge(ye_ps, base + (n - 3))
                    act.activation(hhT[:, (n - 2) % 2, :], PT[(n - 2) % 2][0:FH, 0:2 * PN], ACT.Copy).then_inc(hht_done, 1)
                if lo <= n - 3 < hi and n % 2 == 0:
                    pair = (n - 4) // 2
                    act.wait_ge(ye_done, base + (n - 2))
                    act.dma_start(y_d[bass.ds((base + (n - 4)) * CAP, 2 * CAP), :].rearrange("(a p) h -> p a h", p=PN),
                                  ye[:, 2 * (pair % 2):2 * (pair % 2) + 2, :]).then_inc(st_y[pair % 2], 16)

            def shared_inputs(q):
                for dst, part in ((xs_hi, 0), (xs_lo, 1)):
                    act.dma_start(dst[:, :, :].bitcast(F32), xnt_d[bass.ds(q, 1), :, part, :, :].rearrange("a p c s -> (a p) c s"))\
                       .then_inc(ld_xs, 16)

            def shared(q, more=True):
                for f in range(FT):
                    fw = min(PN, FS - f * PN)
                    act.wait_ge(sh_ps, FT * q + (f + 1))
                    if f >= 2 or later(q):
                        act.wait_ge(hs_done, FT * q + (f - 1))
                    act.activation(sg2[0:fw, f % 2, :], PJ[f % 2][0:fw, :], ACT.Silu).then_inc(sg2_done, 1)
                if more:
                    shared_inputs(q + 1)
                for t in range(TT):
                    act.wait_ge(dn_ps, TT * q + (t + 1))
                    act.activation(shrow[:, bass.ds(TT * q + t, 1), :].rearrange("p a h -> p (a h)"), (OB, XB)[t % 2][:, 0:H],
                                   ACT.Copy, scale=sgate[:, bass.ds(q, 1), t:t + 1].rearrange("p a t -> p (a t)"))\
                       .then_inc(shrow_done, 1)

            act.wait_ge(st_all, 1)
            shared_inputs(0)
            shared(0)
            for n in range(RING):
                expert_slot(0, n)
            with act.Fori(1, E // RING) as r:
                for n in range(RING):
                    expert_slot(RING * r, n, lo=-RING)
            for n in range(4):
                expert_slot(E, n, lo=-RING, hi=0)
            with act.Fori(1, NPAIR - 1) as q:
                shared(q)
            shared(NPAIR - 1, more=False)

        @block.gpsimd
        def _(pool):
            for start in (y_ps, yg_done, route_done, xnt_lo_done, lg_ps, base_done,
                          st_xnt, st_base, st_out[0], st_out[1]):
                pool.sem_inc(start, FREE)
            pool.memset(vN[:, :, :], 0.0).then_inc(fills, 1)
            pool.memset(wr[:, :, :], 0.0).then_inc(fills, 1)
            pool.memset(k0[:, :, 0:1], 0.0).then_inc(fills, 1)
            pool.memset(v0[:, :, 0:1], 0.0).then_inc(fills, 1)
            pool.memset(ones[:, :], 1.0).then_inc(fills, 1)
            pool.memset(carry[:, :, :], 0.0).then_inc(fills, 1)
            pool.memset(modT[:, :, B:B + 2], 0.0).then_inc(fills, 1)

            def rope(p, m):
                g, r = m // 4, m % 4
                if r == 2:
                    return
                n = 3 * g + ROPE_OF[r]
                pool.wait_ge(pj_act, UNITS * p + (m + 1))
                pool.tensor_tensor(pair3(qsw[:, n % 2, :]), pair3(qsw[:, n % 2, :]), both(sinT[:, :]),
                                   ALU.mult).then_inc(t2_done, 1)
                pool.wait_ge(t2_done, ROPES * p + (n + 1))
                pool.wait_ge(pj_dve, UNITS * p + (m + 1))
                pool.tensor_tensor(rope_buffer(m), rope_buffer(m), qsw[:, n % 2, :], ALU.add).then_inc(rope_done, 1)

            def scatter(c):
                pool.indirect_dma_start(out=slots_d, out_offset=bass.IndirectOffsetOnAxis(ap=sidx[:, c:c + 1], axis=0),
                                        in_=xn[:, c // TOPK, :], in_offset=None, bounds_check=E * CAP - 1,
                                        oob_is_err=False).then_inc(st_scat, 16)

            pool.wait_ge(ld_const, 160)
            for m in range(4):
                rope(0, m)
            pool.wait_ge(modt_done, 1)
            pool.wait_ge(st_mod, 16)
            pool.memset(sidx[:, :], SKIP).then_inc(fills, 1)
            pool.memset(xn[:, :, :], 0.0).then_inc(fills, 1)
            pool.wait_ge(fills, 9)
            pool.wait_ge(st_zero, 16)
            with pool.Fori(0, NPAIR) as p:
                own = Chain(pool, pool_own, POOL_ROUND * p)
                for n in range(UNITS - 4):
                    rope(p, n + 4)
                    if n < TT * TOPK:
                        if n == 0:
                            pool.wait_ge(route_done, p + FREE)
                            met(pool)
                        scatter(n)
                pool.wait_ge(ld_xres, 16 * (p + 1))
                for b in range(2):
                    t = slice(2 * b, 2 * b + 2)
                    pool.wait_ge(yg_done, 2 * p + (b + 1) + FREE)
                    pool.tensor_tensor(xres[:, t, :], xres[:, t, :], yg[:, b, :, :], ALU.add).then_inc(x1_done, 1)
                for b in range(2):
                    t = slice(2 * b, 2 * b + 2)
                    pool.wait_ge(xh2_done, 2 * p + (b + 1))
                    own(pool.tensor_tensor(h2[:, t, :], h2[:, t, :],
                                           bcm[:, b, 2 * H:3 * H].unsqueeze(1).broadcast_to([PN, 2, H]), ALU.mult))
                    pool.tensor_tensor(h2[:, t, :], h2[:, t, :],
                                       bcm[:, b, H:2 * H].unsqueeze(1).broadcast_to([PN, 2, H]), ALU.add).then_inc(h2_done, 1)
                for m in range(4):
                    rope(p + 1, m)
                for b in range(2):
                    t = slice(2 * b, 2 * b + 2)
                    pool.wait_ge(xn_done, 2 * p + (b + 1))
                    pool.wait_ge(rms_done, 2 * p + (b + 1))
                    own(pool.tensor_tensor(h2[:, t, :], h2[:, t, :],
                                           bcm[:, b, 3 * H:4 * H].unsqueeze(1).broadcast_to([PN, 2, H]), ALU.mult))
                    pool.tensor_tensor(h2[:, t, :], h2[:, t, :], xres[:, t, :], ALU.add).then_inc(base_done, 1)
                assert own.n == POOL_ROUND, own.n

            for c in range(TT * TOPK):
                if c == 0:
                    pool.wait_ge(sidx_done, NPAIR)
                scatter(c)

            for par in range(2):
                pool.wait_ge(st_y[par], 16 * E // 4)
            for q in range(NPAIR):
                for t in range(TT):
                    if q >= 1:
                        pool.wait_ge(acc_done, TT * (q - 1) + (t + 1))
                    for c in range(t * TOPK, (t + 1) * TOPK):
                        pool.indirect_dma_start(out=gat[:, t, c % TOPK, :], out_offset=None, in_=y_d,
                                                in_offset=bass.IndirectOffsetOnAxis(ap=gidx[:, q, c:c + 1], axis=0))\
                            .then_inc(ld_gat[t], 16)

        @block.vector
        def _(dve):
            pre = Chain(dve, dve_own)
            dve.wait_ge(sct_ps, 1)
            dve.tensor_copy(scT[:, :, :], PT[0][:, 0:HC * B].rearrange("p (c b) -> p c b", b=B)).then_inc(sct_done, 1)
            dve.wait_ge(mod_ps, 1)
            for j, bk in enumerate((PJ[0], PJ[1], SC[0])):
                pre(dve.tensor_copy(mod[:, j * 512:(j + 1) * 512], bk[0:B, :]))
            for part in (1, 4):
                pre(dve.tensor_scalar(mod[:, part * H:(part + 1) * H], mod[:, part * H:(part + 1) * H], 1.0, None, ALU.add))
            for part in (2, 5):
                gate = mod[:, part * H:(part + 1) * H]
                pre(dve.scalar_tensor_tensor(gabs[:, :], gate, -1.0, gate, ALU.mult, ALU.max))
                pre(dve.tensor_scalar(gabs[:, :], gabs[:, :], 0.25, None, ALU.max))
                pre(dve.tensor_scalar(gsgn[:, :], gate, 0.0, 2.0, ALU.is_ge, ALU.mult))
                pre(dve.scalar_tensor_tensor(gate, gsgn[:, :], -1.0, gabs[:, :], ALU.add, ALU.mult))
            dve.tensor_copy(gsgn[:, 0:1], gabs[:, 0:1]).then_inc(mod_done, 1)
            dve.wait_ge(modt_ps, 1)
            dve.tensor_copy(modT[:, :, 0:B], PT[0][:, 64:64 + 4 * B].rearrange("p (k b) -> p k b", b=B)).then_inc(modt_done, 1)

            def prepare_norm(p, own):
                dve.wait_ge(ld_xin, 16 * (p + 1))
                for t in range(TT):
                    last = dve.bn_stats(st1[:, t, :], xin[:, t, :])
                own(last, plain=True)
                for t in range(TT):
                    last = dve.bn_aggr(mv1[:, t, :], st1[:, t, :])
                last.then_inc(var1, 1)
                dve.wait_ge(std1_done, p + 1)
                own(dve.reciprocal(std1[:, 1, :], std1[:, 0, :]))
                for t in range(TT):
                    last = dve.tensor_scalar(xin[:, t, :], xin[:, t, :], mv1[:, t, 0:1], std1[:, 1, t:t + 1],
                                             ALU.subtract, ALU.mult)
                last.then_inc(xhat_done, 1)

            def prepare_lo(p):
                dve.wait_ge(h_hi_done, p + 1)
                dve.tensor_tensor(hT_lo[:, :, :], qsw[:, :, :], hT_hi[:, :, :].bitcast(F32), ALU.subtract).then_inc(h_lo_done, 1)

            def project(p, m):
                g, r = m // 4, m % 4
                dve.wait_ge(pj_act, UNITS * p + (m + 1))
                if r == 2:
                    if g >= 1 or later(p):
                        dve.wait_ge(vt_ps, GROUPS * p + g)
                    dve.scalar_tensor_tensor(pair3(vT[:, :]), pair3(PJ[m % 2][:, :]), cwv[:, 2 * g + 1:2 * g + 2],
                                             v0[:, :, 0:S], ALU.mult, ALU.add).then_inc(pj_dve, 1)
                    return
                dve.tensor_tensor(pair3(rope_buffer(m)), pair3(PJ[m % 2][:, :]), both(cosT[:, :]), ALU.mult).then_inc(pj_dve, 1)

            def k_conv(p, g):
                dve.wait_ge(k0_done, GROUPS * p + (g + 1))
                dve.scalar_tensor_tensor(pair3(kc[:, g % 2, :]), pair3(kr[:, :]), cwk[:, 2 * g + 1:2 * g + 2],
                                         k0[:, :, 0:S], ALU.mult, ALU.add).then_inc(kc_done, 1)

            def first_group(p):
                project(p, 0)
                project(p, 1)
                project(p, 2)
                k_conv(p, 0)
                project(p, 3)

            def scores(p, n):
                dve.wait_ge(sc_ps, UNITS * p + (n + 1))
                if n >= 2:
                    dve.wait_ge(exp_done, UNITS * p + (n - 1))
                met(dve)
                for j, (a, z) in enumerate(((0, PN), (PN, 3 * PN))):
                    last = dve.tensor_tensor_reduce(out=sneg[:, n % 2, a:z], in0=SC[n % 2][:, a:z], in1=mask[:, a:z],
                                                    scale=-float(HD) ** -0.5, scalar=3.4e38, op0=ALU.add, op1=ALU.min,
                                                    accum_out=nmax[:, n % 4, j:j + 1])
                last.then_inc(sneg_done, 1)

            def normalise(p, n):
                dve.wait_ge(exp_done, UNITS * p + (n + 1))
                dve.reciprocal(rinv[:, n % 4, :], rsum[:, n % 4, :]).then_inc(rinv_done, 1)
                dve.wait_ge(rinv_done, UNITS * p + (n + 1))
                for j, (a, z) in enumerate(((0, PN), (PN, 3 * PN))):
                    last = dve.tensor_scalar(prob[:, n % 3, a:z], prob[:, n % 3, a:z], rinv[:, n % 4, j:j + 1], None, ALU.mult)
                last.then_inc(norm_done, 1)

            def transposed(p, n):
                dve.wait_ge(pt_ps, UNITS * p + (n + 1))
                if n >= 2:
                    dve.wait_ge(pv_ps, UNITS * p + (n - 1))
                dve.tensor_copy(pT[:, n % 2, :], PT[n % 2][:, 0:3 * PN]).then_inc(pt_done, 1)

            def slot(p, n):
                m = n + 4
                if n < UNITS:
                    scores(p, n)
                if 0 < n <= UNITS:
                    normalise(p, n - 1)
                if m < UNITS:
                    project(p, m)
                if m < UNITS and m % 4 == 2:
                    k_conv(p, m // 4)
                if T_LAG <= n < UNITS + T_LAG:
                    transposed(p, n - T_LAG)

            prepare_norm(0, pre)
            for n, j in enumerate(W_ORDER):
                dve.wait_ge(w_hi_done, n + 1)
                dve.tensor_tensor(w_lo[:, :, j * WC:(j + 1) * WC], wraw[:, :, j * WC:(j + 1) * WC],
                                  w_hi[:, :, j * WC:(j + 1) * WC].bitcast(F32), ALU.subtract).then_inc(w_lo_done, 1)
                if n == 0:
                    prepare_lo(0)
            dve.wait_ge(wr_hi_done, 1)
            dve.tensor_tensor(wr_lo[:, :, :], wr[:, :, :], wr_hi[:, :, :].bitcast(F32), ALU.subtract).then_inc(wr_lo_done, 1)
            dve.wait_ge(fills, 7)
            dve.wait_ge(ld_const, 160)
            first_group(0)
            dve.wait_ge(st_mod, 16)
            pre(dve.memset(zz[:, :, E:E + TOPK], SENTINEL))
            assert pre.n == DVE_PRE, pre.n

            with dve.Fori(0, NPAIR) as p:
                own = Chain(dve, dve_own, DVE_PRE + DVE_ROUND * p)
                for n in range(UNITS + T_LAG):
                    slot(p, n)
                    if n == UNITS - 2:
                        prepare_norm(p + 1, own)
                dve.wait_ge(ld_bcm, 32 * (p + 1))
                dve.wait_ge(st_base, 32 * p + FREE)
                dve.wait_ge(st_scat, 16 * TT * TOPK * (p + 1))
                prepare_lo(p + 1)
                for b in range(2):
                    dve.wait_ge(y_ps, TT * p + (2 * b + 2) + FREE)
                    dve.tensor_tensor(yg[:, b, :, :], SC[b][:, :].rearrange("p (t h) -> p t h", h=H),
                                      bcm[:, b, 0:H].unsqueeze(1).broadcast_to([PN, 2, H]), ALU.mult).then_inc(yg_done, 1)
                for b in range(2):
                    dve.wait_ge(x1_done, 2 * p + (b + 1))
                    for t in range(2 * b, 2 * b + 2):
                        last = dve.bn_stats(st2[:, t, :], xres[:, t, :])
                    own(last, plain=True)
                    for t in range(2 * b, 2 * b + 2):
                        last = dve.bn_aggr(mv2[:, t, :], st2[:, t, :])
                    last.then_inc(var2, 1)
                for b in range(2):
                    dve.wait_ge(std2_done, 2 * p + (b + 1))
                    own(dve.reciprocal(std2[:, 1, 2 * b:2 * b + 2], std2[:, 0, 2 * b:2 * b + 2]))
                    for t in range(2 * b, 2 * b + 2):
                        last = dve.tensor_scalar(h2[:, t, :], xres[:, t, :], mv2[:, t, 0:1], std2[:, 1, t:t + 1],
                                                 ALU.subtract, ALU.mult)
                    last.then_inc(xh2_done, 1)
                for b in range(2):
                    dve.wait_ge(rms_done, 2 * p + (b + 1))
                    own(dve.reciprocal(rms[:, 2, 2 * b:2 * b + 2], rms[:, 1, 2 * b:2 * b + 2]))
                    for t in range(2 * b, 2 * b + 2):
                        last = dve.scalar_tensor_tensor(xn[:, t, :], h2[:, t, :], rms[:, 2, t:t + 1], wnorm[:, :],
                                                        ALU.mult, ALU.mult)
                    last.then_inc(xn_done, 1)
                first_group(p + 1)
                for b in range(2):
                    dve.wait_ge(xnt_hi_done, 2 * p + (b + 1))
                    dve.wait_ge(st_xnt, 64 * p + 32 * b + FREE)
                    for c in range(HC):
                        last = dve.tensor_tensor(xnT_lo[:, c, :], PT[c][:, b * S:(b + 1) * S],
                                                 xnT_hi[:, c, :].bitcast(F32), ALU.subtract)
                    last.then_inc(xnt_lo_done, 1)
                logits = XB[:, 0:TT * LCOL].rearrange("p (t c) -> p t c", c=LCOL)[:, :, 0:E]
                dve.wait_ge(lg_ps, 2 * p + 2 + FREE)
                own(dve.tensor_reduce(red[:, 0, :], logits, AXX, ALU.max))
                own(dve.tensor_tensor(zz[:, :, 0:E], logits, red[:, 0, :].unsqueeze(2).broadcast_to([PN, TT, E]), ALU.subtract))
                dve.tensor_scalar(zz[:, :, 0:E], zz[:, :, 0:E], PROB_FLOOR, None, ALU.max).then_inc(z_done, 1)
                dve.wait_ge(z_done, p + 1)
                met(dve)
                for t in range(TT):
                    last = dve.max(top8[:, t, :], zz[:, t, :])
                own(last, plain=True)
                for t in range(TT):
                    last = dve.match_replace(zz2[:, t, :], top8[:, t, :], zz[:, t, :], TAKEN)
                own(last)
                dve.tensor_scalar(chosen[:, :, :], zz2[:, :, 0:E], TAKEN / 2, None, ALU.is_lt).then_inc(chosen_done, 1)
                dve.wait_ge(ex_done, p + 1)
                own(dve.tensor_reduce(red[:, 1, :], ex[:, :, :], AXX, ALU.add))
                own(dve.reciprocal(red[:, 3, :], red[:, 1, :]))
                own(dve.tensor_tensor(ex[:, :, :], ex[:, :, :], red[:, 3, :].unsqueeze(2).broadcast_to([PN, TT, E]), ALU.mult))
                own(dve.tensor_scalar(red[:, 2, :], red[:, 2, :], 1.0, None, ALU.add))
                own(dve.reciprocal(sgate[:, bass.ds(p, 1), :].rearrange("p a t -> p (a t)"), red[:, 2, :]))
                dve.wait_ge(pos_ps, p + 1)
                pos = XB[:, 256:256 + TT * E].rearrange("p (t e) -> p t e", e=E)
                own(dve.scalar_tensor_tensor(kept[:, :, :], pos, float(CAP), chosen[:, :, :], ALU.is_lt, ALU.mult))
                own(dve.tensor_tensor(key[:, :, :], pos, ebase[:, :].unsqueeze(1).broadcast_to([PN, TT, E]), ALU.add))
                own(dve.tensor_tensor(key[:, :, :], key[:, :, :], kept[:, :, :], ALU.mult))
                own(dve.tensor_tensor(ex[:, :, :], ex[:, :, :], kept[:, :, :], ALU.mult), plain=True)
                for t in range(TT):
                    last = dve.max(key8[:, t, :], key[:, t, :])
                own(last)
                own(dve.tensor_scalar(late[:, :, :], key8[:, :, 0:TOPK], 0.0, float(SKIP), ALU.is_equal, ALU.mult))
                dve.scalar_tensor_tensor(sidx[:, :].rearrange("p (t k) -> p t k", k=TOPK), key8[:, :, 0:TOPK], -1.0,
                                         late[:, :, :], ALU.add, ALU.add).then_inc(sidx_done, 1)
                own(dve.tensor_scalar(gidx[:, bass.ds(p, 1), :].rearrange("p a (t k) -> p (a t) k", k=TOPK),
                                      key8[:, :, 0:TOPK], -1.0, 0.0, ALU.add, ALU.max))
                own(dve.tensor_tensor(eq[:, :, :, :], key[:, :, :].unsqueeze(2).broadcast_to([PN, TT, TOPK, E]),
                                      key8[:, :, 0:TOPK].unsqueeze(3).broadcast_to([PN, TT, TOPK, E]), ALU.is_equal))
                own(dve.tensor_tensor(eq[:, :, :, :], eq[:, :, :, :],
                                      ex[:, :, :].unsqueeze(2).broadcast_to([PN, TT, TOPK, E]), ALU.mult))
                own(dve.tensor_reduce(wsel[:, bass.ds(p, 1), :].rearrange("p a (t k) -> p (a t) k", k=TOPK),
                                      eq[:, :, :, :], AXX, ALU.add))
                own(dve.tensor_reduce(carry[:, 1, :], chosen[:, :, :].rearrange("p t e -> p e t"), AXX, ALU.add))
                own(dve.tensor_tensor(carry[:, 0, :], carry[:, 0, :], carry[:, 1, :], ALU.add))
                assert own.n == DVE_ROUND, own.n
                dve.tensor_copy(carry[:, 1, 0:1], carry[:, 0, 0:1]).then_inc(route_done, 1)

            dve.wait_ge(sw_hi_done, 1)
            dve.tensor_tensor(sw_lo[:, :, :], swraw[:, :, :], sw_hi[:, :, :].bitcast(F32), ALU.subtract).then_inc(sw_lo_done, 1)

            def expert_slot(base, n, lo=0, hi=10 ** 9):
                if lo <= n < hi:
                    dve.wait_ge(xe_ps, base + (n + 1))
                    if n >= 2 or later(base):
                        dve.wait_ge(gu_ps, base + (n - 1))
                    dve.tensor_copy(xeT[:, n % 2, :], PJ[n % 2][:, 0:H]).then_inc(xe_done, 1)
                if lo <= n - 1 < hi:
                    dve.wait_ge(sgl_done, base + n)
                    if n - 1 >= 2 or later(base):
                        dve.wait_ge(hh_ps, base + (n - 2))
                    dve.tensor_tensor(hh[:, (n - 1) % 2, :], SC[(n - 1) % 2][:, F:2 * F], sgl[:, (n - 1) % 2, :],
                                      ALU.mult).then_inc(hh_done, 1)
                if lo <= n - 3 < hi:
                    dve.wait_ge(ye_ps, base + (n - 2))
                    pair = (n - 3) // 2
                    if pair >= 2 or later(base):
                        dve.wait_ge(st_y[pair % 2], 4 * base + 16 * (pair // 2))
                    bk = (OB, XB)[(n - 3) % 2]
                    dve.tensor_copy(ye[:, (n - 3) % 4, :], bk[:, 0:H]).then_inc(ye_done, 1)

            def hidden(q, f):
                fw = min(PN, FS - f * PN)
                dve.wait_ge(sg2_done, FT * q + (f + 1))
                if f == 0 and later(q):
                    dve.wait_ge(dn_ps, TT * q)
                dve.tensor_tensor(hs[0:fw, f, :], SC[f % 2][0:fw, :], sg2[0:fw, f % 2, :], ALU.mult).then_inc(hs_done, 1)

            def combine(q, t):
                own = Chain(dve, acc_own, TOPK * (TT * q + t))
                dve.wait_ge(shrow_done, TT * q + (t + 1))
                dve.wait_ge(ld_gat[t], 16 * TOPK * (q + 1))
                before = shrow[:, bass.ds(TT * q + t, 1), :].rearrange("p a h -> p (a h)")
                for k in range(TOPK):
                    own(dve.scalar_tensor_tensor(
                        acc[:, t % 2, :], gat[:, t, k, :],
                        wsel[:, bass.ds(q, 1), t * TOPK + k:t * TOPK + k + 1].rearrange("p a t -> p (a t)"),
                        before, ALU.mult, ALU.add))
                    before = acc[:, t % 2, :]
                dve.wait_ge(st_out[t % 2], 8 * TT * q + 16 * (t // 2) + FREE)
                dve.tensor_tensor(fin[:, t % 2, :], acc[:, t % 2, :],
                                  gball[:, bass.ds(2 * q + t // 2, 1), :].rearrange("p a h -> p (a h)"),
                                  ALU.mult).then_inc(acc_done, 1)
                dve.wait_ge(acc_done, TT * q + (t + 1))
                dve.wait_ge(ld_bas[t % 2], 8 * TT * q + 16 * (t // 2 + 1))
                dve.tensor_tensor(fin[:, t % 2, :], fin[:, t % 2, :], bas[:, t % 2, :], ALU.add).then_inc(fin_done, 1)

            dve.wait_ge(base_done, 2 * NPAIR + FREE)
            for f in range(FT):
                hidden(0, f)

            for n in range(RING):
                expert_slot(0, n)
            with dve.Fori(1, E // RING) as r:
                for n in range(RING):
                    expert_slot(RING * r, n, lo=-RING)
            for n in range(3):
                expert_slot(E, n, lo=-RING, hi=0)

            dve.wait_ge(ld_gb, 16)
            with dve.Fori(1, NPAIR) as q:
                for f in range(FT):
                    hidden(q, f)
                    if f >= FT - 3:
                        combine(q - 1, f - (FT - 3))
                combine(q - 1, TT - 1)
            for t in range(TT):
                combine(NPAIR - 1, t)

        @block.tensor
        def _(pe):
            def halves(out_ap, pieces, hi_lo):
                (w1, w2), (x1, x2) = hi_lo
                steps = [(c, a, b_) for c in range(pieces) for a, b_ in ((w1, x1), (w1, x2), (w2, x1))]
                for n, (c, a, b_) in enumerate(steps):
                    last = pe.matmul(out_ap, a(c), b_(c), start=(n == 0), stop=(n == len(steps) - 1))
                return last

            pe.wait_ge(silu_done, 1)
            for c in range(HC):
                last = pe.transpose(PT[0][:, c * B:(c + 1) * B], sc[:, c * PN:(c + 1) * PN], ident[0:B, 0:B])
            last.then_inc(sct_ps, 1)
            pe.wait_ge(sct_done, 1)
            pe.wait_ge(ld_wm, 16)
            for j, bk in enumerate((PJ[0], PJ[1], SC[0])):
                for c in range(HC):
                    last = pe.matmul(bk[0:B, :], scT[:, c, :], wm[:, c, j * 512:(j + 1) * 512], start=(c == 0), stop=(c == HC - 1))
            last.then_inc(mod_ps, 1)
            pe.wait_ge(mod_done, 1)
            for k in range(4):
                last = pe.transpose(PT[0][:, 64 + k * B:64 + (k + 1) * B], mod[:, k * PN:(k + 1) * PN], ident[0:B, 0:B])
            last.then_inc(modt_ps, 1)
            pe.wait_ge(modt_done, 1)

            def prepare_t(p):
                pe.wait_ge(xhat_done, p + 1)
                for c in range(HC):
                    for t in range(TT):
                        last = pe.transpose(PT[c][:, t * PN:(t + 1) * PN], xin[:, t, c * PN:(c + 1) * PN], ident[:, :])
                last.then_inc(ht_ps, 1)

            def project(p, m):
                g, r = m // 4, m % 4
                head = {0: NH + g, 1: 2 * g, 2: NH + NKV + g, 3: 2 * g + 1}[r]
                cols = slice(head * HD, (head + 1) * HD)
                if m == 0:
                    pe.wait_ge(h_lo_done, p + 1)
                if m >= 2 or later(p):
                    pe.wait_ge(pj_act, UNITS * p + (m - 1))
                    pe.wait_ge(pj_dve, UNITS * p + (m - 1))
                halves(PJ[m % 2][:, :], HC,
                       ((lambda c: w_hi[:, c, cols], lambda c: w_lo[:, c, cols]),
                        (lambda c: hT_hi[:, c, :], lambda c: hT_lo[:, c, :]))).then_inc(pj_ps, 1)

            def scores(p, n):
                g, h, b = n // 4, (n % 4) // 2, n % 2
                if n == 0:
                    pe.wait_ge(yg_done, 2 * p + FREE)
                if n >= 2:
                    pe.wait_ge(sneg_done, UNITS * p + (n - 1))
                if n % 4 == 0:
                    pe.wait_ge(kc_done, GROUPS * p + (g + 1))
                if n % 2 == 0:
                    pe.wait_ge(rope_done, ROPES * p + (3 * g + h + 2))
                q = qr[:, h, g % 2, b * S:(b + 1) * S]
                k = kc[:, g % 2, b * S:(b + 1) * S]
                pe.matmul(SC[n % 2][:, 0:PN], q[:, 0:PN], k[:, 0:PN], start=True, stop=True)
                pe.matmul(SC[n % 2][:, PN:3 * PN], q[:, PN:S], k, start=True, stop=True).then_inc(sc_ps, 1)

            def v_transpose(p, g):
                pe.wait_ge(pj_dve, UNITS * p + (4 * g + 3))
                if g >= 1:
                    pe.wait_ge(vn_done, GROUPS * p + g)
                else:
                    pe.wait_ge(route_done, p + FREE)
                for j in range(TT):
                    last = pe.transpose(XB[:, j * PN:(j + 1) * PN], vT[:, j * PN:(j + 1) * PN], ident[:, :])
                last.then_inc(vt_ps, 1)

            def p_transpose(p, n):
                pe.wait_ge(norm_done, UNITS * p + (n + 1))
                if n >= 2:
                    pe.wait_ge(pt_done, UNITS * p + (n - 1))
                elif n == 0:
                    pe.wait_ge(xnt_lo_done, 2 * p + FREE)
                for j in range(3):
                    last = pe.transpose(PT[n % 2][:, j * PN:(j + 1) * PN], prob[:, n % 3, j * PN:(j + 1) * PN], ident[:, :])
                last.then_inc(pt_ps, 1)

            def weighted_v(p, n):
                g, b = n // 4, n % 2
                pe.wait_ge(pt_done, UNITS * p + (n + 1))
                if n >= 1:
                    pe.wait_ge(ot_done, UNITS * p + n)
                if n % 4 == 0:
                    pe.wait_ge(vn_done, GROUPS * p + (g + 1))
                o = OB[:, (n % 2) * S:(n % 2 + 1) * S]
                v = vN[:, g % 2, b * S:(b + 1) * S]
                pe.matmul(o, v[:, 0:PN], pT[:, n % 2, 0:S], start=True, stop=False)
                pe.matmul(o[:, PN:S], v[:, PN:S], pT[:, n % 2, S:S + PN], start=False, stop=True).then_inc(pv_ps, 1)

            prepare_t(0)
            for m in range(4):
                if m in (0, 1, 2):
                    pe.wait_ge(w_lo_done, m + 1)
                project(0, m)
            pe.wait_ge(w_lo_done, 8)
            pe.wait_ge(ld_wo, 16)
            pe.wait_ge(wr_lo_done, 1)
            pe.wait_ge(fills, 7)
            pe.wait_ge(ld_const, 160)

            with pe.Fori(0, NPAIR) as p:
                for n in range(UNITS + PV_LAG):
                    if n + 4 < UNITS:
                        project(p, n + 4)
                    if n < UNITS:
                        scores(p, n)
                        if n % 4 == 0:
                            v_transpose(p, n // 4)
                    if T_LAG <= n < UNITS + T_LAG:
                        p_transpose(p, n - T_LAG)
                    if n >= PV_LAG:
                        weighted_v(p, n - PV_LAG)
                pe.wait_ge(pt_done, UNITS * (p + 1))
                prepare_t(p + 1)
                pe.wait_ge(ot_done, UNITS * (p + 1))
                for t in range(TT):
                    for h in range(NH):
                        last = pe.matmul(SC[t // 2][:, (t % 2) * H:(t % 2 + 1) * H], oT[:, h, t * PN:(t + 1) * PN],
                                         wo[:, h, :], start=(h == 0), stop=(h == NH - 1))
                    last.then_inc(y_ps, 1)
                for m in range(4):
                    project(p + 1, m)
                pe.wait_ge(h_hi_done, p + 2)
                for b in range(2):
                    pe.wait_ge(xn_done, 2 * p + (b + 1))
                    for c in range(HC):
                        for t in range(2 * b, 2 * b + 2):
                            last = pe.transpose(PT[c][:, t * PN:(t + 1) * PN], xn[:, t, c * PN:(c + 1) * PN], ident[:, :])
                    last.then_inc(xnt_ps, 1)
                    pe.wait_ge(xnt_lo_done, 2 * p + (b + 1) + FREE)
                    for t in range(2 * b, 2 * b + 2):
                        tk = slice((t % 2) * PN, (t % 2 + 1) * PN)
                        last = halves(XB[:, t * LCOL:t * LCOL + E + 2], HC,
                                      ((lambda c: xnT_hi[:, c, tk], lambda c: xnT_lo[:, c, tk]),
                                       (lambda c: wr_hi[:, c, :], lambda c: wr_lo[:, c, :])))
                    last.then_inc(lg_ps, 1)
                pe.wait_ge(chosen_done, p + 1)
                pe.wait_ge(ex_done, p + 1)
                for t in range(TT):
                    o = XB[:, 256 + t * E:256 + (t + 1) * E]
                    pe.matmul(o, ones[:, :], carry[:, 0, :], start=True, stop=False)
                    for u in range(t):
                        pe.matmul(o, ones[:, :], chosen[:, u, :], start=False, stop=False)
                    last = pe.matmul(o, tri[:, :], chosen[:, t, :], start=False, stop=True)
                last.then_inc(pos_ps, 1)

            def expert_slot(base, n, rnd, lo=0, hi=10 ** 9):
                if lo <= n < hi:
                    if n % 2 == 0:
                        pe.wait_ge(ld_xe[n // 2], 16 * rnd)
                    if n >= 2 or later(base):
                        pe.wait_ge(xe_done, base + (n - 1))
                    for c in range(HC):
                        last = pe.transpose(PJ[n % 2][:, c * PN:(c + 1) * PN], xe[:, n % RING, c * PN:(c + 1) * PN], ident[:, :])
                    last.then_inc(xe_ps, 1)
                if lo <= n - 1 < hi:
                    e, i = n - 1, (n - 1) % RING
                    pe.wait_ge(xe_done, base + (e + 1))
                    if e % 2 == 0:
                        pe.wait_ge(ld_e[i // 2], 48 * rnd)
                    if e >= 2 or later(base):
                        pe.wait_ge(hh_done, base + (e - 1))
                    for c in range(HC):
                        last = pe.matmul(SC[e % 2][:, 0:2 * F], xeT[:, e % 2, c * PN:(c + 1) * PN], wgu[:, i, c, :],
                                         start=(c == 0), stop=(c == HC - 1))
                    last.then_inc(gu_ps, 1)
                if lo <= n - 2 < hi:
                    e = n - 2
                    pe.wait_ge(hh_done, base + (e + 1))
                    if e >= 2 or later(base):
                        pe.wait_ge(hht_done, base + (e - 1))
                    for c in range(2):
                        last = pe.transpose(PT[e % 2][0:FH, c * PN:(c + 1) * PN], hh[:, e % 2, c * FH:(c + 1) * FH], ident[:, :])
                    last.then_inc(hh_ps, 1)
                if lo <= n - 3 < hi:
                    e, i = n - 3, (n - 3) % RING
                    pe.wait_ge(hht_done, base + (e + 1))
                    if e >= 2 or later(base):
                        pe.wait_ge(ye_done, base + (e - 1))
                    bk = (OB, XB)[e % 2]
                    for c in range(2):
                        last = pe.matmul(bk[:, 0:H], hhT[:, e % 2, c * PN:(c + 1) * PN], wd[:, i, c, :],
                                         start=(c == 0), stop=(c == 1))
                    last.then_inc(ye_ps, 1)

            def shared(q):
                pe.wait_ge(ld_xs, 32 * (q + 1))
                for f in range(FT):
                    fw = min(PN, FS - f * PN)
                    if f >= 2 or later(q):
                        pe.wait_ge(hs_done, FT * q + (f - 1))
                    for off, bk in ((0, PJ[f % 2]), (FS, SC[f % 2])):
                        cols = slice(off + f * PN, off + f * PN + fw)
                        last = halves(bk[0:fw, :], HC,
                                      ((lambda c: sw_hi[:, c, cols], lambda c: sw_lo[:, c, cols]),
                                       (lambda c: xs_hi[:, c, :], lambda c: xs_lo[:, c, :])))
                    last.then_inc(sh_ps, 1)
                pe.wait_ge(hs_done, FT * (q + 1))
                for t in range(TT):
                    if t >= 2 or later(q):
                        pe.wait_ge(shrow_done, TT * q + (t - 1))
                    bk = (OB, XB)[t % 2]
                    for f in range(FT):
                        fw = min(PN, FS - f * PN)
                        last = pe.matmul(bk[:, 0:H], hs[0:fw, f, t * PN:(t + 1) * PN], swd[0:fw, f, :],
                                         start=(f == 0), stop=(f == FT - 1))
                    last.then_inc(dn_ps, 1)

            pe.wait_ge(route_done, NPAIR + FREE)
            pe.wait_ge(sw_lo_done, 1)
            pe.wait_ge(ld_swd, 32)
            shared(0)
            pe.wait_ge(shrow_done, TT)
            for n in range(RING):
                expert_slot(0, n, 1)
            with pe.Fori(1, E // RING) as r:
                for n in range(RING):
                    expert_slot(RING * r, n, r + 1, lo=-RING)
            for n in range(3):
                expert_slot(E, n, E // RING + 1, lo=-RING, hi=0)
            pe.wait_ge(ye_done, E)
            with pe.Fori(1, NPAIR) as q:
                shared(q)


_INS = ['L0_attn_hidden', 'L0_attn_W_pack', 'L0_attn_W_o', 'L0_attn_conv_k', 'L0_attn_conv_v', 'L0_ffn_w_norm',
        'L0_ffn_w_router', 'L0_ffn_w_gate', 'L0_ffn_w_up', 'L0_ffn_w_down', 'L0_ffn_sw_gate', 'L0_ffn_sw_up',
        'L0_ffn_sw_down', 'L0_ffn_w_shared_gate', 'L0_c', 'L0_wmod']
_OUTS = [((B, S, H), 'float32')]


def _constants():
    import numpy as _np
    f = _np.float32
    inv_freq = f(1.0) / f(100000.0) ** (_np.arange(0, HD, 2, dtype=f) / f(HD))
    freqs = _np.outer(_np.arange(S, dtype=f), inv_freq).astype(f).T
    cos, sin = _np.cos(freqs).astype(f), _np.sin(freqs).astype(f)
    i, j = _np.arange(PN)[:, None], _np.arange(PN)[None, :]
    causal, window = j <= i, j > i
    allowed = _np.concatenate([causal, window, causal], axis=1)
    return [_np.concatenate([cos, cos], axis=0), _np.concatenate([-sin, sin], axis=0),
            _np.where(allowed, f(0.0), f(-3.0e38)).astype(f), _np.eye(PN, dtype=f), (i < j).astype(f),
            _np.tile((_np.arange(E) * CAP + 1).astype(f), (PN, 1))]


def kernel(**inputs):
    import numpy as _np
    import concourse.bacc as _bacc
    from concourse import mybir as _mybir
    from concourse.bass_utils import run_bass_kernel_spmd as _run

    nc = _bacc.Bacc("TRN2", target_bir_lowering=False, num_devices=1)
    arrays, args = {}, []
    host = [_np.ascontiguousarray(inputs[name]) for name in _INS] + _constants()
    for n, a in enumerate(host):
        if n == 0:
            a = a.reshape(B * S, H)
        name = f"in_{n}_dram"
        arrays[name] = a
        args.append(nc.dram_tensor(name, a.shape, _mybir.dt.from_np(a.dtype), kind="ExternalInput").ap())
    out = nc.dram_tensor("out_0_dram", (B * S, H), _mybir.dt.float32, kind="ExternalOutput").ap()
    adaln_block(nc, *args, out)
    r = _run(nc, [arrays], core_ids=[0])
    return r.results[0]["out_0_dram"].reshape(B, S, H)
```

```python
from contextlib import ExitStack

import concourse.bass as bass
from concourse import mybir

F32 = mybir.dt.float32
F32R = mybir.dt.float32r
I32 = mybir.dt.int32
ALU = mybir.AluOpType
ACT = mybir.ActivationFunctionType
AXX = mybir.AxisListType.X

PN = 128
B, S, H = 8, 256, 256
HC = H // PN
NH, NKV, HD = 16, 8, 128
E, TOPK, F, CAP = 32, 4, 176, 128
FH = F // 2
FS = 704
FT = -(-FS // PN)
NPAIR = B // 2
LAST = NPAIR - 1
TOK = 2 * S
TT = TOK // PN
F_EARLY = 3
GROUPS = NKV
UNITS = 4 * GROUPS
ROPES = 3 * GROUPS
QKV = (NH + 2 * NKV) * HD
LN_EPS, RMS_EPS = 1e-5, 1e-6
ROPE_OF = {0: 0, 1: 1, 3: 2}
EARLY = 25
T_LAG, PV_LAG = 2, 3
PROB_FLOOR = -87.34
SENTINEL, TAKEN = 1.0, -1000.0
SKIP = 2 * E * CAP
RING = 8
HALF = RING // 2
FREE = 1
LCOL = 64


def adaln_block(nc, x, w_pack, w_o, conv_k, conv_v, w_norm, w_router, w_gate, w_up, w_down, sw_gate, sw_up,
                sw_down, w_sgate, c_in, wmod, cos_t, sin_t, mask_t, ident_t, tri_t, ebase_t, out):
    ctx = ExitStack()
    with ctx:
        def sb(name, shape, dt=F32, where=ctx):
            return where.enter_context(nc.sbuf_tensor(name, shape, dt))

        def sem(name):
            return ctx.enter_context(nc.semaphore(name))

        mod_d = nc.dram_tensor("mod_rows", [B, 4 * H], F32, kind="Internal").ap()
        slots_d = nc.dram_tensor("slot_rows", [E * CAP, H], F32, kind="Internal").ap()
        y_d = nc.dram_tensor("expert_rows", [E * CAP, H], F32, kind="Internal").ap()
        base_d = nc.dram_tensor("residual_rows", [B * S, H], F32, kind="Internal").ap()
        xnt_d = nc.dram_tensor("xn_transposed", [NPAIR, PN, 2, HC, TOK], F32, kind="Internal").ap()

        cosT = sb("cosT", [PN, S])
        sinT = sb("sinT", [PN, S])
        mask = sb("mask", [PN, 3 * PN])
        ident = sb("ident", [PN, PN])
        tri = sb("tri", [PN, PN])
        ones = sb("ones", [PN, PN])
        ebase = sb("ebase", [PN, E])
        wnorm = sb("wnorm", [PN, H])
        cwk = sb("cwk", [PN, 2 * NKV])
        cwv = sb("cwv", [PN, 2 * NKV])
        modT = sb("modT", [PN, 4, B])
        scT = sb("scT", [PN, HC, B])
        wr = sb("wr", [PN, HC, E + 2])
        wr_hi = sb("wr_hi", [PN, HC, E + 2], F32R)
        wr_lo = sb("wr_lo", [PN, HC, E + 2], F32R)
        gidx = sb("gidx", [PN, NPAIR, TT * TOPK], I32)
        wsel = sb("wsel", [PN, NPAIR, TT * TOPK])
        sgate = sb("sgate", [PN, NPAIR, TT])
        carry = sb("carry", [PN, 2, E])

        att = ExitStack()
        hT_hi = sb("hT_hi", [PN, HC, TOK], F32R, att)
        hT_lo = sb("hT_lo", [PN, HC, TOK], F32R, att)
        qsw = sb("qsw", [PN, 2, TOK], F32, att)
        qr = sb("qr", [PN, 2, 2, TOK], F32, att)
        kr = sb("kr", [PN, TOK], F32, att)
        k0 = sb("k0", [PN, 2, S + 1], F32, att)
        v0 = sb("v0", [PN, 2, S + 1], F32, att)
        kc = sb("kc", [PN, 2, TOK], F32, att)
        vT = sb("vT", [PN, TOK], F32, att)
        xin = sb("xin", [PN, TT, H], F32, att)
        xres = sb("xres", [PN, TT, H], F32, att)
        bcm = sb("bcm", [PN, 2, 4 * H], F32, att)
        vN = sb("vN", [PN, 2, TOK], F32, att)
        rows8 = ExitStack()
        c_sb = sb("c_sb", [B, H], F32, rows8)
        sc = sb("sc", [B, H], F32, rows8)
        rows8.close()
        sneg = sb("sneg", [PN, 2, 3 * PN], F32, att)
        nmax = sb("nmax", [PN, 4, 2], F32, att)
        prob = sb("prob", [PN, 3, 3 * PN], F32, att)
        rsum = sb("rsum", [PN, 4, 2], F32, att)
        rinv = sb("rinv", [PN, 4, 2], F32, att)
        pT = sb("pT", [PN, 2, 3 * PN], F32, att)
        wo = sb("wo", [PN, NH, H], F32, att)
        st1 = sb("st1", [PN, TT, 6], F32, att)
        mv1 = sb("mv1", [PN, TT, 2], F32, att)
        std1 = sb("std1", [PN, 2, TT], F32, att)
        mods = ExitStack()
        wm = sb("wm", [PN, HC, 6 * H], F32, mods)
        mod = sb("mod", [B, 4 * H], F32, mods)
        gabs = sb("gabs", [B, H], F32, mods)
        gsgn = sb("gsgn", [B, H], F32, mods)
        mods.close()
        xnT_hi = sb("xnT_hi", [PN, HC, TOK], F32R, att)
        xnT_lo = sb("xnT_lo", [PN, HC, TOK], F32R, att)
        yg = sb("yg", [PN, 2, 2, H], F32, att)
        h2 = sb("h2", [PN, TT, H], F32, att)
        xn = sb("xn", [PN, TT, H], F32, att)
        st2 = sb("st2", [PN, TT, 6], F32, att)
        mv2 = sb("mv2", [PN, TT, 2], F32, att)
        std2 = sb("std2", [PN, 2, TT], F32, att)
        rms = sb("rms", [PN, 3, TT], F32, att)
        zz = sb("zz", [PN, TT, E + TOPK], F32, att)
        top8 = sb("top8", [PN, TT, 8], F32, att)
        key8 = sb("key8", [PN, TT, 8], F32, att)
        red = sb("red", [PN, 4, TT], F32, att)
        ex = sb("ex", [PN, TT, E], F32, att)
        chosen = sb("chosen", [PN, TT, E], F32, att)
        key = sb("key", [PN, TT, E], F32, att)
        late = sb("late", [PN, TT, TOPK], F32, att)
        sidx = sb("sidx", [PN, TT * TOPK], I32, att)
        before_eq = ExitStack()
        zz2 = sb("zz2", [PN, TT, E + TOPK], F32, before_eq)
        kept = sb("kept", [PN, TT, E], F32, before_eq)
        before_eq.close()
        eq = sb("eq", [PN, TT, TOPK, E], F32, att)
        outs = ExitStack()
        oT = sb("oT", [PN, NH, TOK], F32, outs)
        proj_w = ExitStack()
        w_hi = sb("w_hi", [PN, HC, QKV], F32R, proj_w)
        raws = ExitStack()
        wraw = sb("wraw", [PN, HC, QKV], F32, raws)
        raws.close()
        w_lo = sb("w_lo", [PN, HC, QKV], F32R, proj_w)
        proj_w.close()

        exps = ExitStack()
        wgu = sb("wgu", [PN, RING, HC, 2 * F], F32, exps)
        wd = sb("wd", [FH, RING, 2, H], F32, exps)
        sw_hi = sb("sw_hi", [PN, HC, 2 * FS], F32R, exps)
        sw_stack = ExitStack()
        swraw = sb("swraw", [PN, HC, 2 * FS], F32, sw_stack)
        sw_stack.close()
        sw_lo = sb("sw_lo", [PN, HC, 2 * FS], F32R, exps)
        exps.close()
        outs.close()
        shar = ExitStack()
        swd = sb("swd", [PN, FT, H], F32, shar)
        shar.close()
        att.close()
        xs_hi = sb("xs_hi", [PN, HC, TOK], F32R)
        xs_lo = sb("xs_lo", [PN, HC, TOK], F32R)
        hs = sb("hs", [PN, FT, TOK])
        sg2 = sb("sg2", [PN, 2, TOK])
        shrow = sb("shrow", [PN, NPAIR * TT, H])
        gat = sb("gat", [PN, TT, TOPK, H])
        gball = sb("gball", [PN, B, H])
        bas = sb("bas", [PN, 2, H])
        acc = sb("acc", [PN, 2, H])
        fin = sb("fin", [PN, 2, H])
        xe = sb("xe", [PN, RING, H])
        xeT = sb("xeT", [PN, 2, H])
        sgl = sb("sgl", [PN, 2, F])
        hh = sb("hh", [PN, 2, F])
        hhT = sb("hhT", [FH, 2, 2 * PN])
        ye = sb("ye", [PN, 4, H])

        def bank(name):
            return ctx.enter_context(nc.psum_tensor(name, [PN, 512], F32))

        PJ = [bank("PJ0"), bank("PJ1")]
        SC = [bank("SC0"), bank("SC1")]
        PT = [bank("PT0"), bank("PT1")]
        OB = bank("OB")
        XB = bank("XB")
        DN = (OB, PT[0])

        ld_c, ld_ident, ld_wm, ld_xin, ld_xres, ld_bcm = sem("ld_c"), sem("ld_ident"), sem("ld_wm"), sem("ld_xin"), sem("ld_xres"), sem("ld_bcm")
        ld_wmr, ld_const, ld_wr, ld_wo = sem("ld_wmr"), sem("ld_const"), sem("ld_wr"), sem("ld_wo")
        ld_w = [sem(f"ld_w{j}") for j in range(8)]
        st_mod, st_zero, st_base, st_xnt, st_scat = sem("st_mod"), sem("st_zero"), sem("st_base"), sem("st_xnt"), sem("st_scat")
        silu_done, sct_ps, sct_done, mod_ps, rows_done, mod_done, modt_ps, modt_done = (
            sem(n) for n in ("silu_done", "sct_ps", "sct_done", "mod_ps", "rows_done", "mod_done", "modt_ps", "modt_done"))
        w_hi_done, w_lo_done, wr_hi_done, wr_lo_done, fills = (
            sem(n) for n in ("w_hi_done", "w_lo_done", "wr_hi_done", "wr_lo_done", "fills"))
        waits_met = sem("waits_met")
        dve_own, act_own, pool_own = sem("dve_own"), sem("act_own"), sem("pool_own")
        var1, std1_done, xhat_done, ht_ps, h_hi_done, h_lo_done = (
            sem(n) for n in ("var1", "std1_done", "xhat_done", "ht_ps", "h_hi_done", "h_lo_done"))
        pj_ps, pj_act, pj_dve, t2_done, rope_done, k0_done, kc_done, vt_ps, vn_done = (
            sem(n) for n in ("pj_ps", "pj_act", "pj_dve", "t2_done", "rope_done", "k0_done", "kc_done", "vt_ps", "vn_done"))
        sc_ps, sneg_done, exp_done, rinv_done, norm_done, pt_ps, pt_done, pv_ps, ot_done = (
            sem(n) for n in ("sc_ps", "sneg_done", "exp_done", "rinv_done", "norm_done", "pt_ps", "pt_done", "pv_ps", "ot_done"))
        y_ps, yg_done, x1_done, var2, std2_done, xh2_done, h2_done, rms_done, xn_done, base_done = (
            sem(n) for n in ("y_ps", "yg_done", "x1_done", "var2", "std2_done", "xh2_done", "h2_done", "rms_done", "xn_done", "base_done"))
        xnt_ps, xnt_hi_done, xnt_lo_done, lg_ps, z_done, ex_done, chosen_done, pos_ps, pos_used, route_done, wsel_done = (
            sem(n) for n in ("xnt_ps", "xnt_hi_done", "xnt_lo_done", "lg_ps", "z_done", "ex_done", "chosen_done", "pos_ps", "pos_used", "route_done", "wsel_done"))
        ld_e = [sem(f"ld_e{i}") for i in range(HALF)]
        ld_xe = [sem(f"ld_xe{i}") for i in range(HALF)]
        st_y = [sem("st_y0"), sem("st_y1")]
        xe_ps, xe_done, gu_ps, sgl_done, hh_done, hh_ps, hht_done, ye_ps, ye_done = (
            sem(n) for n in ("xe_ps", "xe_done", "gu_ps", "sgl_done", "hh_done", "hh_ps", "hht_done", "ye_ps", "ye_done"))
        ld_sw, ld_swd, ld_gb = sem("ld_sw"), sem("ld_swd"), sem("ld_gb")
        ld_xs = sem("ld_xs")
        ld_bas = [sem("ld_bas0"), sem("ld_bas1")]
        ld_gat = [sem(f"ld_gat{t}") for t in range(TT)]
        st_out = [sem("st_out0"), sem("st_out1")]
        sw_hi_done, sw_lo_done, sh_ps, sg2_done, hs_done, dn_ps, shrow_done, acc_done, fin_done, acc_own = (
            sem(n) for n in ("sw_hi_done", "sw_lo_done", "sh_ps", "sg2_done", "hs_done", "dn_ps", "shrow_done", "acc_done", "fin_done", "acc_own"))

        def met(eng):
            eng.sem_inc(waits_met, 1)

        class Chain:

            def __init__(self, eng, own, base=0):
                self.eng, self.own, self.base, self.n = eng, own, base, 0

            def __call__(self, ins, plain=False):
                ins.then_inc(self.own, 1)
                self.n += 1
                self.eng.wait_ge(self.own, self.base + self.n)
                if plain:
                    met(self.eng)

        DVE_PRE, DVE_ROUND = 12, 27
        ACT_PRE, ACT_ROUND = 1, 3
        POOL_ROUND = 4
        W_ORDER = (4, 0, 6, 1, 5, 2, 7, 3)
        WC = QKV // 8
        W_FIRST = 3

        def w_chunks(m):
            g = m // 4
            head = (NH + g, 2 * g, NH + NKV + g, 2 * g + 1)[m % 4]
            return W_ORDER.index(head * HD // WC) + 1

        def x_pair(p):
            return x[bass.ds(p * TOK, TOK), :].rearrange("(t p) h -> p t h", p=PN)

        def rows(ap, row):
            return ap[bass.ds(row, PN), :]

        def both(ap):
            return ap.unsqueeze(1).broadcast_to([PN, 2, S])

        def pair3(ap):
            return ap.rearrange("p (b s) -> p b s", b=2)

        def rope_buffer(m):
            g, r = m // 4, m % 4
            return kr[:, :] if r == 0 else qr[:, 0 if r == 1 else 1, g % 2, :]

        def later(n):
            return not isinstance(n, int) or n > 0

        block = ctx.enter_context(nc.Block())

        @block.sync
        def _(sp):
            sp.dma_start(c_sb[:, :], c_in).then_inc(ld_c, 16)
            sp.dma_start(ident[:, :], ident_t).then_inc(ld_ident, 16)
            sp.dma_start(xin[:, :, :], x_pair(0)).then_inc(ld_xin, 16)
            wm_src = wmod.rearrange("(c p) n -> p c n", p=PN)
            sp.dma_start(wm[:, :, 0:2 * H], wm_src[:, :, 0:2 * H]).then_inc(ld_wm, 16)

            def w_load(j):
                sp.dma_start(wraw[:, :, j * WC:(j + 1) * WC],
                             w_pack.rearrange("(c p) n -> p c n", p=PN)[:, :, j * WC:(j + 1) * WC]).then_inc(ld_w[j], 16)

            for j in W_ORDER[:W_FIRST]:
                w_load(j)
            sp.dma_start(wm[:, :, 2 * H:6 * H], wm_src[:, :, 2 * H:6 * H]).then_inc(ld_wmr, 16)
            for j in W_ORDER[W_FIRST:]:
                w_load(j)
            sp.dma_start(wo[:, :, :], w_o.rearrange("(n p) h -> p n h", p=PN)).then_inc(ld_wo, 16)
            sp.wait_ge(fills, 2)
            sp.dma_start(wr[:, :, 0:E], w_router.rearrange("(c p) e -> p c e", p=PN)).then_inc(ld_wr, 16)
            sp.dma_start(wr[:, :, E:E + 1], w_sgate.rearrange("(c p) e -> p c e", p=PN), allow_slow_non_contiguous=True).then_inc(ld_wr, 16)
            sp.dma_start(slots_d.rearrange("(a p) h -> p a h", p=PN),
                         eq[:, 0:2, :, :].rearrange("p t k e -> p (t k e)").unsqueeze(1).broadcast_to([PN, E, H])).then_inc(st_zero, 16)
            sp.wait_ge(mod_done, 1)
            sp.dma_start(mod_d, mod[:, :]).then_inc(st_mod, 16)
            sp.wait_ge(st_mod, 16)

            def pair_loads(p):
                if later(p):
                    sp.wait_ge(base_done, 2 * p)
                for b in range(2):
                    sp.dma_start(bcm[:, b, :], mod_d[bass.ds(2 * p + b, 1), :].rearrange("a n -> (a n)")
                                 .partition_broadcast(PN)).then_inc(ld_bcm, 16)
                sp.dma_start(xres[:, :, :], x_pair(p)).then_inc(ld_xres, 16)

            def pair_stores(p):
                sp.wait_ge(base_done, 2 * p + 2)
                sp.dma_start(base_d[bass.ds(p * TOK, TOK), :].rearrange("(t p) h -> p t h", p=PN), h2[:, :, :]).then_inc(st_base, 16)
                sp.wait_ge(xnt_hi_done, 2 * p + 2)
                sp.wait_ge(xnt_lo_done, 2 * p + 2)
                for part, src in ((0, xnT_hi), (1, xnT_lo)):
                    sp.dma_start(xnt_d[bass.ds(p, 1), :, part, :, :].rearrange("a p c s -> (a p) c s"),
                                 src[:, :, :].bitcast(F32)).then_inc(st_xnt, 16)

            def next_x(p):
                sp.wait_ge(ht_ps, p)
                sp.dma_start(xin[:, :, :], x_pair(p)).then_inc(ld_xin, 16)

            pair_loads(0)
            next_x(1)
            with sp.Fori(0, NPAIR - 2) as p:
                next_x(p + 2)
                pair_stores(p)
                pair_loads(p + 1)
            pair_stores(NPAIR - 2)
            pair_loads(NPAIR - 1)

            def expert_weights(e, i):
                two = slice(2 * i, 2 * i + 2)
                for dst, src in ((wgu[:, two, :, 0:F], w_gate), (wgu[:, two, :, F:2 * F], w_up)):
                    sp.dma_start(dst.rearrange("p e c f -> p (e c) f"),
                                 src[bass.ds(e, 2), :, :].rearrange("a (c p) f -> p (a c) f", p=PN)).then_inc(ld_e[i], 16)
                sp.dma_start(wd[:, two, :, :].rearrange("p e c h -> p (e c) h"),
                             w_down[bass.ds(e, 2), :, :].rearrange("a (c p) h -> p (a c) h", p=FH)).then_inc(ld_e[i], 16)

            sp.wait_ge(pj_ps, UNITS * NPAIR)
            for n, src in enumerate((sw_gate, sw_up)):
                sp.dma_start(swraw[:, :, n * FS:(n + 1) * FS], src.rearrange("(c p) f -> p c f", p=PN)).then_inc(ld_sw, 16)
            sp.wait_ge(st_xnt, 32 * LAST + FREE)
            for dst, part in ((xs_hi, 0), (xs_lo, 1)):
                sp.dma_start(dst[:, :, :].bitcast(F32), xnt_d[0, :, part, :, :]).then_inc(ld_xs, 16)
            for i in range(HALF):
                expert_weights(2 * i, i)
            sp.wait_ge(y_ps, TT * NPAIR)
            sp.dma_start(swd[:, 0:FT - 1, :], sw_down[0:(FT - 1) * PN, :].rearrange("(t p) h -> p t h", p=PN)).then_inc(ld_swd, 16)
            sp.dma_start(swd[0:FS - (FT - 1) * PN, FT - 1, :], sw_down[(FT - 1) * PN:FS, :]).then_inc(ld_swd, 16)
            pair_stores(NPAIR - 1)

            def slot_rows(e, i):
                sp.dma_start(xe[:, 2 * i:2 * i + 2, :], slots_d[bass.ds(e * CAP, 2 * CAP), :].rearrange("(a p) h -> p a h", p=PN))\
                  .then_inc(ld_xe[i], 16)

            sp.wait_ge(st_base, 16 * NPAIR + FREE)
            sp.wait_ge(st_scat, 16 * (NPAIR + 1) * TT * TOPK)
            for i in range(HALF):
                slot_rows(2 * i, i)
            sp.dma_start(gball[:, :, :], mod_d[:, 3 * H:4 * H].partition_broadcast(PN)).then_inc(ld_gb, 16)

            def residual(tile, par):
                sp.dma_start(bas[:, par, :], rows(base_d, tile * PN)).then_inc(ld_bas[par], 16)

            for j in range(2):
                residual(j, j)
            with sp.Fori(1, E // RING) as r:
                for i in range(HALF):
                    sp.wait_ge(ye_ps, RING * r + (2 * i + 2 - RING))
                    slot_rows(RING * r + 2 * i, i)
                    expert_weights(RING * r + 2 * i, i)

            for tile in range(NPAIR * TT):
                sp.wait_ge(fin_done, tile + 1)
                sp.dma_start(rows(out, tile * PN), fin[:, tile % 2, :]).then_inc(st_out[tile % 2], 16)
                if tile + 2 < NPAIR * TT:
                    residual(tile + 2, tile % 2)
            for par in range(2):
                sp.wait_ge(st_out[par], 16 * NPAIR * TT // 2 + FREE)

        @block.scalar
        def _(act):
            act.dma_start(cosT[:, :], cos_t).then_inc(ld_const, 16)
            act.dma_start(sinT[:, :], sin_t).then_inc(ld_const, 16)
            act.wait_ge(ld_c, 16)
            act.activation(sc[:, :], c_sb[:, :], ACT.Silu).then_inc(silu_done, 1)
            for dst, src in ((mask[:, :], mask_t), (tri[:, :], tri_t),
                             (ebase[:, :], ebase_t), (wnorm[:, :], w_norm.partition_broadcast(PN)),
                             (cwk[:, :], conv_k.rearrange("g t -> (g t)").partition_broadcast(PN)),
                             (cwv[:, :], conv_v.rearrange("g t -> (g t)").partition_broadcast(PN))):
                act.dma_start(dst, src).then_inc(ld_const, 16)

            def prepare_norm(p):
                act.wait_ge(var1, 2 * p + 2)
                act.activation(std1[:, 0, :], mv1[:, :, 1], ACT.Sqrt, bias=LN_EPS).then_inc(std1_done, 1)

            def prepare_h(p, own):
                act.wait_ge(ht_ps, p + 1)
                act.wait_ge(modt_done, 1)
                if later(p):
                    act.wait_ge(rope_done, ROPES * p)
                for c in range(HC):
                    for b in range(2):
                        last = act.activation(qsw[:, c, b * S:(b + 1) * S], PT[c][:, b * S:(b + 1) * S], ACT.Identity,
                                              scale=modT[:, 2 + c, bass.ds(2 * p + b, 1)],
                                              bias=modT[:, c, bass.ds(2 * p + b, 1)])
                own(last)
                if later(p):
                    act.wait_ge(pj_ps, UNITS * p)
                act.activation(hT_hi[:, :, :], qsw[:, :, :], ACT.Copy).then_inc(h_hi_done, 1)

            def project(p, m):
                g, r = m // 4, m % 4
                bank = PJ[m % 2]
                act.wait_ge(pj_ps, UNITS * p + (m + 1))
                if r == 2:
                    if m >= 4 or later(p):
                        act.wait_ge(pj_dve, UNITS * p + (m - 3))
                    act.activation(v0[:, :, 1:S + 1], pair3(bank[:, :]), ACT.Copy,
                                   scale=cwv[:, 2 * g:2 * g + 1]).then_inc(pj_act, 1)
                    return
                rope = 3 * g + ROPE_OF[r]
                if rope >= 2 or later(p):
                    act.wait_ge(rope_done, ROPES * p + (rope - 1))
                half = HD // 2
                act.activation(qsw[0:half, rope % 2, :], bank[half:HD, :], ACT.Copy)
                act.activation(qsw[half:HD, rope % 2, :], bank[0:half, :], ACT.Copy).then_inc(pj_act, 1)

            def k_tap(p, g):
                if g >= 1 or later(p):
                    act.wait_ge(kc_done, GROUPS * p + g)
                act.wait_ge(rope_done, ROPES * p + (3 * g + 1))
                act.activation(k0[:, :, 1:S + 1], pair3(kr[:, :]), ACT.Copy,
                               scale=cwk[:, 2 * g:2 * g + 1]).then_inc(k0_done, 1)

            def exps_of(p, n):
                act.wait_ge(sneg_done, UNITS * p + (n + 1))
                if n >= 3:
                    act.wait_ge(pt_ps, UNITS * p + (n - 2))
                for j, (a, z) in enumerate(((0, PN), (PN, 3 * PN))):
                    last = act.activation(prob[:, n % 3, a:z], sneg[:, n % 2, a:z], ACT.Exp, scale=-1.0,
                                          bias=nmax[:, n % 4, j:j + 1], accum_out=rsum[:, n % 4, j:j + 1])
                last.then_inc(exp_done, 1)

            def v_rows(p, g):
                act.wait_ge(vt_ps, GROUPS * p + (g + 1))
                act.activation(vN[:, g % 2, :], XB[:, :], ACT.Copy).then_inc(vn_done, 1)

            def head_out(p, n):
                g, h, b = n // 4, (n % 4) // 2, n % 2
                act.wait_ge(pv_ps, UNITS * p + (n + 1))
                if n == 0 and later(p):
                    act.wait_ge(y_ps, TT * p)
                act.activation(oT[:, 2 * g + h, b * S:(b + 1) * S], OB[:, (n % 2) * S:(n % 2 + 1) * S],
                               ACT.Copy).then_inc(ot_done, 1)

            def slot(p, n):
                m = n + 4
                if m < UNITS:
                    if m % 4 == 2:
                        k_tap(p, m // 4)
                    project(p, m)
                if n < UNITS:
                    exps_of(p, n)
                    if n % 4 == 0:
                        v_rows(p, n // 4)
                if n >= PV_LAG:
                    head_out(p, n - PV_LAG)

            def first_group(p):
                project(p, 0)
                project(p, 1)
                k_tap(p, 0)
                project(p, 2)
                project(p, 3)

            def w_high(n):
                j = W_ORDER[n]
                act.wait_ge(ld_w[j], 16)
                act.activation(w_hi[:, :, j * WC:(j + 1) * WC], wraw[:, :, j * WC:(j + 1) * WC], ACT.Copy).then_inc(w_hi_done, 1)

            prepare_norm(0)
            w_high(0)
            own = Chain(act, act_own)
            prepare_h(0, own)
            assert own.n == ACT_PRE
            for n in range(1, W_FIRST):
                w_high(n)
            act.wait_ge(mod_ps, 1)
            for j in range(2):
                last = act.activation(mod[:, j * 2 * H:(j + 1) * 2 * H], SC[j][0:B, :], ACT.Copy)
            last.then_inc(rows_done, 1)
            act.wait_ge(ld_const, 128)
            act.wait_ge(fills, 4)
            first_group(0)

            def late_units(p):
                for n in range(EARLY, UNITS + PV_LAG):
                    slot(p, n)
                    if n == EARLY + 1 and p is not LAST:
                        prepare_norm(p + 1)

            def post_std(p, b):
                act.wait_ge(var2, 2 * p + (b + 1))
                act.activation(std2[:, 0, 2 * b:2 * b + 2], mv2[:, 2 * b:2 * b + 2, 1], ACT.Sqrt, bias=LN_EPS).then_inc(std2_done, 1)

            def post_rms(p, b, own):
                act.wait_ge(h2_done, 2 * p + (b + 1))
                act.wait_ge(st_scat, 16 * TT * TOPK * (p + 1))
                for t in range(2 * b, 2 * b + 2):
                    last = act.activation(xn[:, t, :], h2[:, t, :], ACT.Square, accum_out=rms[:, 0, t:t + 1])
                own(last)
                act.activation(rms[:, 1, 2 * b:2 * b + 2], rms[:, 0, 2 * b:2 * b + 2], ACT.Sqrt, scale=1.0 / H, bias=RMS_EPS)\
                   .then_inc(rms_done, 1)

            def post_xnt(p, b):
                act.wait_ge(xnt_ps, 2 * p + (b + 1))
                if b == 0:
                    act.wait_ge(st_xnt, 32 * p + FREE)
                    act.wait_ge(lg_ps, p + FREE)
                act.activation(xnT_hi[:, :, b * S:(b + 1) * S], XB[:, :].rearrange("p (c s) -> p c s", c=HC), ACT.Copy)\
                   .then_inc(xnt_hi_done, 1)

            def post_exp(p):
                act.wait_ge(z_done, p + 1)
                act.activation(red[:, 2, :], XB[:, 0:TT * LCOL].rearrange("p (t c) -> p t c", c=LCOL)[:, :, E], ACT.Exp, scale=-1.0)
                act.activation(ex[:, :, :], zz[:, :, 0:E], ACT.Exp).then_inc(ex_done, 1)

            for n in range(EARLY):
                slot(0, n)
                if n % 2 == 0 and W_FIRST + n // 2 < 8:
                    w_high(W_FIRST + n // 2)
                if n == 10:
                    act.wait_ge(ld_wr, 32)
                    act.activation(wr_hi[:, :, :], wr[:, :, :], ACT.Copy).then_inc(wr_hi_done, 1)
            with act.Fori(0, LAST) as p:
                own = Chain(act, act_own, ACT_PRE + ACT_ROUND * p)
                late_units(p)
                prepare_h(p + 1, own)
                first_group(p + 1)
                for n in range(EARLY):
                    slot(p + 1, n)
                    if n == 3:
                        post_std(p, 0)
                        post_std(p, 1)
                    if n == 10:
                        post_rms(p, 0, own)
                        post_rms(p, 1, own)
                    if n in (13, 15):
                        post_xnt(p, (n - 13) // 2)
                    if n == 18:
                        post_exp(p)
                assert own.n == ACT_ROUND, own.n
            own = Chain(act, act_own, ACT_PRE + ACT_ROUND * LAST)
            late_units(LAST)

            def shared_inputs(q):
                for dst, part in ((xs_hi, 0), (xs_lo, 1)):
                    act.dma_start(dst[:, :, :].bitcast(F32), xnt_d[bass.ds(q, 1), :, part, :, :].rearrange("a p c s -> (a p) c s"))\
                       .then_inc(ld_xs, 16)

            def silu_of(q, f):
                fw = min(PN, FS - f * PN)
                act.wait_ge(sh_ps, FT * q + (f + 1))
                if f >= 2 or later(q):
                    act.wait_ge(hs_done, FT * q + (f - 1))
                act.activation(sg2[0:fw, f % 2, :], PJ[f % 2][0:fw, :], ACT.Silu).then_inc(sg2_done, 1)

            def shared_rows(q):
                for t in range(TT):
                    act.wait_ge(dn_ps, TT * q + (t + 1))
                    act.activation(shrow[:, bass.ds(TT * q + t, 1), :].rearrange("p a h -> p (a h)"), DN[t % 2][:, 0:H],
                                   ACT.Copy, scale=sgate[:, bass.ds(q, 1), t:t + 1].rearrange("p a t -> p (a t)"))\
                       .then_inc(shrow_done, 1)

            act.wait_ge(ld_sw, 32)
            act.activation(sw_hi[:, :, :], swraw[:, :, :], ACT.Copy).then_inc(sw_hi_done, 1)
            def expert_slot(base, n, lo=0, hi=10 ** 9):
                if lo <= n - 1 < hi:
                    act.wait_ge(gu_ps, base + n)
                    if n - 1 >= 2 or later(base):
                        act.wait_ge(hh_done, base + (n - 2))
                    act.activation(sgl[:, (n - 1) % 2, :], SC[(n - 1) % 2][:, 0:F], ACT.Silu).then_inc(sgl_done, 1)
                if lo <= n - 2 < hi:
                    act.wait_ge(hh_ps, base + (n - 1))
                    if n - 2 >= 2 or later(base):
                        act.wait_ge(ye_ps, base + (n - 3))
                    act.activation(hhT[:, (n - 2) % 2, :], PT[(n - 2) % 2][0:FH, 0:2 * PN], ACT.Copy).then_inc(hht_done, 1)
                if lo <= n - 3 < hi and n % 2 == 0:
                    pair = (n - 4) // 2
                    act.wait_ge(ye_done, base + (n - 2))
                    act.dma_start(y_d[bass.ds((base + (n - 4)) * CAP, 2 * CAP), :].rearrange("(a p) h -> p a h", p=PN),
                                  ye[:, 2 * (pair % 2):2 * (pair % 2) + 2, :]).then_inc(st_y[pair % 2], 16)

            post_std(LAST, 0)
            post_rms(LAST, 0, own)
            post_xnt(LAST, 0)
            post_std(LAST, 1)
            silu_of(0, 0)
            silu_of(0, 1)
            post_rms(LAST, 1, own)
            silu_of(0, 2)
            post_xnt(LAST, 1)
            silu_of(0, 3)
            post_exp(LAST)
            silu_of(0, 4)
            silu_of(0, 5)
            shared_inputs(1)
            shared_rows(0)
            for f in range(F_EARLY):
                silu_of(1, f)
            for n in range(RING):
                expert_slot(0, n)
            with act.Fori(1, E // RING) as r:
                for n in range(RING):
                    expert_slot(RING * r, n, lo=-RING)
            for n in range(4):
                expert_slot(E, n, lo=-RING, hi=0)
            for f in range(F_EARLY, FT):
                silu_of(1, f)
            act.wait_ge(st_xnt, 32 * NPAIR + FREE)
            with act.Fori(1, LAST) as q:
                shared_inputs(q + 1)
                shared_rows(q)
                for f in range(FT):
                    silu_of(q + 1, f)
            shared_rows(LAST)

        @block.gpsimd
        def _(pool):
            for start in (route_done, lg_ps, st_xnt, st_base, st_out[0], st_out[1]):
                pool.sem_inc(start, FREE)
            pool.memset(eq[:, :, :, :], 0.0).then_inc(fills, 1)
            pool.memset(wr[:, :, :], 0.0).then_inc(fills, 1)
            pool.memset(k0[:, :, 0:1], 0.0).then_inc(fills, 1)
            pool.memset(v0[:, :, 0:1], 0.0).then_inc(fills, 1)
            pool.memset(ones[:, :], 1.0).then_inc(fills, 1)
            pool.memset(carry[:, :, :], 0.0).then_inc(fills, 1)

            def rope(p, m):
                g, r = m // 4, m % 4
                if r == 2:
                    return
                n = 3 * g + ROPE_OF[r]
                pool.wait_ge(pj_act, UNITS * p + (m + 1))
                pool.tensor_tensor(pair3(qsw[:, n % 2, :]), pair3(qsw[:, n % 2, :]), both(sinT[:, :]),
                                   ALU.mult).then_inc(t2_done, 1)
                pool.wait_ge(t2_done, ROPES * p + (n + 1))
                pool.wait_ge(pj_dve, UNITS * p + (m + 1))
                pool.tensor_tensor(rope_buffer(m), rope_buffer(m), qsw[:, n % 2, :], ALU.add).then_inc(rope_done, 1)

            def scatter(c):
                pool.indirect_dma_start(out=slots_d, out_offset=bass.IndirectOffsetOnAxis(ap=sidx[:, c:c + 1], axis=0),
                                        in_=xn[:, c // TOPK, :], in_offset=None, bounds_check=E * CAP - 1,
                                        oob_is_err=False).then_inc(st_scat, 16)

            pool.wait_ge(ld_const, 128)
            for m in range(4):
                rope(0, m)
            def post_x1(p, b):
                t = slice(2 * b, 2 * b + 2)
                pool.wait_ge(yg_done, 2 * p + (b + 1))
                pool.tensor_tensor(xres[:, t, :], xres[:, t, :], yg[:, b, :, :], ALU.add).then_inc(x1_done, 1)

            def of_rows(b, part):
                return bcm[:, b, part * H:(part + 1) * H].unsqueeze(1).broadcast_to([PN, 2, H])

            def post_h2(p, b, step, own):
                h = h2[:, 2 * b:2 * b + 2, :]
                if step == 0:
                    pool.wait_ge(xh2_done, 2 * p + (b + 1))
                    own(pool.tensor_tensor(h, h, of_rows(b, 2), ALU.mult))
                else:
                    pool.tensor_tensor(h, h, of_rows(b, 1), ALU.add).then_inc(h2_done, 1)

            def post_base(p, b, step, own):
                h = h2[:, 2 * b:2 * b + 2, :]
                if step == 0:
                    pool.wait_ge(xn_done, 2 * p + (b + 1))
                    own(pool.tensor_tensor(h, h, of_rows(b, 3), ALU.mult))
                else:
                    pool.tensor_tensor(h, h, xres[:, 2 * b:2 * b + 2, :], ALU.add).then_inc(base_done, 1)

            def late_units(p):
                for n in range(EARLY, UNITS):
                    if n + 4 < UNITS:
                        rope(p, n + 4)
                    if n == EARLY:
                        pool.wait_ge(route_done, p + FREE)
                        met(pool)
                    scatter(n - EARLY)
                for c in range(UNITS - EARLY, TT * TOPK):
                    scatter(c)

            for n in range(EARLY):
                rope(0, n + 4)
            pool.wait_ge(modt_done, 1)
            pool.wait_ge(st_mod, 16)
            pool.memset(sidx[:, :], SKIP).then_inc(fills, 1)
            pool.memset(xn[:, :, :], 0.0).then_inc(fills, 1)
            pool.wait_ge(fills, 8)
            pool.wait_ge(st_zero, 16)
            with pool.Fori(0, LAST) as p:
                own = Chain(pool, pool_own, POOL_ROUND * p)
                late_units(p)
                rope(p + 1, 0)
                rope(p + 1, 1)
                pool.wait_ge(ld_xres, 16 * (p + 1))
                post_x1(p, 0)
                rope(p + 1, 3)
                post_x1(p, 1)
                for n in range(EARLY):
                    rope(p + 1, n + 4)
                    if 5 <= n < 9:
                        post_h2(p, (n - 5) // 2, (n - 5) % 2, own)
                    if 13 <= n < 17:
                        post_base(p, (n - 13) // 2, (n - 13) % 2, own)
                assert own.n == POOL_ROUND, own.n
            own = Chain(pool, pool_own, POOL_ROUND * LAST)
            late_units(LAST)
            pool.wait_ge(ld_xres, 16 * NPAIR)
            for b in range(2):
                post_x1(LAST, b)
                post_h2(LAST, b, 0, own)
                post_h2(LAST, b, 1, own)
            for n in range(4):
                post_base(LAST, n // 2, n % 2, own)
            pool.wait_ge(route_done, NPAIR + FREE)
            for c in range(TT * TOPK):
                scatter(c)

            for par in range(2):
                pool.wait_ge(st_y[par], 16 * E // 4)
            for q in range(NPAIR):
                for t in range(TT):
                    if q >= 1:
                        pool.wait_ge(acc_done, TT * (q - 1) + (t + 1))
                    for c in range(t * TOPK, (t + 1) * TOPK):
                        pool.indirect_dma_start(out=gat[:, t, c % TOPK, :], out_offset=None, in_=y_d,
                                                in_offset=bass.IndirectOffsetOnAxis(ap=gidx[:, q, c:c + 1], axis=0))\
                            .then_inc(ld_gat[t], 16)

        @block.vector
        def _(dve):
            pre = Chain(dve, dve_own)
            dve.wait_ge(sct_ps, 1)
            dve.tensor_copy(scT[:, :, :], PT[0][:, 0:HC * B].rearrange("p (c b) -> p c b", b=B)).then_inc(sct_done, 1)

            def mod_features():
                dve.wait_ge(modt_ps, 1)
                by_k = PT[1][:, 0:4 * B].rearrange("p (k b) -> p k b", b=B)
                dve.tensor_copy(modT[:, 0:2, :], by_k[:, 0:2, :])
                dve.tensor_scalar(modT[:, 2:4, :], by_k[:, 2:4, :], 1.0, None, ALU.add).then_inc(modt_done, 1)

            def bounded_gate(part):
                gate = mod[:, part * H:(part + 1) * H]
                pre(dve.scalar_tensor_tensor(gabs[:, :], gate, -1.0, gate, ALU.mult, ALU.max))
                pre(dve.tensor_scalar(gabs[:, :], gabs[:, :], 0.25, None, ALU.max))
                pre(dve.tensor_scalar(gsgn[:, :], gate, 0.0, 2.0, ALU.is_ge, ALU.mult))
                pre(dve.scalar_tensor_tensor(gate, gsgn[:, :], -1.0, gabs[:, :], ALU.add, ALU.mult))

            def prepare_stats(p, b, own):
                if b == 0:
                    dve.wait_ge(ld_xin, 16 * (p + 1))
                for t in range(2 * b, 2 * b + 2):
                    last = dve.bn_stats(st1[:, t, :], xin[:, t, :])
                own(last, plain=True)
                for t in range(2 * b, 2 * b + 2):
                    last = dve.bn_aggr(mv1[:, t, :], st1[:, t, :])
                last.then_inc(var1, 1)

            def prepare_norm(p, b, own):
                if b == 0:
                    dve.wait_ge(std1_done, p + 1)
                    own(dve.reciprocal(std1[:, 1, :], std1[:, 0, :]))
                for t in range(2 * b, 2 * b + 2):
                    last = dve.tensor_scalar(xin[:, t, :], xin[:, t, :], mv1[:, t, 0:1], std1[:, 1, t:t + 1],
                                             ALU.subtract, ALU.mult)
                last.then_inc(xhat_done, 1)

            def prepare_lo(p):
                dve.wait_ge(h_hi_done, p + 1)
                dve.tensor_tensor(hT_lo[:, :, :], qsw[:, :, :], hT_hi[:, :, :].bitcast(F32), ALU.subtract).then_inc(h_lo_done, 1)

            def project(p, m):
                g, r = m // 4, m % 4
                dve.wait_ge(pj_act, UNITS * p + (m + 1))
                if r == 2:
                    if g >= 1 or later(p):
                        dve.wait_ge(vt_ps, GROUPS * p + g)
                    dve.scalar_tensor_tensor(pair3(vT[:, :]), pair3(PJ[m % 2][:, :]), cwv[:, 2 * g + 1:2 * g + 2],
                                             v0[:, :, 0:S], ALU.mult, ALU.add).then_inc(pj_dve, 1)
                    return
                dve.tensor_tensor(pair3(rope_buffer(m)), pair3(PJ[m % 2][:, :]), both(cosT[:, :]), ALU.mult).then_inc(pj_dve, 1)

            def k_conv(p, g):
                dve.wait_ge(k0_done, GROUPS * p + (g + 1))
                dve.scalar_tensor_tensor(pair3(kc[:, g % 2, :]), pair3(kr[:, :]), cwk[:, 2 * g + 1:2 * g + 2],
                                         k0[:, :, 0:S], ALU.mult, ALU.add).then_inc(kc_done, 1)

            def first_group(p):
                project(p, 0)
                project(p, 1)
                project(p, 2)
                k_conv(p, 0)
                project(p, 3)

            def scores(p, n):
                dve.wait_ge(sc_ps, UNITS * p + (n + 1))
                if n >= 2:
                    dve.wait_ge(exp_done, UNITS * p + (n - 1))
                met(dve)
                for j, (a, z) in enumerate(((0, PN), (PN, 3 * PN))):
                    last = dve.tensor_tensor_reduce(out=sneg[:, n % 2, a:z], in0=SC[n % 2][:, a:z], in1=mask[:, a:z],
                                                    scale=-float(HD) ** -0.5, scalar=3.4e38, op0=ALU.add, op1=ALU.min,
                                                    accum_out=nmax[:, n % 4, j:j + 1])
                last.then_inc(sneg_done, 1)

            def normalise(p, n):
                dve.wait_ge(exp_done, UNITS * p + (n + 1))
                dve.reciprocal(rinv[:, n % 4, :], rsum[:, n % 4, :]).then_inc(rinv_done, 1)
                dve.wait_ge(rinv_done, UNITS * p + (n + 1))
                for j, (a, z) in enumerate(((0, PN), (PN, 3 * PN))):
                    last = dve.tensor_scalar(prob[:, n % 3, a:z], prob[:, n % 3, a:z], rinv[:, n % 4, j:j + 1], None, ALU.mult)
                last.then_inc(norm_done, 1)

            def transposed(p, n):
                dve.wait_ge(pt_ps, UNITS * p + (n + 1))
                if n >= 2:
                    dve.wait_ge(pv_ps, UNITS * p + (n - 1))
                dve.tensor_copy(pT[:, n % 2, :], PT[n % 2][:, 0:3 * PN]).then_inc(pt_done, 1)

            def slot(p, n):
                m = n + 4
                if n < UNITS:
                    scores(p, n)
                if 0 < n <= UNITS:
                    normalise(p, n - 1)
                if m < UNITS:
                    project(p, m)
                if m < UNITS and m % 4 == 2:
                    k_conv(p, m // 4)
                if T_LAG <= n < UNITS + T_LAG:
                    transposed(p, n - T_LAG)

            def w_low(n):
                j = W_ORDER[n]
                dve.wait_ge(w_hi_done, n + 1)
                dve.tensor_tensor(w_lo[:, :, j * WC:(j + 1) * WC], wraw[:, :, j * WC:(j + 1) * WC],
                                  w_hi[:, :, j * WC:(j + 1) * WC].bitcast(F32), ALU.subtract).then_inc(w_lo_done, 1)

            for b in range(2):
                prepare_stats(0, b, pre)
            mod_features()
            for b in range(2):
                prepare_norm(0, b, pre)
            w_low(0)
            prepare_lo(0)
            for n in range(1, W_FIRST):
                w_low(n)
            dve.wait_ge(fills, 6)
            dve.wait_ge(ld_const, 128)
            first_group(0)

            def late_units(p, own):
                for n in range(EARLY, UNITS + T_LAG):
                    slot(p, n)
                    if n in (EARLY, EARLY + 1) and p is not LAST:
                        prepare_stats(p + 1, n - EARLY, own)
                    if n in (EARLY + 2, EARLY + 3) and p is not LAST:
                        prepare_norm(p + 1, n - (EARLY + 2), own)

            def post_gate(p, b):
                if b == 0:
                    dve.wait_ge(ld_bcm, 32 * (p + 1))
                dve.wait_ge(y_ps, TT * p + (2 * b + 2))
                dve.tensor_tensor(yg[:, b, :, :], SC[b][:, :].rearrange("p (t h) -> p t h", h=H),
                                  bcm[:, b, 0:H].unsqueeze(1).broadcast_to([PN, 2, H]), ALU.mult).then_inc(yg_done, 1)

            def post_stats(p, b, own):
                dve.wait_ge(x1_done, 2 * p + (b + 1))
                for t in range(2 * b, 2 * b + 2):
                    last = dve.bn_stats(st2[:, t, :], xres[:, t, :])
                own(last, plain=True)
                for t in range(2 * b, 2 * b + 2):
                    last = dve.bn_aggr(mv2[:, t, :], st2[:, t, :])
                last.then_inc(var2, 1)

            def post_xhat(p, b, own):
                dve.wait_ge(std2_done, 2 * p + (b + 1))
                own(dve.reciprocal(std2[:, 1, 2 * b:2 * b + 2], std2[:, 0, 2 * b:2 * b + 2]))
                dve.wait_ge(st_base, 16 * p + FREE)
                for t in range(2 * b, 2 * b + 2):
                    last = dve.tensor_scalar(h2[:, t, :], xres[:, t, :], mv2[:, t, 0:1], std2[:, 1, t:t + 1],
                                             ALU.subtract, ALU.mult)
                last.then_inc(xh2_done, 1)

            def post_xn(p, b, own):
                dve.wait_ge(rms_done, 2 * p + (b + 1))
                own(dve.reciprocal(rms[:, 2, 2 * b:2 * b + 2], rms[:, 1, 2 * b:2 * b + 2]))
                for t in range(2 * b, 2 * b + 2):
                    last = dve.scalar_tensor_tensor(xn[:, t, :], h2[:, t, :], rms[:, 2, t:t + 1], wnorm[:, :],
                                                    ALU.mult, ALU.mult)
                last.then_inc(xn_done, 1)

            def post_xnt(p, b):
                dve.wait_ge(xnt_hi_done, 2 * p + (b + 1))
                cols = slice(b * S, (b + 1) * S)
                dve.tensor_tensor(xnT_lo[:, :, cols], XB[:, :].rearrange("p (c s) -> p c s", c=HC),
                                  xnT_hi[:, :, cols].bitcast(F32), ALU.subtract).then_inc(xnt_lo_done, 1)

            def post_logits(p, own):
                logits = XB[:, 0:TT * LCOL].rearrange("p (t c) -> p t c", c=LCOL)[:, :, 0:E]
                dve.wait_ge(lg_ps, p + 1 + FREE)
                own(dve.tensor_reduce(red[:, 0, :], logits, AXX, ALU.max))
                own(dve.tensor_tensor(zz[:, :, 0:E], logits, red[:, 0, :].unsqueeze(2).broadcast_to([PN, TT, E]), ALU.subtract))
                dve.tensor_scalar(zz[:, :, 0:E], zz[:, :, 0:E], PROB_FLOOR, None, ALU.max).then_inc(z_done, 1)

            def post_choice(p, own):
                dve.wait_ge(z_done, p + 1)
                met(dve)
                for t in range(TT):
                    last = dve.max(top8[:, t, :], zz[:, t, :])
                own(last, plain=True)
                for t in range(TT):
                    last = dve.match_replace(zz2[:, t, :], top8[:, t, :], zz[:, t, :], TAKEN)
                own(last)
                dve.tensor_scalar(chosen[:, :, :], zz2[:, :, 0:E], TAKEN / 2, None, ALU.is_lt).then_inc(chosen_done, 1)

            def post_probs(p, own):
                dve.wait_ge(ex_done, p + 1)
                own(dve.tensor_reduce(red[:, 1, :], ex[:, :, :], AXX, ALU.add))
                own(dve.reciprocal(red[:, 3, :], red[:, 1, :]))
                own(dve.tensor_tensor(ex[:, :, :], ex[:, :, :], red[:, 3, :].unsqueeze(2).broadcast_to([PN, TT, E]), ALU.mult))
                own(dve.tensor_scalar(red[:, 2, :], red[:, 2, :], 1.0, None, ALU.add))
                dve.reciprocal(sgate[:, bass.ds(p, 1), :].rearrange("p a t -> p (a t)"), red[:, 2, :])

            def post_slots(p, own):
                dve.wait_ge(pos_ps, p + 1)
                pos = XB[:, 256:256 + TT * E].rearrange("p (t e) -> p t e", e=E)
                own(dve.scalar_tensor_tensor(kept[:, :, :], pos, float(CAP), chosen[:, :, :], ALU.is_lt, ALU.mult))
                dve.tensor_tensor(key[:, :, :], pos, ebase[:, :].unsqueeze(1).broadcast_to([PN, TT, E]), ALU.add).then_inc(pos_used, 1)
                dve.wait_ge(pos_used, p + 1)
                own(dve.tensor_tensor(key[:, :, :], key[:, :, :], kept[:, :, :], ALU.mult), plain=True)

            def post_keys(p, own):
                for t in range(TT):
                    last = dve.max(key8[:, t, :], key[:, t, :])
                own(last)
                own(dve.tensor_scalar(late[:, :, :], key8[:, :, 0:TOPK], 0.0, float(SKIP), ALU.is_equal, ALU.mult))
                dve.scalar_tensor_tensor(sidx[:, :].rearrange("p (t k) -> p t k", k=TOPK), key8[:, :, 0:TOPK], -1.0,
                                         late[:, :, :], ALU.add, ALU.add).then_inc(route_done, 1)
                own(dve.tensor_scalar(gidx[:, bass.ds(p, 1), :].rearrange("p a (t k) -> p (a t) k", k=TOPK),
                                      key8[:, :, 0:TOPK], -1.0, 0.0, ALU.add, ALU.max))

            def post_pick(p, own):
                own(dve.tensor_tensor(ex[:, :, :], ex[:, :, :], kept[:, :, :], ALU.mult))
                own(dve.tensor_tensor(eq[:, :, :, :], key[:, :, :].unsqueeze(2).broadcast_to([PN, TT, TOPK, E]),
                                      key8[:, :, 0:TOPK].unsqueeze(3).broadcast_to([PN, TT, TOPK, E]), ALU.is_equal))

            def post_weights(p, own):
                own(dve.tensor_tensor(eq[:, :, :, :], eq[:, :, :, :],
                                      ex[:, :, :].unsqueeze(2).broadcast_to([PN, TT, TOPK, E]), ALU.mult))
                own(dve.tensor_reduce(wsel[:, bass.ds(p, 1), :].rearrange("p a (t k) -> p (a t) k", k=TOPK),
                                      eq[:, :, :, :], AXX, ALU.add))
                own(dve.tensor_reduce(carry[:, 1, :], chosen[:, :, :].rearrange("p t e -> p e t"), AXX, ALU.add))
                dve.tensor_tensor(carry[:, 0, :], carry[:, 0, :], carry[:, 1, :], ALU.add).then_inc(wsel_done, 1)

            for n in range(EARLY):
                slot(0, n)
                if n % 2 == 1 and W_FIRST + n // 2 < 8:
                    w_low(W_FIRST + n // 2)
                if n == 2:
                    dve.wait_ge(rows_done, 1)
                    bounded_gate(0)
                if n == 4:
                    bounded_gate(3)
                if n == 6:
                    dve.tensor_scalar(mod[:, 2 * H:3 * H], mod[:, 2 * H:3 * H], 1.0, None, ALU.add).then_inc(mod_done, 1)
                if n == 11:
                    dve.wait_ge(wr_hi_done, 1)
                    dve.tensor_tensor(wr_lo[:, :, :], wr[:, :, :], wr_hi[:, :, :].bitcast(F32), ALU.subtract).then_inc(wr_lo_done, 1)
            dve.wait_ge(st_mod, 16)
            pre(dve.memset(zz[:, :, E:E + TOPK], SENTINEL))
            assert pre.n == DVE_PRE, pre.n
            with dve.Fori(0, LAST) as p:
                own = Chain(dve, dve_own, DVE_PRE + DVE_ROUND * p)
                late_units(p, own)
                prepare_lo(p + 1)
                post_gate(p, 0)
                first_group(p + 1)
                post_gate(p, 1)
                for n in range(EARLY):
                    slot(p + 1, n)
                    if n in (1, 2):
                        post_stats(p, n - 1, own)
                    if n in (4, 5):
                        post_xhat(p, n - 4, own)
                    if n in (11, 12):
                        post_xn(p, n - 11, own)
                    if n in (13, 15):
                        post_xnt(p, (n - 13) // 2)
                    if n == 17:
                        post_logits(p, own)
                    if n == 18:
                        post_choice(p, own)
                    if n == 20:
                        post_probs(p, own)
                    if n == 21:
                        post_slots(p, own)
                    if n == 22:
                        post_keys(p, own)
                    if n == 23:
                        post_pick(p, own)
                    if n == 24:
                        post_weights(p, own)
                assert own.n == DVE_ROUND, own.n
            own = Chain(dve, dve_own, DVE_PRE + DVE_ROUND * LAST)
            late_units(LAST, own)
            dve.wait_ge(sw_hi_done, 1)
            dve.tensor_tensor(sw_lo[:, :, :], swraw[:, :, :], sw_hi[:, :, :].bitcast(F32), ALU.subtract)\
               .then_inc(sw_lo_done, 1)

            def hidden(q, f):
                fw = min(PN, FS - f * PN)
                dve.wait_ge(sg2_done, FT * q + (f + 1))
                if f == 0 and later(q):
                    dve.wait_ge(dn_ps, TT * q)
                dve.tensor_tensor(hs[0:fw, f, :], SC[f % 2][0:fw, :], sg2[0:fw, f % 2, :], ALU.mult).then_inc(hs_done, 1)

            post_gate(LAST, 0)
            post_stats(LAST, 0, own)
            post_xhat(LAST, 0, own)
            post_xn(LAST, 0, own)
            post_gate(LAST, 1)
            post_xnt(LAST, 0)
            post_stats(LAST, 1, own)
            post_xhat(LAST, 1, own)
            hidden(0, 0)
            hidden(0, 1)
            post_xn(LAST, 1, own)
            hidden(0, 2)
            post_xnt(LAST, 1)
            hidden(0, 3)
            post_logits(LAST, own)
            post_choice(LAST, own)
            hidden(0, 4)
            post_slots(LAST, own)
            post_keys(LAST, own)
            hidden(0, 5)
            post_probs(LAST, own)
            post_pick(LAST, own)
            post_weights(LAST, own)
            for f in range(F_EARLY):
                hidden(1, f)

            def expert_slot(base, n, lo=0, hi=10 ** 9):
                if lo <= n < hi:
                    dve.wait_ge(xe_ps, base + (n + 1))
                    if n >= 2 or later(base):
                        dve.wait_ge(gu_ps, base + (n - 1))
                    dve.tensor_copy(xeT[:, n % 2, :], PJ[n % 2][:, 0:H]).then_inc(xe_done, 1)
                if lo <= n - 1 < hi:
                    dve.wait_ge(sgl_done, base + n)
                    if n - 1 >= 2 or later(base):
                        dve.wait_ge(hh_ps, base + (n - 2))
                    dve.tensor_tensor(hh[:, (n - 1) % 2, :], SC[(n - 1) % 2][:, F:2 * F], sgl[:, (n - 1) % 2, :],
                                      ALU.mult).then_inc(hh_done, 1)
                if lo <= n - 3 < hi:
                    dve.wait_ge(ye_ps, base + (n - 2))
                    pair = (n - 3) // 2
                    if pair >= 2 or later(base):
                        dve.wait_ge(st_y[pair % 2], 4 * base + 16 * (pair // 2))
                    bk = (OB, XB)[(n - 3) % 2]
                    dve.tensor_copy(ye[:, (n - 3) % 4, :], bk[:, 0:H]).then_inc(ye_done, 1)

            def combine(q, t):
                own = Chain(dve, acc_own, TOPK * (TT * q + t))
                dve.wait_ge(shrow_done, TT * q + (t + 1))
                dve.wait_ge(ld_gat[t], 16 * TOPK * (q + 1))
                before = shrow[:, bass.ds(TT * q + t, 1), :].rearrange("p a h -> p (a h)")
                for k in range(TOPK):
                    own(dve.scalar_tensor_tensor(
                        acc[:, t % 2, :], gat[:, t, k, :],
                        wsel[:, bass.ds(q, 1), t * TOPK + k:t * TOPK + k + 1].rearrange("p a t -> p (a t)"),
                        before, ALU.mult, ALU.add))
                    before = acc[:, t % 2, :]
                dve.wait_ge(st_out[t % 2], 8 * TT * q + 16 * (t // 2) + FREE)
                dve.tensor_tensor(fin[:, t % 2, :], acc[:, t % 2, :],
                                  gball[:, bass.ds(2 * q + t // 2, 1), :].rearrange("p a h -> p (a h)"),
                                  ALU.mult).then_inc(acc_done, 1)
                dve.wait_ge(acc_done, TT * q + (t + 1))
                dve.wait_ge(ld_bas[t % 2], 8 * TT * q + 16 * (t // 2 + 1))
                dve.tensor_tensor(fin[:, t % 2, :], fin[:, t % 2, :], bas[:, t % 2, :], ALU.add).then_inc(fin_done, 1)


            for n in range(RING):
                expert_slot(0, n)
            with dve.Fori(1, E // RING) as r:
                for n in range(RING):
                    expert_slot(RING * r, n, lo=-RING)
            for n in range(3):
                expert_slot(E, n, lo=-RING, hi=0)

            dve.wait_ge(ld_gb, 16)
            for f in range(F_EARLY, FT):
                hidden(1, f)
            for t in range(3):
                combine(0, t)
            hidden(2, 0)
            hidden(2, 1)
            combine(0, 3)
            hidden(2, 2)
            hidden(2, 3)
            combine(1, 0)
            hidden(2, 4)
            hidden(2, 5)
            for t in range(1, TT):
                combine(1, t)
            combine(2, 0)
            for t in range(1, TT):
                hidden(3, 2 * t - 2)
                hidden(3, 2 * t - 1)
                combine(2, t)
            for t in range(TT):
                combine(3, t)

        @block.tensor
        def _(pe):
            def halves(out_ap, pieces, hi_lo):
                (w1, w2), (x1, x2) = hi_lo
                steps = [(c, a, b_) for c in range(pieces) for a, b_ in ((w1, x1), (w1, x2), (w2, x1))]
                for n, (c, a, b_) in enumerate(steps):
                    last = pe.matmul(out_ap, a(c), b_(c), start=(n == 0), stop=(n == len(steps) - 1))
                return last

            pe.wait_ge(silu_done, 1)
            pe.wait_ge(ld_ident, 16)
            for c in range(HC):
                last = pe.transpose(PT[0][:, c * B:(c + 1) * B], sc[:, c * PN:(c + 1) * PN], ident[0:B, 0:B])
            last.then_inc(sct_ps, 1)
            pe.wait_ge(sct_done, 1)
            pe.wait_ge(ld_wm, 16)
            for k in range(4):
                for c in range(HC):
                    last = pe.matmul(PT[1][:, k * B:(k + 1) * B], wm[:, c, k * PN:(k + 1) * PN], scT[:, c, :],
                                     start=(c == 0), stop=(c == HC - 1))
            last.then_inc(modt_ps, 1)
            pe.wait_ge(modt_done, 1)

            def prepare_t(p):
                pe.wait_ge(xhat_done, 2 * p + 2)
                for c in range(HC):
                    for t in range(TT):
                        last = pe.transpose(PT[c][:, t * PN:(t + 1) * PN], xin[:, t, c * PN:(c + 1) * PN], ident[:, :])
                last.then_inc(ht_ps, 1)

            def project(p, m):
                g, r = m // 4, m % 4
                head = {0: NH + g, 1: 2 * g, 2: NH + NKV + g, 3: 2 * g + 1}[r]
                cols = slice(head * HD, (head + 1) * HD)
                if m == 0:
                    pe.wait_ge(h_lo_done, p + 1)
                if m >= 2 or later(p):
                    pe.wait_ge(pj_act, UNITS * p + (m - 1))
                    pe.wait_ge(pj_dve, UNITS * p + (m - 1))
                halves(PJ[m % 2][:, :], HC,
                       ((lambda c: w_hi[:, c, cols], lambda c: w_lo[:, c, cols]),
                        (lambda c: hT_hi[:, c, :], lambda c: hT_lo[:, c, :]))).then_inc(pj_ps, 1)

            def scores(p, n):
                g, h, b = n // 4, (n % 4) // 2, n % 2
                if n < 2 and later(p):
                    pe.wait_ge(yg_done, 2 * p + (n - 1))
                if n >= 2:
                    pe.wait_ge(sneg_done, UNITS * p + (n - 1))
                if n % 4 == 0:
                    pe.wait_ge(kc_done, GROUPS * p + (g + 1))
                if n % 2 == 0:
                    pe.wait_ge(rope_done, ROPES * p + (3 * g + h + 2))
                q = qr[:, h, g % 2, b * S:(b + 1) * S]
                k = kc[:, g % 2, b * S:(b + 1) * S]
                pe.matmul(SC[n % 2][:, 0:PN], q[:, 0:PN], k[:, 0:PN], start=True, stop=True)
                pe.matmul(SC[n % 2][:, PN:3 * PN], q[:, PN:S], k, start=True, stop=True).then_inc(sc_ps, 1)

            def v_transpose(p, g):
                pe.wait_ge(pj_dve, UNITS * p + (4 * g + 3))
                if g >= 1:
                    pe.wait_ge(vn_done, GROUPS * p + g)
                if g == 4 and later(p):
                    pe.wait_ge(xnt_lo_done, 2 * p)
                if g == 5 and later(p):
                    pe.wait_ge(ex_done, p)
                if g == 6 and later(p):
                    pe.wait_ge(pos_used, p)
                for j in range(TT):
                    last = pe.transpose(XB[:, j * PN:(j + 1) * PN], vT[:, j * PN:(j + 1) * PN], ident[:, :])
                last.then_inc(vt_ps, 1)

            def p_transpose(p, n):
                pe.wait_ge(norm_done, UNITS * p + (n + 1))
                if n >= 2:
                    pe.wait_ge(pt_done, UNITS * p + (n - 1))
                for j in range(3):
                    last = pe.transpose(PT[n % 2][:, j * PN:(j + 1) * PN], prob[:, n % 3, j * PN:(j + 1) * PN], ident[:, :])
                last.then_inc(pt_ps, 1)

            def weighted_v(p, n):
                g, b = n // 4, n % 2
                pe.wait_ge(pt_done, UNITS * p + (n + 1))
                if n >= 1:
                    pe.wait_ge(ot_done, UNITS * p + n)
                if n % 4 == 0:
                    pe.wait_ge(vn_done, GROUPS * p + (g + 1))
                o = OB[:, (n % 2) * S:(n % 2 + 1) * S]
                v = vN[:, g % 2, b * S:(b + 1) * S]
                pe.matmul(o, v[:, 0:PN], pT[:, n % 2, 0:S], start=True, stop=False)
                pe.matmul(o[:, PN:S], v[:, PN:S], pT[:, n % 2, S:S + PN], start=False, stop=True).then_inc(pv_ps, 1)

            prepare_t(0)
            pe.wait_ge(ld_wmr, 16)
            for j in range(2):
                for c in range(HC):
                    last = pe.matmul(SC[j][0:B, :], scT[:, c, :], wm[:, c, 2 * H + j * 2 * H:2 * H + (j + 1) * 2 * H],
                                     start=(c == 0), stop=(c == HC - 1))
            last.then_inc(mod_ps, 1)
            for m in range(4):
                pe.wait_ge(w_lo_done, w_chunks(m))
                project(0, m)
            pe.wait_ge(rows_done, 1)
            pe.wait_ge(ld_const, 128)

            def unit(p, n, post=False):
                if n + 4 < UNITS:
                    project(p, n + 4)
                if post and n in (13, 17, 21):
                    pe.wait_ge(vn_done, GROUPS * p + (n // 4 + 1))
                if post and n in (13, 15):
                    post_xnt(p - 1, (n - 13) // 2)
                if post and n == 17:
                    post_logits(p - 1)
                if post and n == 21:
                    post_prefix(p - 1)
                if n < UNITS:
                    scores(p, n)
                    if n % 4 == 0:
                        v_transpose(p, n // 4)
                if T_LAG <= n < UNITS + T_LAG:
                    p_transpose(p, n - T_LAG)
                if n >= PV_LAG:
                    weighted_v(p, n - PV_LAG)

            def late_units(p):
                for n in range(EARLY, UNITS + PV_LAG):
                    unit(p, n)
                pe.wait_ge(pt_done, UNITS * (p + 1))

            def output(p, t):
                if t == 0:
                    pe.wait_ge(ot_done, UNITS * (p + 1))
                for h in range(NH):
                    last = pe.matmul(SC[t // 2][:, (t % 2) * H:(t % 2 + 1) * H], oT[:, h, t * PN:(t + 1) * PN],
                                     wo[:, h, :], start=(h == 0), stop=(h == NH - 1))
                last.then_inc(y_ps, 1)

            def post_xnt(p, b):
                pe.wait_ge(xn_done, 2 * p + (b + 1))
                if b == 1:
                    pe.wait_ge(xnt_lo_done, 2 * p + 1)
                for c in range(HC):
                    for t in range(2):
                        last = pe.transpose(XB[:, c * S + t * PN:c * S + (t + 1) * PN],
                                            xn[:, 2 * b + t, c * PN:(c + 1) * PN], ident[:, :])
                last.then_inc(xnt_ps, 1)

            def post_logits(p):
                pe.wait_ge(xnt_lo_done, 2 * p + 2)
                for t in range(TT):
                    tk = slice(t * PN, (t + 1) * PN)
                    last = halves(XB[:, t * LCOL:t * LCOL + E + 2], HC,
                                  ((lambda c: xnT_hi[:, c, tk], lambda c: xnT_lo[:, c, tk]),
                                   (lambda c: wr_hi[:, c, :], lambda c: wr_lo[:, c, :])))
                last.then_inc(lg_ps, 1)

            def post_prefix(p):
                pe.wait_ge(chosen_done, p + 1)
                if later(p):
                    pe.wait_ge(wsel_done, p)
                pe.wait_ge(ex_done, p + 1)
                for t in range(TT):
                    o = XB[:, 256 + t * E:256 + (t + 1) * E]
                    pe.matmul(o, ones[:, :], carry[:, 0, :], start=True, stop=False)
                    for u in range(t):
                        pe.matmul(o, ones[:, :], chosen[:, u, :], start=False, stop=False)
                    last = pe.matmul(o, tri[:, :], chosen[:, t, :], start=False, stop=True)
                last.then_inc(pos_ps, 1)

            for n in range(EARLY):
                pe.wait_ge(w_lo_done, w_chunks(n + 4))
                unit(0, n)
            pe.wait_ge(w_lo_done, 8)
            pe.wait_ge(ld_wo, 16)
            pe.wait_ge(wr_lo_done, 1)
            pe.wait_ge(fills, 6)
            with pe.Fori(0, LAST) as p:
                late_units(p)
                prepare_t(p + 1)
                output(p, 0)
                output(p, 1)
                project(p + 1, 0)
                project(p + 1, 1)
                output(p, 2)
                project(p + 1, 2)
                project(p + 1, 3)
                output(p, 3)
                for n in range(EARLY):
                    unit(p + 1, n, post=True)
            late_units(LAST)
            for t in range(TT):
                output(LAST, t)

            def expert_slot(base, n, rnd, lo=0, hi=10 ** 9):
                if lo <= n < hi:
                    if n % 2 == 0:
                        pe.wait_ge(ld_xe[n // 2], 16 * rnd)
                    if n >= 2 or later(base):
                        pe.wait_ge(xe_done, base + (n - 1))
                    for c in range(HC):
                        last = pe.transpose(PJ[n % 2][:, c * PN:(c + 1) * PN], xe[:, n % RING, c * PN:(c + 1) * PN], ident[:, :])
                    last.then_inc(xe_ps, 1)
                if lo <= n - 1 < hi:
                    e, i = n - 1, (n - 1) % RING
                    pe.wait_ge(xe_done, base + (e + 1))
                    if e % 2 == 0:
                        pe.wait_ge(ld_e[i // 2], 48 * rnd)
                    if e >= 2 or later(base):
                        pe.wait_ge(hh_done, base + (e - 1))
                    for c in range(HC):
                        last = pe.matmul(SC[e % 2][:, 0:2 * F], xeT[:, e % 2, c * PN:(c + 1) * PN], wgu[:, i, c, :],
                                         start=(c == 0), stop=(c == HC - 1))
                    last.then_inc(gu_ps, 1)
                if lo <= n - 2 < hi:
                    e = n - 2
                    pe.wait_ge(hh_done, base + (e + 1))
                    if e >= 2 or later(base):
                        pe.wait_ge(hht_done, base + (e - 1))
                    for c in range(2):
                        last = pe.transpose(PT[e % 2][0:FH, c * PN:(c + 1) * PN], hh[:, e % 2, c * FH:(c + 1) * FH], ident[:, :])
                    last.then_inc(hh_ps, 1)
                if lo <= n - 3 < hi:
                    e, i = n - 3, (n - 3) % RING
                    pe.wait_ge(hht_done, base + (e + 1))
                    if e >= 2 or later(base):
                        pe.wait_ge(ye_done, base + (e - 1))
                    bk = (OB, XB)[e % 2]
                    for c in range(2):
                        last = pe.matmul(bk[:, 0:H], hhT[:, e % 2, c * PN:(c + 1) * PN], wd[:, i, c, :],
                                         start=(c == 0), stop=(c == 1))
                    last.then_inc(ye_ps, 1)

            def gate_up(q, f):
                if f == 0:
                    pe.wait_ge(ld_xs, 32 * (q + 1))
                fw = min(PN, FS - f * PN)
                if f >= 2 or later(q):
                    pe.wait_ge(hs_done, FT * q + (f - 1))
                for off, bk in ((0, PJ[f % 2]), (FS, SC[f % 2])):
                    cols = slice(off + f * PN, off + f * PN + fw)
                    last = halves(bk[0:fw, :], HC,
                                  ((lambda c: sw_hi[:, c, cols], lambda c: sw_lo[:, c, cols]),
                                   (lambda c: xs_hi[:, c, :], lambda c: xs_lo[:, c, :])))
                last.then_inc(sh_ps, 1)

            def down(q, t):
                if t == 0:
                    pe.wait_ge(hs_done, FT * (q + 1))
                if t >= 2 or later(q):
                    pe.wait_ge(shrow_done, TT * q + (t - 1))
                for f in range(FT):
                    fw = min(PN, FS - f * PN)
                    last = pe.matmul(DN[t % 2][:, 0:H], hs[0:fw, f, t * PN:(t + 1) * PN], swd[0:fw, f, :],
                                     start=(f == 0), stop=(f == FT - 1))
                last.then_inc(dn_ps, 1)

            post_xnt(LAST, 0)
            pe.wait_ge(yg_done, 2 * NPAIR)
            pe.wait_ge(sw_lo_done, 1)
            for f in range(3):
                gate_up(0, f)
            post_xnt(LAST, 1)
            gate_up(0, 3)
            post_logits(LAST)
            gate_up(0, 4)
            post_prefix(LAST)
            gate_up(0, 5)
            pe.wait_ge(ld_swd, 32)
            for t in range(TT):
                down(0, t)
            for f in range(F_EARLY):
                gate_up(1, f)
            pe.wait_ge(pos_used, NPAIR)
            pe.wait_ge(shrow_done, TT)
            pe.wait_ge(hs_done, FT + F_EARLY)
            for n in range(RING):
                expert_slot(0, n, 1)
            with pe.Fori(1, E // RING) as r:
                for n in range(RING):
                    expert_slot(RING * r, n, r + 1, lo=-RING)
            for n in range(3):
                expert_slot(E, n, E // RING + 1, lo=-RING, hi=0)
            pe.wait_ge(ye_done, E)
            for f in range(F_EARLY, FT):
                gate_up(1, f)
            with pe.Fori(1, LAST) as q:
                for t in range(TT):
                    down(q, t)
                for f in range(FT):
                    gate_up(q + 1, f)
            for t in range(TT):
                down(LAST, t)


_INS = ['L0_attn_hidden', 'L0_attn_W_pack', 'L0_attn_W_o', 'L0_attn_conv_k', 'L0_attn_conv_v', 'L0_ffn_w_norm',
        'L0_ffn_w_router', 'L0_ffn_w_gate', 'L0_ffn_w_up', 'L0_ffn_w_down', 'L0_ffn_sw_gate', 'L0_ffn_sw_up',
        'L0_ffn_sw_down', 'L0_ffn_w_shared_gate', 'L0_c', 'L0_wmod']
_OUTS = [((B, S, H), 'float32')]


def _constants():
    import numpy as _np
    f = _np.float32
    inv_freq = f(1.0) / f(100000.0) ** (_np.arange(0, HD, 2, dtype=f) / f(HD))
    freqs = _np.outer(_np.arange(S, dtype=f), inv_freq).astype(f).T
    cos, sin = _np.cos(freqs).astype(f), _np.sin(freqs).astype(f)
    i, j = _np.arange(PN)[:, None], _np.arange(PN)[None, :]
    causal, window = j <= i, j > i
    allowed = _np.concatenate([causal, window, causal], axis=1)
    return [_np.concatenate([cos, cos], axis=0), _np.concatenate([-sin, sin], axis=0),
            _np.where(allowed, f(0.0), f(-3.0e38)).astype(f), _np.eye(PN, dtype=f), (i < j).astype(f),
            _np.tile((_np.arange(E) * CAP + 1).astype(f), (PN, 1))]


def kernel(**inputs):
    import numpy as _np
    import concourse.bacc as _bacc
    from concourse import mybir as _mybir
    from concourse.bass_utils import run_bass_kernel_spmd as _run

    nc = _bacc.Bacc("TRN2", target_bir_lowering=False, num_devices=1)
    arrays, args = {}, []
    host = [_np.ascontiguousarray(inputs[name]) for name in _INS] + _constants()
    for n, a in enumerate(host):
        if n == 0:
            a = a.reshape(B * S, H)
        name = f"in_{n}_dram"
        arrays[name] = a
        args.append(nc.dram_tensor(name, a.shape, _mybir.dt.from_np(a.dtype), kind="ExternalInput").ap())
    out = nc.dram_tensor("out_0_dram", (B * S, H), _mybir.dt.float32, kind="ExternalOutput").ap()
    adaln_block(nc, *args, out)
    r = _run(nc, [arrays], core_ids=[0])
    return r.results[0]["out_0_dram"].reshape(B, S, H)
```
